# Optimizing a Trainium2 kernel written in Bass

```python
import numpy as np
import jax
import jax.numpy as jnp

def _softmax(x, axis=-1):
    return jax.nn.softmax(x, axis=axis)

def _gelu(x):
    return jax.nn.gelu(x, approximate=True)

def _silu(x):
    return jax.nn.silu(x)

def _sigmoid(x):
    return jax.nn.sigmoid(x)

def _layernorm(x, axis=-1, eps=1e-05):
    m = jnp.mean(x, axis=axis, keepdims=True)
    v = jnp.var(x, axis=axis, keepdims=True)
    return (x - m) / jnp.sqrt(v + eps)

def _scatter_add(tgt, idx, src, axis=0):
    return tgt.at[idx].add(src)

def _segment_sum(src, seg, n):
    return jax.ops.segment_sum(src, seg, n)
kernel_name = 'mk_prb_d1_jaxref_r4_f3efc2'

def setup_inputs(seed: int=0):
    np.random.seed(seed)
    _w = jnp.asarray

    def _L0_attn_setup():
        import jax, jax.numpy as jnp
        import numpy as np
        NUM_HEADS = 16
        DIM = 256
        HARMONICS = 32
        B, L = (2, 512)

        def holo_linear(x, basis, phase, amp):
            resonance = jnp.einsum('bli,hi->blh', x, basis)
            w = amp * jnp.cos(phase)
            return jnp.einsum('blh,oh->blo', resonance, w)
        key = jax.random.key(seed)
        ks = jax.random.split(key, 13)
        two_pi = 2.0 * np.pi

        def make_proj(k0, k1):
            basis = jax.random.normal(k0, (HARMONICS, DIM), dtype=jnp.float32)
            basis = basis / jnp.linalg.norm(basis, axis=1, keepdims=True)
            phase = jax.random.normal(k1, (DIM, HARMONICS), dtype=jnp.float32) * two_pi
            amp = jnp.ones((DIM, HARMONICS), dtype=jnp.float32) / HARMONICS
            return (basis, phase, amp)
        x = jax.random.normal(ks[0], (B, L, DIM), dtype=jnp.float32)
        bq, pq, aq = make_proj(ks[1], ks[2])
        bk, pk, ak = make_proj(ks[3], ks[4])
        bv, pv, av = make_proj(ks[5], ks[6])
        bo, po, ao = make_proj(ks[7], ks[8])
        return {'x': x, 'basis_q': bq, 'phase_q': pq, 'amp_q': aq, 'basis_k': bk, 'phase_k': pk, 'amp_k': ak, 'basis_v': bv, 'phase_v': pv, 'amp_v': av, 'basis_o': bo, 'phase_o': po, 'amp_o': ao}
    _L0_attn_in = _L0_attn_setup()

    def _L0_ffn_setup():
        import jax, jax.numpy as jnp
        import numpy as np
        B, S, D = (1, 512, 256)
        E, K, F = (8, 2, 352)
        NS = 2
        SCALE = 2.5

        def _swiglu_mlp(x, wg, wu, wd):
            return jax.nn.silu(x @ wg) * (x @ wu) @ wd
        key = jax.random.key(seed)
        ks = jax.random.split(key, 8)
        s = 0.02
        return {'hidden_states': jax.random.normal(ks[0], (B, S, D), jnp.float32), 'gate_w': jax.random.normal(ks[1], (E, D), jnp.float32) * s, 'w_gate': jax.random.normal(ks[2], (E, D, F), jnp.float32) * s, 'w_up': jax.random.normal(ks[3], (E, D, F), jnp.float32) * s, 'w_down': jax.random.normal(ks[4], (E, F, D), jnp.float32) * s, 'sw_gate': jax.random.normal(ks[5], (D, F * NS), jnp.float32) * s, 'sw_up': jax.random.normal(ks[6], (D, F * NS), jnp.float32) * s, 'sw_down': jax.random.normal(ks[7], (F * NS, D), jnp.float32) * s}
    _L0_ffn_in = _L0_ffn_setup()
    _d = {'L0_attn_x': _L0_attn_in['x'], 'L0_attn_basis_q': _L0_attn_in['basis_q'], 'L0_attn_phase_q': _L0_attn_in['phase_q'], 'L0_attn_amp_q': _L0_attn_in['amp_q'], 'L0_attn_basis_k': _L0_attn_in['basis_k'], 'L0_attn_phase_k': _L0_attn_in['phase_k'], 'L0_attn_amp_k': _L0_attn_in['amp_k'], 'L0_attn_basis_v': _L0_attn_in['basis_v'], 'L0_attn_phase_v': _L0_attn_in['phase_v'], 'L0_attn_amp_v': _L0_attn_in['amp_v'], 'L0_attn_basis_o': _L0_attn_in['basis_o'], 'L0_attn_phase_o': _L0_attn_in['phase_o'], 'L0_attn_amp_o': _L0_attn_in['amp_o'], 'L0_ffn_gate_w': _L0_ffn_in['gate_w'], 'L0_ffn_w_gate': _L0_ffn_in['w_gate'], 'L0_ffn_w_up': _L0_ffn_in['w_up'], 'L0_ffn_w_down': _L0_ffn_in['w_down'], 'L0_ffn_sw_gate': _L0_ffn_in['sw_gate'], 'L0_ffn_sw_up': _L0_ffn_in['sw_up'], 'L0_ffn_sw_down': _L0_ffn_in['sw_down']}
    _x0 = _d['L0_attn_x']
    _d['L0_attn_x'] = jax.random.normal(jax.random.fold_in(jax.random.key(seed), 1), (8, 512, 256), dtype=_x0.dtype)
    del _x0
    return _d

def reference(L0_attn_x, L0_attn_basis_q, L0_attn_phase_q, L0_attn_amp_q, L0_attn_basis_k, L0_attn_phase_k, L0_attn_amp_k, L0_attn_basis_v, L0_attn_phase_v, L0_attn_amp_v, L0_attn_basis_o, L0_attn_phase_o, L0_attn_amp_o, L0_ffn_gate_w, L0_ffn_w_gate, L0_ffn_w_up, L0_ffn_w_down, L0_ffn_sw_gate, L0_ffn_sw_up, L0_ffn_sw_down):

    def _L0_attn_ref(x, basis_q, phase_q, amp_q, basis_k, phase_k, amp_k, basis_v, phase_v, amp_v, basis_o, phase_o, amp_o):
        import jax, jax.numpy as jnp
        import numpy as np
        NUM_HEADS = 16
        DIM = 256
        HARMONICS = 32
        B, L = (2, 512)

        def holo_linear(x, basis, phase, amp):
            resonance = jnp.einsum('bli,hi->blh', x, basis)
            w = amp * jnp.cos(phase)
            return jnp.einsum('blh,oh->blo', resonance, w)
        Bsz, Ls, C = x.shape
        head_dim = C // NUM_HEADS
        scale = head_dim ** (-0.5)

        def split_heads(t):
            return t.reshape(Bsz, Ls, NUM_HEADS, head_dim).transpose(0, 2, 1, 3)
        q = split_heads(holo_linear(x, basis_q, phase_q, amp_q))
        k = split_heads(holo_linear(x, basis_k, phase_k, amp_k))
        v = split_heads(holo_linear(x, basis_v, phase_v, amp_v))
        attn = jnp.einsum('bhqd,bhkd->bhqk', q, k) * scale
        attn = jax.nn.softmax(attn, axis=-1)
        out = jnp.einsum('bhqk,bhkd->bhqd', attn, v)
        out = out.transpose(0, 2, 1, 3).reshape(Bsz, Ls, C)
        return holo_linear(out, basis_o, phase_o, amp_o)

    def _L0_ffn_ref(hidden_states, gate_w, w_gate, w_up, w_down, sw_gate, sw_up, sw_down):
        import jax, jax.numpy as jnp
        import numpy as np
        B, S, D = (1, 512, 256)
        E, K, F = (8, 2, 352)
        NS = 2
        SCALE = 2.5

        def _swiglu_mlp(x, wg, wu, wd):
            return jax.nn.silu(x @ wg) * (x @ wu) @ wd
        identity = hidden_states
        x = hidden_states.reshape(-1, hidden_states.shape[-1])
        T = x.shape[0]
        logits = x.astype(jnp.float32) @ gate_w.astype(jnp.float32).T
        scores = jax.nn.softmax(logits, axis=-1)
        topk_w, topk_i = jax.lax.top_k(scores, K)
        topk_w = topk_w / (topk_w.sum(-1, keepdims=True) + 1e-20) * SCALE
        combine = jnp.zeros((T, E), jnp.float32).at[jnp.arange(T)[:, None], topk_i].set(topk_w)
        g = jax.nn.silu(jnp.einsum('td,edf->etf', x, w_gate)) * jnp.einsum('td,edf->etf', x, w_up)
        expert_out = jnp.einsum('etf,efd->etd', g, w_down)
        y = jnp.einsum('te,etd->td', combine, expert_out).astype(x.dtype)
        y = y.reshape(identity.shape)
        return y + _swiglu_mlp(identity, sw_gate, sw_up, sw_down)
    x = L0_attn_x
    xn = _layernorm(x, axis=-1)
    x = x + _L0_attn_ref(xn, L0_attn_basis_q, L0_attn_phase_q, L0_attn_amp_q, L0_attn_basis_k, L0_attn_phase_k, L0_attn_amp_k, L0_attn_basis_v, L0_attn_phase_v, L0_attn_amp_v, L0_attn_basis_o, L0_attn_phase_o, L0_attn_amp_o) + _L0_ffn_ref(xn, L0_ffn_gate_w, L0_ffn_w_gate, L0_ffn_w_up, L0_ffn_w_down, L0_ffn_sw_gate, L0_ffn_sw_up, L0_ffn_sw_down)
    return x

_drawn_inputs = setup_inputs


def setup_inputs(seed=0):
    import zlib

    import numpy as np

    out = dict(_drawn_inputs(seed))
    spreads = {'L0_attn_amp_q': (0.03125, 0.6),
     'L0_attn_amp_k': (0.03125, 0.6),
     'L0_attn_amp_v': (0.03125, 0.6),
     'L0_attn_amp_o': (0.03125, 0.6)}
    factors = {'L0_attn_basis_q': 8.0,
     'L0_attn_phase_q': 8.0,
     'L0_attn_basis_k': 8.0,
     'L0_attn_phase_k': 8.0,
     'L0_attn_basis_v': 8.0,
     'L0_attn_phase_v': 8.0,
     'L0_attn_basis_o': 8.0,
     'L0_attn_phase_o': 8.0}
    for name, (base, spread) in spreads.items():
        noise = np.random.default_rng([zlib.crc32(name.encode()), seed]).standard_normal(out[name].shape)
        drawn = base * np.exp(spread * noise) if base else spread * noise
        out[name] = jnp.asarray(drawn.astype(out[name].dtype))
    for name, factor in factors.items():
        out[name] = (out[name] * factor).astype(out[name].dtype)
    return out
```

```python
import math
from contextlib import ExitStack

import concourse.bass as bass
from concourse import mybir

P = 128
ALU = mybir.AluOpType
ACT = mybir.ActivationFunctionType
AX_X = mybir.AxisListType.X
F32 = mybir.dt.float32
F32R = mybir.dt.float32r
BF16 = mybir.dt.bfloat16
I32 = mybir.dt.int32
U32 = mybir.dt.uint32

HI, LO = 0, 1
PRODUCTS = ((HI, HI), (LO, HI), (HI, LO))

LN_EPS = 1e-5
TOPK_EPS = 1e-20
ROUTE_SCALE = 2.5
TURN_1 = 6.28125
TURN_2 = math.floor((2 * math.pi - TURN_1) * 2**21) / 2**21
TURN_3 = 2 * math.pi - TURN_1 - TURN_2
PI_BELOW = 3.1415925
ROUNDER = 1.5 * 2**23


class Steps:

    def __init__(self, eng, sem, base=0):
        self.eng, self.sem, self.base, self.n = eng, sem, base, 0

    def did(self, ins):
        ins.then_inc(self.sem, 1)
        self.n += 1
        return self.n

    def value(self, n=None):
        return self.base + (self.n if n is None else n)

    def wait(self, n=None):
        self.eng.wait_ge(self.sem, self.value(n))

    def then(self, ins):
        self.did(ins)
        self.wait()


def wait(eng, sem, value):
    if isinstance(value, int) and value <= 0:
        return
    eng.wait_ge(sem, value)


def build_program(nc, x, attn, gate_w, w_gate, w_up, w_down, sw_gate, sw_up, sw_down, out):
    NB, L, D = x.shape
    NE, _, F = w_gate.shape
    SF = sw_gate.shape[1]
    HARM = attn["q"][0].shape[0]
    HEADS = 16
    HD = D // HEADS
    PROJ = ("q", "k", "v", "o")
    KT = D // P
    TPB = L // P
    NT = NB * TPB
    FT = -(-F // P)
    F_LAST = F - (FT - 1) * P
    GU = 2 * F
    W_GU = KT * GU
    W_ALL = W_GU + FT * D
    NS = 2 * NT + NE
    N_RING = 4

    xn_dram = nc.dram_tensor("xn_split", (NB * L, 2 * D), F32).ap()
    y_dram = nc.dram_tensor("expert_rows", (NS * P, D), F32).ap()

    ctx = ExitStack()

    def sb(name, shape, dt, where=None):
        return (where or ctx).enter_context(nc.sbuf_tensor(name, shape, dt))

    def sem(name):
        return ctx.enter_context(nc.semaphore(name))

    with ctx:
        bank = [ctx.enter_context(nc.psum_tensor(f"bank{i}", [P, 512], F32)) for i in range(8)]

        ident_f = sb("ident_f", [P, P], F32)
        ident_r = sb("ident_r", [P, P], F32R)
        q_minus = sb("q_minus", [P, 1], F32)
        k_minus = sb("k_minus", [P, 1], F32)
        basis_T = sb("basis_T", [P, KT, 2, len(PROJ), 3, HARM], F32R)
        wq_rows = sb("wq_rows", [97, HEADS, 64], F32R)
        wk_rows = sb("wk_rows", [97, HEADS, 64], F32R)
        wv_rows = sb("wv_rows", [96, D], F32R)
        wo_rows = sb("wo_rows", [96, D], F32R)
        share = sb("share", [P, NT, 2], F32)
        slot_of = sb("slot_of", [P, 2, NT], I32)
        token_of = sb("token_of", [P, NS], I32)
        expert_of = sb("expert_of", [1, NS], I32)

        early = ExitStack()
        w_exp = sb("w_exp", [P, NE, 2, W_ALL], F32R, early)
        raw = [sb(f"raw{i}", [P, W_ALL], F32, early) for i in range(2)]
        zeros = sb("zeros", [P, NT], F32, early)

        region = ExitStack()
        x_all = sb("x_all", [P, NT, D], F32, region)
        gate_T = sb("gate_T", [P, KT, 2, NE], F32R, region)
        stats = sb("stats", [P, NT, 6], F32, region)
        mean_var = sb("mean_var", [P, NT, 2], F32, region)
        rs = sb("rs", [P, 4, NT], F32, region)
        iota_e = sb("iota_e", [P, NE], F32, region)
        iota_s = sb("iota_s", [P, NS], F32, region)
        iota_r = sb("iota_r", [P, P], F32, region)
        token_id = sb("token_id", [P, NT], F32, region)
        region.close()

        in_c = ExitStack()
        xg = [sb(f"xg{i}", [P, 2 * D], F32R, in_c) for i in range(4)]
        xg_T = [sb(f"xg_T{i}", [P, 2 * KT, P], F32R, in_c) for i in range(2)]
        c_sil = [sb(f"c_sil{i}", [P, F], F32, in_c) for i in range(2)]
        c_h = [sb(f"c_h{i}", [P, F], F32, in_c) for i in range(2)]
        c_hh = [sb(f"c_hh{i}", [P, FT * P], F32R, in_c) for i in range(2)]
        c_hl = [sb(f"c_hl{i}", [P, FT * P], F32R, in_c) for i in range(2)]
        c_hT = [sb(f"c_hT{i}", [P, 2, FT, P], F32R, in_c) for i in range(2)]
        c_y = [sb(f"c_y{i}", [P, D], F32, in_c) for i in range(4)]
        in_c.close()
        early.close()

        tail = ExitStack()
        sb("first_experts", [P, NE - 2, 2, W_ALL], F32R, tail)
        x_rows = sb("x_rows", [P, TPB, 2, D], F32R, tail)
        x_T = sb("x_T", [P, 2, KT, L], F32R, tail)
        upper = sb("upper", [P, P], BF16, tail)
        ones_b = sb("ones_b", [P, P], BF16, tail)
        prep = ExitStack()
        gate_raw = sb("gate_raw", [NE, D], F32, prep)
        basis_raw = sb("basis_raw", [P, D], F32, prep)
        phase = sb("phase", [P, len(PROJ), KT, HARM], F32, prep)
        amp = sb("amp", [P, len(PROJ), KT, HARM], F32, prep)
        turns = sb("turns", [P, len(PROJ) * KT * HARM], F32, prep)
        angle = sb("angle", [P, len(PROJ) * KT * HARM], F32, prep)
        w_thrice = sb("w_thrice", [P, len(PROJ) * KT, 3, HARM], F32, prep)
        w_hi = sb("w_hi", [96, len(PROJ), D], F32R, prep)
        prep.close()
        lg = sb("lg", [P, NT, NE], F32, tail)
        pr = sb("pr", [P, NT, NE], F32, tail)
        best = sb("best", [P, NT, NE], F32, tail)
        best_at = sb("best_at", [P, NT, NE], U32, tail)
        best_atf = sb("best_atf", [P, 2, NT], F32, tail)
        row = sb("row", [P, 4, NT], F32, tail)
        hot = [sb(f"hot{k}", [P, NT, NE], F32, tail) for k in range(2)]
        hot_b = sb("hot_b", [P, NT, NE], BF16, tail)
        before = sb("before", [P, NE, NT], F32, tail)
        totals = sb("totals", [P, NE, NT], F32, tail)
        tiles = sb("tiles", [P, 4, NE], F32, tail)
        slot_base, slot_hot = pr, lg
        slot_f = sb("slot_f", [P, 2, NT], F32, tail)
        slot_q = sb("slot_q", [P, 2, NT], F32, tail)
        slot_r = sb("slot_r", [P, 2, NT], F32, tail)
        started = sb("started", [1, NS, NE], F32, tail)
        started_n = sb("started_n", [1, NS], F32, tail)
        at_row = [sb(f"at_row{i}", [P, P], F32R, tail) for i in range(N_RING)]
        at_tile = [sb(f"at_tile{i}", [P, NS], F32R, tail) for i in range(N_RING)]
        tail.close()

        SFT = -(-SF // P)
        SF_LAST = SF - (SFT - 1) * P
        S_GU = KT * 2 * SF
        S_ALL = S_GU + SFT * D
        NG = HEADS // 4
        QKV_ROWS = 50
        late = ExitStack()
        w_sh = sb("w_sh", [P, 2, S_ALL], F32R, late)
        x_b = sb("x_b", [P, TPB, D], F32, late)
        xr_b = sb("xr_b", [P, TPB, 2, D], F32R, late)
        xT_b = sb("xT_b", [P, 2, KT, L], F32R, late)
        r_rows = [sb(f"r_{n}", [97, L], F32R, late) for n in "qkv"]
        qk_hi = [sb(f"qk_hi{i}", [P, L], F32R, late) for i in range(2)]
        q_rows = [sb(f"q_rows{i}", [P, 2, L], F32R, late) for i in range(2)]
        k_rows = [sb(f"k_rows{i}", [P, 2, L], F32R, late) for i in range(2)]
        top = [sb(f"top{i}", [P, 2, 2, TPB], F32, late) for i in range(2)]
        top_parts = [sb(f"top_parts{i}", [P, TPB, 2, 2, 2], F32R, late) for i in range(2)]
        top_T = [sb(f"top_T{i}", [8, L], F32R, late) for i in range(2)]
        prob = [sb(f"prob{i}", [P, 4, L], F32, late) for i in range(2)]
        v_ones = sb("v_ones", [P, TPB, HEADS, 2 * HD], F32, late)
        o_T = sb("o_T", [P, NG, L], F32, late)
        o_inv = sb("o_inv", [P, 2, HEADS], F32, late)
        ao = [sb(f"ao{i}", [P, D], F32, late) for i in range(2)]
        ao_T = sb("ao_T", [P, 2, KT, L], F32R, late)
        ro = sb("ro", [96, L], F32R, late)
        gate_th = [sb(f"gate_th{i}", [P, L], F32, late) for i in range(2)]
        gate_a = [sb(f"gate_a{i}", [P, L], F32, late) for i in range(2)]
        h_f = [sb(f"h_f{i}", [P, L], F32, late) for i in range(2)]
        o_b = [sb(f"o_b{t}", [P, D], F32, late) for t in range(TPB)]
        y_b = sb("y_b", [P, TPB, 2, D], F32, late)
        over = ExitStack()
        s_raw = sb("s_raw", [P, S_ALL], F32, over)
        over.close()
        h_T = sb("h_T", [P, 2, SFT, L], F32R, late)
        late.close()

        x_in = [sem(f"x_in{q}") for q in range(4)]
        small_in = sem("small_in")
        raw_in = [sem(f"raw_in{i}") for i in range(2)]
        hi_done = sem("hi_done")
        lo_done = sem("lo_done")
        consts = sem("consts")
        dve_a = sem("dve_a")
        act_a = sem("act_a")
        sin_done = sem("sin_done")
        pe_prep = sem("pe_prep")
        prep_done = sem("prep_done")
        stats_ok = sem("stats_ok")
        root_ok = sem("root_ok")
        rs_ok = sem("rs_ok")
        xn_ok = sem("xn_ok")
        xhi_ok = sem("xhi_ok")
        xlo_ok = sem("xlo_ok")
        xn_stored = sem("xn_stored")
        xt_ps = sem("xt_ps")
        xt_hi = sem("xt_hi")
        xt_lo = sem("xt_lo")
        lg_ps = sem("lg_ps")
        lg_max = sem("lg_max")
        lg_exp = sem("lg_exp")
        hot_ok = sem("hot_ok")
        count_ps = sem("count_ps")
        inv_ok = sem("inv_ok")
        inv_ps = sem("inv_ps")
        a_done = sem("a_done")

        c_x = [sem(f"c_x{i}") for i in range(4)]
        c_xt = sem("c_xt")
        c_xe = sem("c_xe")
        c_g = sem("c_g")
        c_u = sem("c_u")
        c_sl = sem("c_sl")
        c_hk = sem("c_hk")
        c_hi = sem("c_hi")
        c_lo = sem("c_lo")
        c_ht = sem("c_ht")
        c_hea = sem("c_hea")
        c_hed = sem("c_hed")
        c_d = sem("c_d")
        c_yk = sem("c_yk")
        c_st = [sem(f"c_st{i}") for i in range(4)]
        c_pad = sem("c_pad")

        s_in = sem("s_in")
        s_pad = sem("s_pad")
        s_hi = sem("s_hi")
        s_lo = sem("s_lo")
        xr_in = sem("xr_in")
        xb_in = sem("xb_in")
        y_in = sem("y_in")
        m_in = [sem(f"m_in{i}") for i in range(2)]
        b_xt, b_r, b_v, b_qk, b_s, b_mt, b_st, b_pv, b_gu, b_ot, b_at, b_res, b_out = (
            sem(f"b_{n}") for n in ("xt", "r", "v", "qk", "s", "mt", "st", "pv", "gu", "ot", "at", "res", "out"))
        a_xt, a_r, a_v, a_qk, a_exp, a_th, a_ot, a_at, a_res = (
            sem(f"a_{n}") for n in ("xt", "r", "v", "qk", "exp", "th", "ot", "at", "res"))
        d_xt, d_r, d_qk, d_max, d_mh, d_m, d_mt, d_ga, d_hf, d_hh, d_h, d_inv, d_ao, d_at, d_res, d_sum, d_out = (
            sem(f"d_{n}") for n in ("xt", "r", "qk", "max", "mh", "m", "mt", "ga", "hf", "hh", "h", "inv", "ao", "at", "res", "sum", "out"))
        o_st = [sem(f"o_st{t}") for t in range(TPB)]

        block = ctx.enter_context(nc.Block())

        s_bank, st_bank, ot_bank, g_bank, u_bank, m_bank = bank[0:2], bank[2:4], bank[4], bank[5], bank[6], bank[7]
        xT_bank = [[bank[0], bank[1]], [bank[2], bank[3]]]
        r_bank = [g_bank, u_bank, m_bank]
        v_bank = [g_bank, u_bank]
        qk_bank = [g_bank, u_bank, m_bank, g_bank]

        xt_bank = [[bank[2], bank[3]], [bank[4], bank[5]]]
        lg_bank = bank[6]
        gu_bank = [[bank[0], bank[1]], [bank[2], bank[3]]]
        xg_bank, y_bank = bank[4], bank[5]
        ht_bank = [bank[6], bank[7]]

        @block.sync
        def _(sp):
            def load_x(q):
                n = NB // 4
                for j in range(n):
                    sp.dma_start(x_all[:, (q * n + j) * TPB:(q * n + j + 1) * TPB, :],
                                 x[q * n + j].rearrange("(t p) d -> p t d", p=P)).then_inc(x_in[q], 16)

            load_x(0)
            sp.dma_start(gate_raw[:, :], gate_w).then_inc(small_in, 16)
            for i, name in enumerate(PROJ):
                basis, ph, am = attn[name]
                sp.dma_start(basis_raw[i * HARM:(i + 1) * HARM, :], basis).then_inc(small_in, 16)
                sp.dma_start(phase[:, i, :, :], ph.rearrange("(a p) h -> p a h", p=P)).then_inc(small_in, 16)
                sp.dma_start(amp[:, i, :, :], am.rearrange("(a p) h -> p a h", p=P)).then_inc(small_in, 16)
            for q in range(1, 4):
                load_x(q)
            wait(sp, consts, 1)
            def load_experts(e2):
                for i in range(2):
                    e = e2 * 2 + i
                    r = raw[i]
                    wait(sp, hi_done, e2 * 2 + i - 1 if i else e2 * 2)
                    wait(sp, lo_done, e2 * 2 + i - 1 if i else e2 * 2)
                    gu = r[:, 0:W_GU].rearrange("p (k n) -> p k n", k=KT)
                    dn = r[:, W_GU:W_ALL].rearrange("p (k n) -> p k n", k=FT)
                    one = lambda w: w[bass.ds(e, 1)] if not isinstance(e, int) else w[e:e + 1]
                    sp.dma_start(gu[:, :, 0:F], one(w_gate).rearrange("a (k p) f -> p (a k) f", p=P)).then_inc(raw_in[i], 16)
                    sp.dma_start(gu[:, :, F:GU], one(w_up).rearrange("a (k p) f -> p (a k) f", p=P)).then_inc(raw_in[i], 16)
                    sp.dma_start(dn[:, 0:FT - 1, :],
                                 w_down[bass.ds(e, 1), 0:(FT - 1) * P, :].rearrange("a (k p) f -> p (a k) f", p=P)).then_inc(raw_in[i], 16)
                    sp.dma_start(dn[0:F_LAST, FT - 1, :],
                                 w_down[bass.ds(e, 1), (FT - 1) * P:F, :].rearrange("a p f -> (a p) f")).then_inc(raw_in[i], 16)

            with sp.Fori(0, NE // 2 - 1) as e2:
                load_experts(e2)
            with sp.Fori(0, NB // 2) as b2:
                for i in range(2):
                    b = b2 * 2 + i
                    wait(sp, xhi_ok, b + 1)
                    wait(sp, xlo_ok, b + 1)
                    sp.dma_start(xn_dram.rearrange("(b t p) c -> p b t c", t=TPB, p=P)[:, bass.ds(b, 1), :, :].rearrange("p b t c -> p (b t) c"),
                                 x_rows[:, :, :, :].rearrange("p t a d -> p t (a d)").bitcast(F32)).then_inc(xn_stored, 16)
            load_experts(NE // 2 - 1)
            with sp.Fori(0, NS // 4) as s4:
                for i in range(4):
                    s = s4 * 4 + i
                    wait(sp, c_yk, s + 1)
                    sp.dma_start(y_dram.rearrange("(s p) d -> s p d", p=P)[bass.ds(s, 1)].rearrange("a p d -> (a p) d"),
                                 c_y[i][:, :]).then_inc(c_st[i], 16)
            for i in range(4):
                sp.wait_ge(c_st[i], 16 * (NS // 4))

            gu = s_raw[:, 0:S_GU].rearrange("p (k n) -> p k n", k=KT)
            dn = s_raw[:, S_GU:S_ALL].rearrange("p (k n) -> p k n", k=SFT)
            sp.dma_start(gu[:, :, 0:SF], sw_gate.rearrange("(k p) f -> p k f", p=P)).then_inc(s_in, 16)
            sp.dma_start(gu[:, :, SF:2 * SF], sw_up.rearrange("(k p) f -> p k f", p=P)).then_inc(s_in, 16)
            sp.dma_start(dn[:, 0:SFT - 1, :], sw_down[0:(SFT - 1) * P, :].rearrange("(k p) f -> p k f", p=P)).then_inc(s_in, 16)
            sp.dma_start(dn[0:SF_LAST, SFT - 1, :], sw_down[(SFT - 1) * P:SF, :]).then_inc(s_in, 16)

            def load_rows(b):
                wait(sp, b_xt, b)
                sp.dma_start(xr_b[:, :, :, :].rearrange("p t a d -> p t (a d)").bitcast(F32),
                             xn_dram.rearrange("(b t p) c -> p b t c", t=TPB, p=P)[:, bass.ds(b, 1), :, :]
                             .rearrange("p b t c -> p (b t) c")).then_inc(xr_in, 16)

            with sp.Fori(0, NB) as b:
                load_rows(b)
                wait(sp, d_out, b * TPB)
                sp.dma_start(x_b[:, :, :], x[bass.ds(b, 1)].rearrange("b (t p) d -> p (b t) d", p=P)).then_inc(xb_in, 16)
                for g in range(NG):
                    wait(sp, d_mt, b * NG + g + 1)
                    for n in range(4):
                        par, pair = n // 2, n % 2
                        sp.dma_start(q_rows[g % 2][64 * par + 48:64 * par + 50, pair, :].bitcast(F32),
                                     top_T[g % 2][2 * n:2 * n + 2, :].bitcast(F32)).then_inc(m_in[g % 2], 16)
                for t in range(TPB):
                    wait(sp, d_out, b * TPB + t + 1)
                    sp.dma_start(out[bass.ds(b, 1), t * P:(t + 1) * P, :].rearrange("a p d -> (a p) d"), o_b[t][:, :]).then_inc(o_st[t], 16)
            for t in range(TPB):
                sp.wait_ge(o_st[t], 16 * NB)

        @block.gpsimd
        def _(pool):
            st = Steps(pool, c_pad)
            for i in range(2):
                pool.memset(raw[i][96:128, W_GU + (FT - 1) * D:W_ALL], 0.0).then_inc(c_pad, 1)
            pool.wait_ge(c_pad, 2)
            pool.memset(zeros[:, :], 0.0).then_inc(consts, 1)
            st.n = 2
            st.did(pool.memset(ident_f[:, :], 0.0))
            st.did(pool.memset(upper[:, :], 1.0))
            pool.memset(ones_b[:, :], 1.0)
            pool.iota(iota_e[:, :], [[1, NE]], base=0, channel_multiplier=0, allow_small_or_imprecise_dtypes=True)
            pool.iota(iota_s[:, :], [[1, NS]], base=0, channel_multiplier=0, allow_small_or_imprecise_dtypes=True)
            pool.iota(iota_r[:, :], [[1, P]], base=0, channel_multiplier=0, allow_small_or_imprecise_dtypes=True)
            pool.iota(token_id[:, :], [[P, NT]], base=0, channel_multiplier=1, allow_small_or_imprecise_dtypes=True)
            pool.memset(wq_rows[:, :, :].bitcast(F32), 0.0)
            st.did(pool.memset(wk_rows[:, :, :].bitcast(F32), 0.0))
            st.wait()
            st.did(pool.affine_select(out=ident_f[:, :], in_=ident_f[:, :], compare_op=ALU.not_equal, fill=1.0,
                                      base=0, pattern=[[-1, P]], channel_multiplier=1))
            st.did(pool.affine_select(out=upper[:, :], in_=upper[:, :], compare_op=ALU.is_gt, fill=0.0,
                                      base=0, pattern=[[1, P]], channel_multiplier=-1))
            st.wait()
            st.did(pool.tensor_copy(ident_r[:, :], ident_f[:, :]))
            st.wait()
            pool.memset(zeros[:, :], 0.0).then_inc(consts, 1)
            def low_parts(e2):
                for i in range(2):
                    e = e2 * 2 + i
                    wait(pool, hi_done, e + 1)
                    pool.tensor_tensor(w_exp[:, bass.ds(e, 1), LO, :].rearrange("p a n -> p (a n)"), raw[i][:, :],
                                       w_exp[:, bass.ds(e, 1), HI, :].rearrange("p a n -> p (a n)").bitcast(F32),
                                       ALU.subtract).then_inc(lo_done, 1)

            with pool.Fori(0, NE // 2 - 1) as e2:
                low_parts(e2)
            pool.wait_ge(a_done, 1)
            pool.wait_ge(xn_stored, 16 * NB)

            def gather(s):
                wait(pool, c_xt, s - 3)
                pool.indirect_dma_start(xg[s % 4][:, :].bitcast(F32), None, xn_dram,
                                        bass.IndirectOffsetOnAxis(token_of[:, s:s + 1], 0)).then_inc(c_x[s % 4], 16)

            for s in range(4):
                gather(s)
            low_parts(NE // 2 - 1)
            for s in range(4, NS):
                gather(s)

            for i in range(4):
                pool.wait_ge(c_st[i], 16 * (NS // 4))
            for n in range(NT):
                wait(pool, d_out, n - TPB + 1)
                for k in range(2):
                    pool.indirect_dma_start(y_b[:, n % TPB, k, :], None, y_dram,
                                            bass.IndirectOffsetOnAxis(slot_of[:, k, n:n + 1], 0)).then_inc(y_in, 16)

        @block.scalar
        def _(act):
            st = Steps(act, act_a)
            wait(act, dve_a, A_ANGLE)
            act.activation(angle[:, :], angle[:, :], ACT.Sin).then_inc(sin_done, 1)
            wait(act, stats_ok, 1)
            act.activation(rs[:, 1, :], rs[:, 0, :], ACT.Sqrt).then_inc(root_ok, 1)

            def high_parts(e2):
                for i in range(2):
                    e = e2 * 2 + i
                    wait(act, raw_in[i], (e2 + 1) * 64)
                    act.activation(w_exp[:, bass.ds(e, 1), HI, :].rearrange("p a n -> p (a n)"), raw[i][:, :],
                                   ACT.Copy).then_inc(hi_done, 1)

            with act.Fori(0, NE // 2 - 1) as e2:
                high_parts(e2)
            with act.Fori(0, NB // 2) as b2:
                for i in range(2):
                    b = b2 * 2 + i
                    wait(act, xn_ok, b + 1)
                    wait(act, xn_stored, b * 16)
                    wait(act, xt_ps, b)
                    act.activation(x_rows[:, :, HI, :], x_all[:, bass.ds(b * TPB, TPB), :], ACT.Copy).then_inc(xhi_ok, 1)
                    wait(act, xt_ps, b + 1)
                    wait(act, lg_ps, b)
                    for k in range(KT):
                        ins = act.activation(x_T[:, HI, k, :], xt_bank[HI][k][:, :], ACT.Copy)
                    ins.then_inc(xt_hi, 1)
            act.wait_ge(lg_max, 1)
            act.activation(pr[:, :, :], lg[:, :, :], ACT.Exp).then_inc(lg_exp, 1)

            def x_out(s, i):
                wait(act, c_xt, s + 1)
                wait(act, c_u, s - 1)
                act.activation(xg_T[i % 2][:, :, :].rearrange("p a t -> p (a t)"), xg_bank[:, :], ACT.Copy).then_inc(c_xe, 1)

            def silu(s, i):
                wait(act, c_g, s + 1)
                wait(act, c_hk, s - 1)
                act.activation(c_sil[i % 2][:, :], gu_bank[i % 2][0][:, 0:F], ACT.Silu).then_inc(c_sl, 1)

            def h_out(s, i):
                wait(act, c_ht, s + 1)
                wait(act, c_d, s - 1)
                act.activation(c_hT[i % 2][:, HI, :, :].rearrange("p a t -> p (a t)"), ht_bank[HI][:, 0:FT * P], ACT.Copy).then_inc(c_hea, 1)

            def y_out(s, i):
                wait(act, c_d, s + 1)
                wait(act, c_st[i], (s // 4) * 16 if isinstance(s, int) else (s - i) * 4)
                act.activation(c_y[i][:, :], y_bank[:, 0:D], ACT.Copy).then_inc(c_yk, 1)

            def step(s, i, first=False, last=False):
                silu(s, i)
                if not (first and i < 1):
                    h_out(s - 1, (i - 1) % 4)
                if not (last and i == 3):
                    x_out(s + 1, (i + 1) % 4)
                if not (first and i < 2):
                    y_out(s - 2, (i - 2) % 4)

            act.wait_ge(a_done, 1)
            high_parts(NE // 2 - 1)
            x_out(0, 0)
            for i in range(4):
                step(i, i, first=True)
            with act.Fori(1, NS // 4 - 1) as s4:
                for i in range(4):
                    step(s4 * 4 + i, i)
            for i in range(4):
                step(NS - 4 + i, i, last=True)
            h_out(NS - 1, 3)
            y_out(NS - 2, 2)
            y_out(NS - 1, 3)

            act.wait_ge(s_in, 64)
            act.wait_ge(s_pad, 1)
            act.activation(w_sh[:, HI, :], s_raw[:, :], ACT.Copy).then_inc(s_hi, 1)

            def qk_high(b, g):
                for n in range(4):
                    wait(act, b_qk, b * 16 + g * 4 + n + 1)
                    wait(act, d_qk, b * 16 + max(g * 4 + n - 1, 0))
                    act.activation(qk_hi[n % 2][:, :], qk_bank[n][:, :], ACT.Copy).then_inc(a_qk, 1)

            def tanh(b, f):
                wait(act, b_gu, b * SFT + f + 1)
                wait(act, d_ga, b * SFT + max(f - 1, 0))
                m = P if f < SFT - 1 else SF_LAST
                act.activation(gate_th[f % 2][0:m, :], g_bank[0:m, :], ACT.Tanh, scale=0.5).then_inc(a_th, 1)

            with act.Fori(0, NB) as b:
                wait(act, b_xt, b + 1)
                for k in range(KT):
                    ins = act.activation(xT_b[:, HI, k, :], xT_bank[HI][k][:, :], ACT.Copy)
                ins.then_inc(a_xt, 1)
                for n in range(3):
                    wait(act, b_r, b * 3 + n + 1)
                    act.activation(r_rows[n][0:96, :], r_bank[n][0:96, :], ACT.Copy).then_inc(a_r, 1)
                for n in range(2):
                    wait(act, b_v, b * 2 + n + 1)
                    act.activation(v_ones[:, 2 * n:2 * n + 2, :, 0:HD],
                                   v_bank[n][:, :].rearrange("p (t h d) -> p t h d", t=2, h=HEADS), ACT.Copy).then_inc(a_v, 1)
                qk_high(b, 0)
                for g in range(NG):
                    if g < NG - 1:
                        qk_high(b, g + 1)
                        for f in range(2 * g, 2 * g + 2):
                            tanh(b, f)
                    for kt in range(TPB):
                        wait(act, b_pv, b * 16 + max(g * 4 + kt - 1, 0))
                        for j in range(4):
                            u = g * 16 + kt * 4 + j
                            wait(act, b_st, b * 64 + u + 1)
                            act.activation(prob[kt % 2][:, j, :], st_bank[u % 2][:, :], ACT.Exp, scale=HD ** -0.5).then_inc(a_exp, 1)
                    wait(act, b_pv, b * 16 + g * 4 + 4)
                    act.activation(o_T[:, g, :], ot_bank[:, :], ACT.Copy).then_inc(a_ot, 1)
                for t in range(TPB):
                    wait(act, b_at, b * TPB + t + 1)
                    act.activation(ao_T[:, HI, :, t * P:(t + 1) * P], ot_bank[:, 0:D].rearrange("p (k t) -> p k t", k=KT),
                                   ACT.Copy).then_inc(a_at, 1)
                wait(act, b_res, b + 1)
                act.activation(ro[:, :], m_bank[0:96, :], ACT.Copy).then_inc(a_res, 1)

        @block.tensor
        def _(pe):
            pe.wait_ge(consts, 2)
            pe.wait_ge(small_in, 16 * 13)
            for k in range(KT):
                pe.matmul(bank[0][:, k * P:(k + 1) * P], basis_raw[:, k * P:(k + 1) * P], ident_f[:, :], start=True, stop=True)
                ins = pe.matmul(bank[0][:, 256 + k * NE:256 + (k + 1) * NE], gate_raw[:, k * P:(k + 1) * P], ident_f[0:NE, 0:NE],
                                start=True, stop=True)
            ins.then_inc(pe_prep, 1)
            wait(pe, dve_a, A_THRICE)
            for i in range(len(PROJ)):
                for k in range(KT):
                    ins = pe.matmul(bank[(1, 7)[i // 2]][0:96, (i % 2) * D + k * P:(i % 2) * D + (k + 1) * P],
                                    w_thrice[:, i * KT + k, :, :].rearrange("p r h -> p (r h)"), ident_f[:, :], start=True, stop=True)
            ins.then_inc(pe_prep, 1)

            with pe.Fori(0, NB // 2) as b2:
                for i in range(2):
                    b = b2 * 2 + i
                    wait(pe, xhi_ok, b + 1)
                    wait(pe, xlo_ok, b + 1)
                    wait(pe, xt_hi, b)
                    wait(pe, xt_lo, b)
                    for part in (HI, LO):
                        for k in range(KT):
                            for t in range(TPB):
                                ins = pe.matmul(xt_bank[part][k][:, t * P:(t + 1) * P], x_rows[:, t, part, k * P:(k + 1) * P],
                                                ident_r[:, :], start=True, stop=True)
                    ins.then_inc(xt_ps, 1)
                    if i == 0:
                        pe.wait_ge(prep_done, 1)
                    wait(pe, xt_hi, b + 1)
                    wait(pe, xt_lo, b + 1)
                    for t in range(TPB):
                        o = lg_bank[:, bass.ds((b * TPB + t) * NE, NE)]
                        for n, (a, c) in enumerate(PRODUCTS):
                            for k in range(KT):
                                ins = pe.matmul(o, x_T[:, a, k, t * P:(t + 1) * P], gate_T[:, k, c, :],
                                                start=(n == 0 and k == 0), stop=(n == 2 and k == KT - 1))
                    ins.then_inc(lg_ps, 1)
            pe.wait_ge(hot_ok, 1)
            hb = hot_b[:, :, :].rearrange("p t e -> p (t e)")
            pe.matmul(bank[0][:, 0:NT * NE], upper[:, :], hb, start=True, stop=True)
            pe.matmul(bank[1][:, 0:NT * NE], ones_b[:, :], hb, start=True, stop=True).then_inc(count_ps, 1)

            def invert(t2, first=False, last=False):
                for n in range(4):
                    wait(pe, inv_ok, t2 * 4 + n + 1)
                    pe.matmul(bank[2][:, 0:NS], at_row[n][:, :], at_tile[n][:, :], start=first and n == 0,
                              stop=last and n == 3).then_inc(inv_ps, 1)

            invert(0, first=True)
            with pe.Fori(1, NT // 2 - 1) as t2:
                invert(t2)
            invert(NT // 2 - 1, last=True)

            def turn_x(s, i):
                wait(pe, c_x[i], (s // 4 + 1) * 16 if isinstance(s, int) else (s - i) * 4 + 16)
                wait(pe, c_xe, s)
                for n in range(2 * KT):
                    ins = pe.matmul(xg_bank[:, n * P:(n + 1) * P], xg[i][:, n * P:(n + 1) * P], ident_r[:, :], start=True, stop=True)
                ins.then_inc(c_xt, 1)

            def gate_up(s, i):
                e = pe.value_load(expert_of[0:1, s:s + 1] if isinstance(s, int) else expert_of[0:1, bass.ds(s, 1)],
                                  min_val=0, max_val=NE - 1)
                wait(pe, c_xe, s + 1)
                for n, (free, done) in enumerate(((c_sl, c_g), (c_hk, c_u))):
                    wait(pe, free, s - 1)
                    for m, (a, c) in enumerate(PRODUCTS):
                        for k in range(KT):
                            w = w_exp[:, bass.ds(e, 1), c, k * GU + n * F:k * GU + (n + 1) * F].rearrange("p a n -> p (a n)")
                            ins = pe.matmul(gu_bank[i % 2][n][:, 0:F], xg_T[i % 2][:, a * KT + k, :], w,
                                            start=(m == 0 and k == 0), stop=(m == 2 and k == KT - 1))
                    ins.then_inc(done, 1)

            def turn_h(s, i):
                wait(pe, c_lo, s + 1)
                wait(pe, c_hea, s)
                wait(pe, c_hed, s)
                for part, h in enumerate((c_hh, c_hl)):
                    for k in range(FT):
                        ins = pe.matmul(ht_bank[part][:, k * P:(k + 1) * P], h[i % 2][:, k * P:(k + 1) * P], ident_r[:, :],
                                        start=True, stop=True)
                ins.then_inc(c_ht, 1)

            def down(s, i):
                e = pe.value_load(expert_of[0:1, s:s + 1] if isinstance(s, int) else expert_of[0:1, bass.ds(s, 1)],
                                  min_val=0, max_val=NE - 1)
                wait(pe, c_hea, s + 1)
                wait(pe, c_hed, s + 1)
                wait(pe, c_yk, s)
                for m, (a, c) in enumerate(PRODUCTS):
                    for k in range(FT):
                        n = P if k < FT - 1 else F_LAST
                        w = w_exp[0:n, bass.ds(e, 1), c, W_GU + k * D:W_GU + (k + 1) * D].rearrange("p a n -> p (a n)")
                        ins = pe.matmul(y_bank[:, 0:D], c_hT[i % 2][0:n, a, k, :], w,
                                        start=(m == 0 and k == 0), stop=(m == 2 and k == FT - 1))
                ins.then_inc(c_d, 1)

            def step(s, i, first=False, last=False):
                gate_up(s, i)
                if not (first and i < 1):
                    turn_h(s - 1, (i - 1) % 4)
                if not (last and i == 3):
                    turn_x(s + 1, (i + 1) % 4)
                if not (first and i < 2):
                    down(s - 2, (i - 2) % 4)

            pe.wait_ge(a_done, 1)
            pe.wait_ge(hi_done, NE - 2)
            pe.wait_ge(lo_done, NE - 2)
            turn_x(0, 0)
            for i in range(4):
                step(i, i, first=True)
            pe.wait_ge(hi_done, NE)
            pe.wait_ge(lo_done, NE)
            with pe.Fori(1, NS // 4 - 1) as s4:
                for i in range(4):
                    step(s4 * 4 + i, i)
            for i in range(4):
                step(NS - 4 + i, i, last=True)
            turn_h(NS - 1, 3)
            down(NS - 2, 2)
            down(NS - 1, 3)

            pe.wait_ge(c_yk, NS)
            pe.wait_ge(c_hed, NS)

            def project(b, g):
                for n in range(4):
                    rows, w, k = (r_rows[0], wq_rows, 96) if n < 2 else (r_rows[1], wk_rows, 97)
                    pair = 2 * g + n % 2
                    if n == 3:
                        wait(pe, d_qk, b * 16 + g * 4 + 1)
                    pe.matmul(qk_bank[n][:, :], w[0:k, 2 * pair:2 * pair + 2, :].rearrange("p h j -> p (h j)"), rows[0:k, :],
                              start=True, stop=True).then_inc(b_qk, 1)

            def score(b, g, j, qt):
                u = g * 16 + j * 4 + qt
                r = 64 * (j % 2)
                if u % 16 == 0:
                    wait(pe, d_qk, b * 16 + g * 4 + 4)
                wait(pe, d_max, b * 64 + max(u - 1, 0))
                pe.matmul(s_bank[u % 2][:, :], q_rows[g % 2][r:r + 48, j // 2, qt * P:(qt + 1) * P], k_rows[g % 2][r:r + 48, j // 2, :],
                          start=True, stop=True).then_inc(b_s, 1)

            def turn_max(b, g):
                wait(pe, d_m, b * NG + g + 1)
                for qt in range(TPB):
                    ins = pe.matmul(m_bank[0:8, qt * P:(qt + 1) * P], top_parts[g % 2][:, qt, :, :, :].rearrange("p a b c -> p (a b c)").bitcast(F32),
                                    ident_f[:, :], start=True, stop=True)
                ins.then_inc(b_mt, 1)

            def gate_up_shared(b, f):
                m = P if f < SFT - 1 else SF_LAST
                wait(pe, d_hf, b * SFT + f)
                for n, dst in enumerate((g_bank, u_bank)):
                    for a, c in PRODUCTS:
                        for k in range(KT):
                            o = k * 2 * SF + n * SF + f * P
                            ins = pe.matmul(dst[0:m, :], w_sh[:, a, o:o + m], xT_b[:, c, k, :],
                                            start=((a, c) == PRODUCTS[0] and k == 0), stop=((a, c) == PRODUCTS[2] and k == KT - 1))
                ins.then_inc(b_gu, 1)

            def score_T(b, g, kt, j):
                u = g * 16 + kt * 4 + j
                r = 64 * (j % 2)
                wait(pe, a_exp, b * 64 + max(u - 1, 0))
                pe.matmul(st_bank[u % 2][:, :], k_rows[g % 2][r:r + QKV_ROWS, j // 2, kt * P:(kt + 1) * P],
                          q_rows[g % 2][r:r + QKV_ROWS, j // 2, :], start=True, stop=True).then_inc(b_st, 1)

            def values(b, g, kt):
                wait(pe, a_exp, b * 64 + g * 16 + kt * 4 + 4)
                if kt == 0:
                    wait(pe, a_ot, b * NG + g)
                for j in range(4):
                    ins = pe.matmul(ot_bank[32 * j:32 * j + 32, :], v_ones[:, kt, 4 * g + j, :], prob[kt % 2][:, j, :],
                                    start=(kt == 0), stop=(kt == TPB - 1))
                ins.then_inc(b_pv, 1)

            with pe.Fori(0, NB) as b:
                wait(pe, xr_in, (b + 1) * 16)
                wait(pe, d_max, b * 64)
                for part in (HI, LO):
                    for k in range(KT):
                        for t in range(TPB):
                            ins = pe.matmul(xT_bank[part][k][:, t * P:(t + 1) * P], xr_b[:, t, part, k * P:(k + 1) * P],
                                            ident_r[:, :], start=True, stop=True)
                ins.then_inc(b_xt, 1)
                wait(pe, a_xt, b + 1)
                wait(pe, d_xt, b + 1)
                wait(pe, d_out, b * TPB)
                for i in range(3):
                    for n, (a, c) in enumerate(PRODUCTS):
                        for k in range(KT):
                            ins = pe.matmul(r_bank[i][0:96, :], basis_T[:, k, a, i, :, :].rearrange("p r h -> p (r h)"), xT_b[:, c, k, :],
                                            start=(n == 0 and k == 0), stop=(n == 2 and k == KT - 1))
                    ins.then_inc(b_r, 1)
                wait(pe, d_r, b * 3 + 3)
                for n in range(2):
                    for t in range(2 * n, 2 * n + 2):
                        ins = pe.matmul(v_bank[n][:, (t % 2) * D:(t % 2 + 1) * D], r_rows[2][0:96, t * P:(t + 1) * P], wv_rows[:, :],
                                        start=True, stop=True)
                    ins.then_inc(b_v, 1)
                wait(pe, a_v, b * 2 + 2)
                project(b, 0)
                for j in range(4):
                    for qt in range(TPB):
                        score(b, 0, j, qt)
                for g in range(NG):
                    if g < NG - 1:
                        wait(pe, d_mt, b * NG + g)
                        project(b, g + 1)
                        wait(pe, d_qk, b * 16 + g * 4 + 8)
                    turn_max(b, g)
                    if g == 0:
                        pe.wait_ge(s_hi, 1)
                        pe.wait_ge(s_lo, 1)
                    if g < NG - 1:
                        gate_up_shared(b, 2 * g)
                        gate_up_shared(b, 2 * g + 1)
                    wait(pe, m_in[g % 2], b * 128 + 64 * (g // 2 + 1))
                    for kt in range(TPB):
                        for j in range(4):
                            score_T(b, g, kt, j)
                            if g < NG - 1:
                                score(b, g + 1, kt, j)
                            if kt and j == 1:
                                values(b, g, kt - 1)
                    values(b, g, TPB - 1)
                wait(pe, a_ot, b * NG + NG)
                for t in range(TPB + 1):
                    if t < TPB:
                        wait(pe, d_ao, b * TPB + t)
                        if t == 0:
                            wait(pe, d_mt, b * NG + NG)
                        for g in range(NG):
                            ins = pe.matmul(m_bank[:, g * P:(g + 1) * P], o_T[:, g, t * P:(t + 1) * P], ident_f[:, :], start=True, stop=True)
                        ins.then_inc(b_ot, 1)
                    if t:
                        wait(pe, d_ao, b * TPB + t)
                        wait(pe, a_at, b * TPB + max(t - 1, 0))
                        wait(pe, d_at, b * TPB + max(t - 1, 0))
                        for k in range(KT):
                            ins = pe.matmul(ot_bank[:, k * P:(k + 1) * P], ao[(t - 1) % 2][:, k * P:(k + 1) * P], ident_f[:, :], start=True, stop=True)
                        ins.then_inc(b_at, 1)
                wait(pe, a_at, b * TPB + TPB)
                wait(pe, d_at, b * TPB + TPB)
                for n, (a, c) in enumerate(PRODUCTS):
                    for k in range(KT):
                        ins = pe.matmul(m_bank[0:96, :], basis_T[:, k, a, 3, :, :].rearrange("p r h -> p (r h)"), ao_T[:, c, k, :],
                                        start=(n == 0 and k == 0), stop=(n == 2 and k == KT - 1))
                ins.then_inc(b_res, 1)
                wait(pe, d_h, b * SFT + SFT)
                for t in range(TPB):
                    dst = (g_bank, u_bank)[t % 2][:, 0:D]
                    wait(pe, d_out, b * TPB + max(t - 1, 0))
                    for n, (a, c) in enumerate(PRODUCTS):
                        for f in range(SFT):
                            m = P if f < SFT - 1 else SF_LAST
                            pe.matmul(dst, h_T[0:m, a, f, t * P:(t + 1) * P], w_sh[0:m, c, S_GU + f * D:S_GU + (f + 1) * D],
                                      start=(n == 0 and f == 0), stop=False)
                    if t == 0:
                        wait(pe, d_res, b + 1)
                    pe.matmul(dst, ro[:, t * P:(t + 1) * P], wo_rows[:, :], start=False, stop=True).then_inc(b_out, 1)

        @block.vector
        def _(dve):
            st = Steps(dve, dve_a)
            dve.wait_ge(small_in, 16 * 13)
            ph = phase[:, :, :, :].rearrange("p i k h -> p (i k h)")
            am = amp[:, :, :, :].rearrange("p i k h -> p (i k h)")
            st.then(dve.tensor_scalar(turns[:, :], ph, 1 / (2 * math.pi), 0.25, ALU.mult, ALU.add))
            st.then(dve.tensor_scalar(turns[:, :], turns[:, :], ROUNDER, ROUNDER, ALU.add, ALU.subtract))
            st.then(dve.scalar_tensor_tensor(angle[:, :], turns[:, :], -TURN_1, ph, ALU.mult, ALU.add))
            st.then(dve.scalar_tensor_tensor(angle[:, :], turns[:, :], -TURN_2, angle[:, :], ALU.mult, ALU.add))
            st.then(dve.scalar_tensor_tensor(angle[:, :], turns[:, :], -TURN_3, angle[:, :], ALU.mult, ALU.add))
            st.then(dve.tensor_scalar(angle[:, :], angle[:, :], math.pi / 2, PI_BELOW, ALU.add, ALU.min))
            st.then(dve.tensor_scalar(angle[:, :], angle[:, :], -PI_BELOW, None, ALU.max))
            assert st.n == A_ANGLE
            st.did(dve.memset(q_minus[:, :], 0.0))
            st.then(dve.memset(k_minus[:, :], 0.0))
            for h in range(2):
                st.did(dve.memset(q_minus[64 * h + 32:64 * h + 48, :], -1.0))
                st.did(dve.memset(k_minus[64 * h:64 * h + 32, :], -1.0))
            st.wait()
            for h in range(2):
                st.did(dve.memset(k_minus[64 * h:64 * h + 16, :], 0.0))
            dve.wait_ge(consts, 2)
            st.did(dve.memset(wk_rows[96:97, :, 48:50].bitcast(F32), -1.0))
            dve.wait_ge(pe_prep, 1)
            for k in range(KT):
                b = bank[0][:, k * P:(k + 1) * P].rearrange("p (i r h) -> p i r h", i=len(PROJ), r=1)
                b = b.to_broadcast([P, len(PROJ), 3, HARM])
                g = bank[0][:, 256 + k * NE:256 + (k + 1) * NE]
                st.did(dve.tensor_copy(basis_T[:, k, HI, :, :, :], b))
                st.then(dve.tensor_copy(gate_T[:, k, HI, :], g))
                st.did(dve.tensor_tensor(basis_T[:, k, LO, :, :, :], b, basis_T[:, k, HI, :, :, :].bitcast(F32), ALU.subtract))
                st.did(dve.tensor_tensor(gate_T[:, k, LO, :], g, gate_T[:, k, HI, :].bitcast(F32), ALU.subtract))
            dve.wait_ge(sin_done, 1)
            sn = angle[:, :].rearrange("p (i r h) -> p i r h", r=1, h=HARM).to_broadcast([P, len(PROJ) * KT, 3, HARM])
            ab = am.rearrange("p (i r h) -> p i r h", r=1, h=HARM).to_broadcast([P, len(PROJ) * KT, 3, HARM])
            st.then(dve.tensor_tensor(w_thrice[:, :, :, :], sn, ab, ALU.mult))
            assert st.n == A_THRICE
            for q in range(4):
                dve.wait_ge(x_in[q], 16 * (NB // 4))
                for n in range(q * NT // 4, (q + 1) * NT // 4):
                    ins = dve.bn_stats(stats[:, n, :], x_all[:, n, :])
                st.did(ins)
            dve.wait_ge(pe_prep, 2)
            dve.wait_ge(consts, 2)
            for i in range(len(PROJ)):
                st.did(dve.tensor_copy(w_hi[:, i, :], bank[(1, 7)[i // 2]][0:96, (i % 2) * D:(i % 2 + 1) * D]))
            st.wait()
            for i in range(len(PROJ)):
                src = bank[(1, 7)[i // 2]][0:96, (i % 2) * D:(i % 2 + 1) * D]
                st.did(dve.tensor_tensor(w_hi[32:64, i, :], src[32:64, :], w_hi[32:64, i, :].bitcast(F32), ALU.subtract))
            st.wait()
            for i, dst in enumerate((wq_rows, wk_rows)):
                v = w_hi[:, i, :].rearrange("p (h r j) -> p h r j", h=HEADS, r=1).to_broadcast([96, HEADS, 3, HD]).bitcast(F32)
                st.did(dve.tensor_copy(dst[0:96, :, 0:48].rearrange("p h (r j) -> p h r j", r=3), v))
            st.did(dve.tensor_copy(wv_rows[:, :], w_hi[:, 2, :].bitcast(F32)))
            st.did(dve.tensor_copy(wo_rows[:, :], w_hi[:, 3, :].bitcast(F32)))
            for n in range(NT):
                ins = dve.bn_aggr(mean_var[:, n, :], stats[:, n, :])
            st.then(ins)
            dve.tensor_scalar(rs[:, 0, :], mean_var[:, :, 1], LN_EPS, None, ALU.add).then_inc(stats_ok, 1)
            dve.wait_ge(root_ok, 1)
            st.then(dve.reciprocal(rs[:, 2, :], rs[:, 1, :]))
            st.then(dve.tensor_tensor(rs[:, 3, :], rs[:, 2, :], rs[:, 2, :], ALU.mult))
            st.then(dve.tensor_tensor(rs[:, 3, :], rs[:, 3, :], rs[:, 0, :], ALU.mult))
            st.then(dve.tensor_scalar(rs[:, 3, :], rs[:, 3, :], -0.5, 1.5, ALU.mult, ALU.add))
            st.then(dve.tensor_tensor(rs[:, 3, :], rs[:, 2, :], rs[:, 3, :], ALU.mult))
            dve.memset(rs[:, 1, :], 0.0).then_inc(prep_done, 1)

            def low_T(i):
                for k in range(KT):
                    ins = dve.tensor_copy(x_T[:, LO, k, :], xt_bank[LO][k][:, :])
                ins.then_inc(xt_lo, 1)

            with dve.Fori(0, NB // 2) as b2:
                for i in range(2):
                    b = b2 * 2 + i
                    for t in range(TPB):
                        n = b * TPB + t
                        xt = x_all[:, bass.ds(n, 1), :].rearrange("p a d -> p (a d)")
                        ins = dve.tensor_scalar(xt, xt, mean_var[:, bass.ds(n, 1), 0:1].rearrange("p a c -> p (a c)"),
                                                rs[:, 3, bass.ds(n, 1)], ALU.subtract, ALU.mult)
                    ins.then_inc(xn_ok, 1)
                    wait(dve, xhi_ok, b + 1)
                    wait(dve, xn_ok, b + 1)
                    dve.tensor_tensor(x_rows[:, :, LO, :], x_all[:, bass.ds(b * TPB, TPB), :],
                                      x_rows[:, :, HI, :].bitcast(F32), ALU.subtract).then_inc(xlo_ok, 1)
                    wait(dve, xt_ps, b + 1)
                    wait(dve, lg_ps, b)
                    low_T(i)

            def over_e(v):
                return v.rearrange("p (t r) -> p t r", r=1).to_broadcast([P, NT, NE])

            def over_t(v):
                return v.rearrange("p (r e) -> p r e", r=1).to_broadcast([P, NT, NE])

            dve.wait_ge(lg_ps, NB)
            st.then(dve.tensor_reduce(row[:, 0, :], lg_bank[:, 0:NT * NE].rearrange("p (t e) -> p t e", e=NE), AX_X, ALU.max))
            dve.tensor_tensor(lg[:, :, :], lg_bank[:, 0:NT * NE].rearrange("p (t e) -> p t e", e=NE),
                              over_e(row[:, 0, :]), ALU.subtract).then_inc(lg_max, 1)
            dve.wait_ge(lg_exp, 1)
            st.then(dve.tensor_reduce(row[:, 1, :], pr[:, :, :], AX_X, ALU.add))
            st.then(dve.reciprocal(row[:, 2, :], row[:, 1, :]))
            st.then(dve.tensor_tensor(pr[:, :, :], pr[:, :, :], over_e(row[:, 2, :]), ALU.mult))
            for n in range(NT):
                ins = dve.max(best[:, n, :], pr[:, n, :])
            st.then(ins)
            for n in range(NT):
                ins = dve.max_index(best_at[:, n, :], best[:, n, :], pr[:, n, :])
            st.did(ins)
            st.then(dve.tensor_tensor(row[:, 3, :], best[:, :, 0], best[:, :, 1], ALU.add))
            st.then(dve.tensor_scalar(row[:, 3, :], row[:, 3, :], TOPK_EPS, None, ALU.add))
            st.then(dve.reciprocal(row[:, 0, :], row[:, 3, :]))
            for k in range(2):
                st.did(dve.scalar_tensor_tensor(share[:, :, k], best[:, :, k], ROUTE_SCALE, row[:, 0, :], ALU.mult, ALU.mult))
                st.did(dve.tensor_copy(best_atf[:, k, :], best_at[:, :, k]))
            st.wait()
            for k in range(2):
                st.did(dve.tensor_tensor(hot[k][:, :, :], over_e(best_atf[:, k, :]), over_t(iota_e[:, :]), ALU.is_equal))
            st.wait()
            st.did(dve.tensor_tensor(hot_b[:, :, :], hot[0][:, :, :], hot[1][:, :, :], ALU.add))
            st.wait()
            dve.memset(row[:, 1, :], 0.0).then_inc(hot_ok, 1)
            dve.wait_ge(count_ps, 1)
            st.then(dve.tensor_copy(totals[:, :, :], bank[1][:, 0:NT * NE].rearrange("p (t e) -> p e t", e=NE)))
            for e in range(NE):
                st.did(dve.tensor_tensor_scan(before[:, e, :], totals[:, e, :], zeros[:, :], 0.0, ALU.add, ALU.add))
            st.wait()
            st.then(dve.tensor_scalar(tiles[:, 0, :], before[:, :, NT - 1], 1 / P, (P - 1) / P - 0.5 + 1 / 512, ALU.mult, ALU.add))
            st.then(dve.tensor_scalar(tiles[:, 0, :], tiles[:, 0, :], ROUNDER, ROUNDER, ALU.add, ALU.subtract))
            st.then(dve.tensor_scalar(tiles[:, 1, :], tiles[:, 0, :], 1.0, None, ALU.max))
            st.then(dve.tensor_tensor_scan(tiles[:, 2, :], tiles[:, 1, :], zeros[:, 0:NE], 0.0, ALU.add, ALU.add))
            st.then(dve.tensor_tensor(tiles[:, 3, :], tiles[:, 2, :], tiles[:, 1, :], ALU.subtract))
            st.then(dve.tensor_tensor(before[:, :, :], before[:, :, :], totals[:, :, :], ALU.subtract))
            st.then(dve.tensor_tensor(slot_base[:, :, :], bank[0][:, 0:NT * NE].rearrange("p (t e) -> p t e", e=NE),
                                      before[:, :, :].rearrange("p e t -> p t e"), ALU.add))
            st.then(dve.scalar_tensor_tensor(slot_base[:, :, :], over_t(tiles[:, 3, :]), float(P), slot_base[:, :, :], ALU.mult, ALU.add))
            for k in range(2):
                st.then(dve.tensor_tensor(slot_hot[:, :, :], slot_base[:, :, :], hot[k][:, :, :], ALU.mult))
                st.then(dve.tensor_reduce(slot_f[:, k, :], slot_hot[:, :, :], AX_X, ALU.add))
            st.did(dve.tensor_copy(slot_of[:, :, :], slot_f[:, :, :]))
            st.then(dve.tensor_scalar(slot_q[:, :, :], slot_f[:, :, :], 1 / P, 1 / 512 - 0.5, ALU.mult, ALU.add))
            st.then(dve.tensor_scalar(slot_q[:, :, :], slot_q[:, :, :], ROUNDER, ROUNDER, ALU.add, ALU.subtract))
            st.did(dve.scalar_tensor_tensor(slot_r[:, :, :], slot_q[:, :, :], -float(P), slot_f[:, :, :], ALU.mult, ALU.add))
            st.then(dve.tensor_tensor(started[:, :, :], iota_s[0:1, :].rearrange("p (s r) -> p s r", r=1).to_broadcast([1, NS, NE]),
                                      tiles[0:1, 3, :].rearrange("p (r e) -> p r e", r=1).to_broadcast([1, NS, NE]), ALU.is_ge))
            st.then(dve.tensor_reduce(started_n[:, :], started[:, :, :], AX_X, ALU.add))
            st.did(dve.tensor_scalar(expert_of[:, :], started_n[:, :], -1.0, None, ALU.add))
            st.wait()

            def one_hots(t2, ring):
                for n in range(4):
                    t, k = t2 * 2 + n // 2, n % 2
                    if ring:
                        wait(dve, inv_ps, t2 * 4 - 3 + n)
                    one = (lambda v: v[:, k, t:t + 1]) if isinstance(t, int) else (lambda v: v[:, k, bass.ds(t, 1)])
                    tid = token_id[:, t:t + 1] if isinstance(t, int) else token_id[:, bass.ds(t, 1)]
                    dve.tensor_scalar(at_row[n][:, :], iota_r[:, :], one(slot_r), None, ALU.is_equal)
                    dve.tensor_scalar(at_tile[n][:, :], iota_s[:, :], one(slot_q), tid, ALU.is_equal, ALU.mult).then_inc(inv_ok, 1)

            one_hots(0, False)
            with dve.Fori(1, NT // 2) as t2:
                one_hots(t2, True)
            dve.wait_ge(inv_ps, 2 * NT)
            st.then(dve.tensor_copy(token_of[:, :], bank[2][:, 0:NS]))
            for i in range(2):
                st.did(dve.memset(c_hh[i][:, F:FT * P].bitcast(F32), 0.0))
                st.did(dve.memset(c_hl[i][:, F:FT * P].bitcast(F32), 0.0))
            st.wait()
            dve.memset(zeros[:, :], 0.0).then_inc(a_done, 1)

            def hidden(s, i):
                wait(dve, c_sl, s + 1)
                wait(dve, c_u, s + 1)
                wait(dve, c_lo, s - 1)
                dve.tensor_tensor(c_h[i % 2][:, :], c_sil[i % 2][:, :], gu_bank[i % 2][1][:, 0:F], ALU.mult).then_inc(c_hk, 1)
                wait(dve, c_hk, s + 1)
                wait(dve, c_ht, s - 1)
                dve.tensor_copy(c_hh[i % 2][:, 0:F], c_h[i % 2][:, :]).then_inc(c_hi, 1)
                wait(dve, c_hi, s + 1)
                dve.tensor_tensor(c_hl[i % 2][:, 0:F], c_h[i % 2][:, :], c_hh[i % 2][:, 0:F].bitcast(F32), ALU.subtract).then_inc(c_lo, 1)

            def h_out(s, i):
                wait(dve, c_ht, s + 1)
                wait(dve, c_d, s - 1)
                dve.tensor_copy(c_hT[i % 2][:, LO, :, :].rearrange("p a t -> p (a t)"), ht_bank[LO][:, 0:FT * P]).then_inc(c_hed, 1)

            def step(s, i, first=False):
                hidden(s, i)
                if not (first and i < 1):
                    h_out(s - 1, (i - 1) % 4)

            for i in range(4):
                step(i, i, first=True)
            with dve.Fori(1, NS // 4) as s4:
                for i in range(4):
                    step(s4 * 4 + i, i)
            h_out(NS - 1, 3)

            dve.wait_ge(c_yk, NS)
            for i in range(4):
                dve.wait_ge(c_st[i], 16 * (NS // 4))
            dve.memset(s_raw[64:128, S_GU + (SFT - 1) * D:S_ALL], 0.0).then_inc(s_pad, 1)
            dve.memset(r_rows[1][96:97, :].bitcast(F32), 1.0)
            dve.memset(v_ones[:, :, :, HD:2 * HD], 1.0)
            dve.wait_ge(s_in, 64)
            dve.wait_ge(s_hi, 1)
            dve.tensor_tensor(w_sh[:, LO, :], s_raw[:, :], w_sh[:, HI, :].bitcast(F32), ALU.subtract).then_inc(s_lo, 1)
            dve.wait_ge(s_lo, 1)

            def qk_split(b, g):
                for n in range(4):
                    minus, dst = (q_minus, q_rows) if n < 2 else (k_minus, k_rows)
                    wait(dve, a_qk, b * 16 + g * 4 + n + 1)
                    if n == 0:
                        wait(dve, b_st, b * 64 + max(g * 16 - 16, 0))
                    dve.scalar_tensor_tensor(dst[g % 2][:, n % 2, :], qk_hi[n % 2][:, :].bitcast(F32), minus[:, 0:1], qk_bank[n][:, :],
                                             ALU.mult, ALU.add).then_inc(d_qk, 1)

            def maximum(b, g, j, qt):
                u = g * 16 + j * 4 + qt
                wait(dve, b_s, b * 64 + u + 1)
                if u % 16 == 0:
                    wait(dve, d_m, b * NG + max(g - 1, 0))
                dve.tensor_reduce(top[g % 2][:, j % 2, j // 2, qt:qt + 1], s_bank[u % 2][:, :], AX_X, ALU.max).then_inc(d_max, 1)

            def split_max(b, g):
                wait(dve, d_max, b * 64 + g * 16 + 16)
                wait(dve, b_mt, b * NG + max(g - 1, 0))
                dst = top_parts[g % 2]
                src = top[g % 2][:, :, :, :].rearrange("p a b t -> p t a b")
                dve.tensor_copy(dst[:, :, :, :, HI], src).then_inc(d_mh, 1)
                wait(dve, d_mh, b * NG + g + 1)
                dve.tensor_tensor(dst[:, :, :, :, LO], src, dst[:, :, :, :, HI].bitcast(F32), ALU.subtract).then_inc(d_m, 1)

            def max_rows(b, g):
                wait(dve, b_mt, b * NG + g + 1)
                wait(dve, m_in[g % 2], b * 128 + 64 * (g // 2))
                dve.tensor_copy(top_T[g % 2][:, :], m_bank[0:8, :]).then_inc(d_mt, 1)

            def hidden_shared(b, f):
                m = P if f < SFT - 1 else SF_LAST
                i = f % 2
                wait(dve, b_gu, b * SFT + f + 1)
                wait(dve, a_th, b * SFT + f + 1)
                wait(dve, d_hf, b * SFT + max(f - 1, 0))
                dve.scalar_tensor_tensor(gate_a[i][0:m, :], gate_th[i][0:m, :], 1.0, u_bank[0:m, :], ALU.add, ALU.mult).then_inc(d_ga, 1)
                wait(dve, d_ga, b * SFT + f + 1)
                wait(dve, d_h, b * SFT + max(f - 1, 0))
                dve.scalar_tensor_tensor(h_f[i][0:m, :], gate_a[i][0:m, :], 0.5, g_bank[0:m, :], ALU.mult, ALU.mult).then_inc(d_hf, 1)
                wait(dve, d_hf, b * SFT + f + 1)
                wait(dve, b_out, b * TPB)
                dve.tensor_copy(h_T[0:m, HI, f, :], h_f[i][0:m, :]).then_inc(d_hh, 1)
                wait(dve, d_hh, b * SFT + f + 1)
                dve.tensor_tensor(h_T[0:m, LO, f, :], h_f[i][0:m, :], h_T[0:m, HI, f, :].bitcast(F32), ALU.subtract).then_inc(d_h, 1)

            with dve.Fori(0, NB) as b:
                wait(dve, b_xt, b + 1)
                for k in range(KT):
                    ins = dve.tensor_copy(xT_b[:, LO, k, :], xT_bank[LO][k][:, :])
                ins.then_inc(d_xt, 1)
                for n in range(3):
                    wait(dve, a_r, b * 3 + n + 1)
                    dve.tensor_tensor(r_rows[n][64:96, :], r_bank[n][64:96, :], r_rows[n][64:96, :].bitcast(F32), ALU.subtract).then_inc(d_r, 1)
                qk_split(b, 0)
                for j in range(4):
                    for qt in range(TPB):
                        maximum(b, 0, j, qt)
                split_max(b, 0)
                for g in range(NG):
                    if g < NG - 1:
                        qk_split(b, g + 1)
                    max_rows(b, g)
                    if g < NG - 1:
                        hidden_shared(b, 2 * g)
                        hidden_shared(b, 2 * g + 1)
                        for kt in range(TPB):
                            for j in range(4):
                                maximum(b, g + 1, kt, j)
                        split_max(b, g + 1)
                for t in range(TPB + 1):
                    if t < TPB:
                        ov = m_bank[:, :].rearrange("p (h c) -> p h c", h=HEADS)
                        wait(dve, b_ot, b * TPB + t + 1)
                        wait(dve, d_ao, b * TPB + max(t - 1, 0))
                        dve.reciprocal(o_inv[:, t % 2, :], ov[:, :, HD]).then_inc(d_inv, 1)
                        wait(dve, d_inv, b * TPB + t + 1)
                        wait(dve, b_at, b * TPB + max(t - 1, 0))
                        dve.tensor_tensor(ao[t % 2][:, :].rearrange("p (h d) -> p h d", h=HEADS), ov[:, :, 0:HD],
                                          o_inv[:, t % 2, :].rearrange("p (h r) -> p h r", r=1).to_broadcast([P, HEADS, HD]),
                                          ALU.mult).then_inc(d_ao, 1)
                    if t:
                        wait(dve, a_at, b * TPB + t)
                        o = ao_T[:, :, :, (t - 1) * P:t * P]
                        dve.tensor_tensor(o[:, LO, :, :], ot_bank[:, 0:D].rearrange("p (k t) -> p k t", k=KT), o[:, HI, :, :].bitcast(F32),
                                          ALU.subtract).then_inc(d_at, 1)
                wait(dve, a_res, b + 1)
                dve.tensor_tensor(ro[64:96, :], m_bank[64:96, :], ro[64:96, :].bitcast(F32), ALU.subtract).then_inc(d_res, 1)
                wait(dve, xb_in, (b + 1) * 16)
                wait(dve, y_in, (b + 1) * TPB * 32)
                for t in range(TPB):
                    wait(dve, b_out, b * TPB + t + 1)
                    wait(dve, o_st[t], b * 16)
                    dve.tensor_tensor(o_b[t][:, :], (g_bank, u_bank)[t % 2][:, 0:D], x_b[:, t, :], ALU.add).then_inc(d_sum, 1)
                    for k in range(2):
                        wait(dve, d_sum, b * TPB * 2 + t * 2 + k + 1)
                        dve.scalar_tensor_tensor(o_b[t][:, :], y_b[:, t, k, :], share[:, bass.ds(b * TPB + t, 1), k:k + 1].rearrange("p a c -> p (a c)"),
                                                 o_b[t][:, :], ALU.mult, ALU.add).then_inc((d_sum, d_out)[k], 1)


A_ANGLE = 7
A_THRICE = 25


_INS = (["L0_attn_x"] + [f"L0_attn_{what}_{name}" for name in "qkvo" for what in ("basis", "phase", "amp")]
        + [f"L0_ffn_{name}" for name in ("gate_w", "w_gate", "w_up", "w_down", "sw_gate", "sw_up", "sw_down")])


def kernel(**inputs):
    import numpy as _np
    import concourse.bacc as _bacc
    from concourse import mybir as _mybir
    from concourse.bass_utils import run_bass_kernel_spmd as _run

    nc = _bacc.Bacc("TRN2", target_bir_lowering=False, num_devices=1)
    arrays, args = {}, {}
    for name in _INS:
        a = _np.ascontiguousarray(inputs[name])
        arrays[f"in_{name}_dram"] = a
        args[name] = nc.dram_tensor(f"in_{name}_dram", a.shape, _mybir.dt.from_np(a.dtype), kind="ExternalInput").ap()
    x = inputs["L0_attn_x"]
    out = nc.dram_tensor("out_0_dram", x.shape, _mybir.dt.from_np(_np.dtype("float32")), kind="ExternalOutput").ap()
    attn = {name: tuple(args[f"L0_attn_{what}_{name}"] for what in ("basis", "phase", "amp")) for name in "qkvo"}
    build_program(nc, args["L0_attn_x"], attn, *(args[f"L0_ffn_{name}"] for name in
                                                 ("gate_w", "w_gate", "w_up", "w_down", "sw_gate", "sw_up", "sw_down")), out)
    r = _run(nc, [arrays], core_ids=[0])
    return r.results[0]["out_0_dram"]
```

```python
import math
from contextlib import ExitStack

import concourse.bass as bass
from concourse import mybir

P = 128
ALU = mybir.AluOpType
ACT = mybir.ActivationFunctionType
AX_X = mybir.AxisListType.X
F32 = mybir.dt.float32
F32R = mybir.dt.float32r
BF16 = mybir.dt.bfloat16
I32 = mybir.dt.int32
U32 = mybir.dt.uint32

HI, LO = 0, 1
PRODUCTS = ((HI, HI), (LO, HI), (HI, LO))

LN_EPS = 1e-5
TOPK_EPS = 1e-20
ROUTE_SCALE = 2.5
TURN_1 = 6.28125
TURN_2 = math.floor((2 * math.pi - TURN_1) * 2**21) / 2**21
TURN_3 = 2 * math.pi - TURN_1 - TURN_2
PI_BELOW = 3.1415925
ROUNDER = 1.5 * 2**23


class Steps:

    def __init__(self, eng, sem, base=0):
        self.eng, self.sem, self.base, self.n = eng, sem, base, 0

    def did(self, ins):
        ins.then_inc(self.sem, 1)
        self.n += 1
        return self.n

    def value(self, n=None):
        return self.base + (self.n if n is None else n)

    def wait(self, n=None):
        self.eng.wait_ge(self.sem, self.value(n))

    def then(self, ins):
        self.did(ins)
        self.wait()


def wait(eng, sem, value):
    if isinstance(value, int) and value <= 0:
        return
    eng.wait_ge(sem, value)


def build_program(nc, x, attn, gate_w, w_gate, w_up, w_down, sw_gate, sw_up, sw_down, out):
    NB, L, D = x.shape
    NE, _, F = w_gate.shape
    SF = sw_gate.shape[1]
    HARM = attn["q"][0].shape[0]
    HEADS = 16
    HD = D // HEADS
    PROJ = ("q", "k", "v", "o")
    KT = D // P
    TPB = L // P
    NT = NB * TPB
    FT = -(-F // P)
    F_LAST = F - (FT - 1) * P
    GU = 2 * F
    W_GU = KT * GU
    W_ALL = W_GU + FT * D
    NS = 2 * NT + NE
    N_RING = 4
    PAIRS = NB // 2
    assert NB == NE

    xn_dram = nc.dram_tensor("xn_rows", (NB * L, D), F32).ap()
    xT_dram = nc.dram_tensor("xn_T_split", (NB, P, 2 * KT * L), F32).ap()
    y_dram = nc.dram_tensor("expert_rows", (NS * P, D), F32).ap()

    ctx = ExitStack()

    def sb(name, shape, dt, where=None):
        return (where or ctx).enter_context(nc.sbuf_tensor(name, shape, dt))

    def sem(name):
        return ctx.enter_context(nc.semaphore(name))

    with ctx:
        bank = [ctx.enter_context(nc.psum_tensor(f"bank{i}", [P, 512], F32)) for i in range(8)]

        ident_f = sb("ident_f", [P, P], F32)
        q_minus = sb("q_minus", [P, 1], F32)
        k_minus = sb("k_minus", [P, 1], F32)
        basis_T = sb("basis_T", [P, KT, 2, len(PROJ), 3, HARM], F32R)
        wq_rows = sb("wq_rows", [97, HEADS, 64], F32R)
        wk_rows = sb("wk_rows", [97, HEADS, 64], F32R)
        wv_rows = sb("wv_rows", [96, D], F32R)
        wo_rows = sb("wo_rows", [96, D], F32R)
        share = sb("share", [P, NT, 2], F32)
        slot_of = sb("slot_of", [P, 2, NT], I32)
        token_of = sb("token_of", [P, NS], I32)
        expert_of = sb("expert_of", [1, NS], I32)

        early = ExitStack()
        w_exp = sb("w_exp", [P, NE, 2, W_ALL], F32R, early)
        raw_all = sb("raw_all", [P, 2 * W_ALL], F32, early)
        raw = [raw_all[:, i * W_ALL:(i + 1) * W_ALL] for i in range(2)]
        zeros = sb("zeros", [P, NT], F32, early)

        region = ExitStack()
        x_all = sb("x_all", [P, NT, D], F32, region)
        gate_T = sb("gate_T", [P, KT, 2, NE], F32R, region)
        stats = sb("stats", [P, NT, 6], F32, region)
        mean_var = sb("mean_var", [P, NT, 2], F32, region)
        rs = sb("rs", [P, 4, NT], F32, region)
        iota_e = sb("iota_e", [P, NE], F32, region)
        iota_s = sb("iota_s", [P, NS], F32, region)
        iota_r = sb("iota_r", [P, P], F32, region)
        token_id = sb("token_id", [P, NT], F32, region)
        region.close()

        in_c = ExitStack()
        xg = [sb(f"xg{i}", [P, D], F32, in_c) for i in range(4)]
        xg_T = [sb(f"xg_T{i}", [P, 2 * KT, P], F32R, in_c) for i in range(2)]
        c_sil = [sb(f"c_sil{i}", [P, F], F32, in_c) for i in range(2)]
        c_h = [sb(f"c_h{i}", [P, FT * P], F32, in_c) for i in range(2)]
        c_hT = [sb(f"c_hT{i}", [P, 2, FT, P], F32R, in_c) for i in range(2)]
        c_y = [sb(f"c_y{i}", [P, D], F32, in_c) for i in range(4)]
        in_c.close()
        early.close()

        tail = ExitStack()
        sb("first_experts", [P, NE - 2, 2, W_ALL], F32R, tail)
        x_n = [sb(f"x_n{i}", [P, TPB, D], F32, tail) for i in range(2)]
        x_T = [sb("x_T0", [P, 2, KT, L], F32R, tail)]
        upper = sb("upper", [P, P], BF16, tail)
        ones_b = sb("ones_b", [P, P], BF16, tail)
        second = ExitStack()
        x_T.append(sb("x_T1", [P, 2, KT, L], F32R, second))
        second.close()
        prep = ExitStack()
        gate_raw = sb("gate_raw", [NE, D], F32, prep)
        basis_raw = sb("basis_raw", [P, D], F32, prep)
        phase = sb("phase", [P, len(PROJ), KT, HARM], F32, prep)
        amp = sb("amp", [P, len(PROJ), KT, HARM], F32, prep)
        turns = sb("turns", [P, len(PROJ) * KT * HARM], F32, prep)
        angle = sb("angle", [P, len(PROJ) * KT * HARM], F32, prep)
        w_thrice = sb("w_thrice", [P, len(PROJ) * KT, 3, HARM], F32, prep)
        w_hi = sb("w_hi", [96, len(PROJ), D], F32R, prep)
        prep.close()
        lg = sb("lg", [P, NT, NE], F32, tail)
        pr = sb("pr", [P, NT, NE], F32, tail)
        best = sb("best", [P, NT, NE], F32, tail)
        best_at = sb("best_at", [P, NT, NE], U32, tail)
        best_atf = sb("best_atf", [P, 2, NT], F32, tail)
        row = sb("row", [P, 4, NT], F32, tail)
        hot = [sb(f"hot{k}", [P, NT, NE], F32, tail) for k in range(2)]
        hot_b = sb("hot_b", [P, NT, NE], BF16, tail)
        before = sb("before", [P, NE, NT], F32, tail)
        totals = sb("totals", [P, NE, NT], F32, tail)
        tiles = sb("tiles", [P, 4, NE], F32, tail)
        slot_base, slot_hot = pr, lg
        slot_f = sb("slot_f", [P, 2, NT], F32, tail)
        slot_q = sb("slot_q", [P, 2, NT], F32, tail)
        slot_r = sb("slot_r", [P, 2, NT], F32, tail)
        started = sb("started", [1, NS, NE], F32, tail)
        started_n = sb("started_n", [1, NS], F32, tail)
        at_row = [sb(f"at_row{i}", [P, P], F32R, tail) for i in range(N_RING)]
        at_tile = [sb(f"at_tile{i}", [P, NS], F32R, tail) for i in range(N_RING)]
        tail.close()

        SFT = -(-SF // P)
        SF_LAST = SF - (SFT - 1) * P
        S_GU = KT * 2 * SF
        S_ALL = S_GU + SFT * D
        NG = HEADS // 4
        QKV_ROWS = 50
        late = ExitStack()
        w_sh = sb("w_sh", [P, 2, S_ALL], F32R, late)
        xT_b = sb("xT_b", [P, 2, KT, L], F32R, late)
        r_rows = [sb(f"r_{n}", [97, L], F32R, late) for n in "qkv"]
        qk_hi = [sb(f"qk_hi{i}", [P, L], F32R, late) for i in range(2)]
        q_rows = [sb(f"q_rows{g}", [P, 2, L], F32R, late) for g in range(NG)]
        k_rows = [sb(f"k_rows{g}", [P, 2, L], F32R, late) for g in range(NG)]
        top = [sb(f"top{i}", [P, 2, 2, TPB], F32, late) for i in range(2)]
        top_parts = [sb(f"top_parts{i}", [P, TPB, 2, 2, 2], F32R, late) for i in range(2)]
        top_T = [sb(f"top_T{i}", [8, L], F32R, late) for i in range(2)]
        prob = [sb(f"prob{i}", [P, 4, L], F32, late) for i in range(2)]
        v_ones = sb("v_ones", [P, TPB, HEADS, 2 * HD], F32, late)
        o_T = sb("o_T", [P, NG, L], F32, late)
        o_inv = sb("o_inv", [P, 2, HEADS], F32, late)
        ao = [sb(f"ao{i}", [P, D], F32, late) for i in range(2)]
        ao_T = sb("ao_T", [P, 2, KT, L], F32R, late)
        ro = sb("ro", [96, L], F32R, late)
        h_f = [sb(f"h_f{i}", [P, L], F32, late) for i in range(2)]
        o_b = sb("o_b", [P, TPB, D], F32, late)
        y_b = sb("y_b", [P, TPB, 2, D], F32, late)
        s_raw = raw_all
        assert S_ALL == 2 * W_ALL
        h_T = sb("h_T", [P, 2, SFT, L], F32R, late)
        late.close()

        x_in = [sem(f"x_in{q}") for q in range(4)]
        small_in = sem("small_in")
        raw_in = [sem(f"raw_in{i}") for i in range(2)]
        hi_done = sem("hi_done")
        lo_done = sem("lo_done")
        consts = sem("consts")
        dve_a = sem("dve_a")
        act_a = sem("act_a")
        sin_done = sem("sin_done")
        pe_prep = sem("pe_prep")
        prep_done = sem("prep_done")
        stats_ok = sem("stats_ok")
        root_ok = sem("root_ok")
        rs_ok = sem("rs_ok")
        xn_ok = sem("xn_ok")
        xn_stored = [sem(f"xn_stored{i}") for i in range(2)]
        xT_stored = [sem(f"xT_stored{i}") for i in range(2)]
        xt_ps = sem("xt_ps")
        xt_hi = sem("xt_hi")
        xt_lo = sem("xt_lo")
        lg_ps = sem("lg_ps")
        lg_max = sem("lg_max")
        lg_exp = sem("lg_exp")
        hot_ok = sem("hot_ok")
        count_ps = sem("count_ps")
        inv_ok = sem("inv_ok")
        inv_ps = sem("inv_ps")
        a_done = sem("a_done")

        c_x = [sem(f"c_x{i}") for i in range(4)]
        c_xt = sem("c_xt")
        c_xe = sem("c_xe")
        c_xl = sem("c_xl")
        c_g = sem("c_g")
        c_u = sem("c_u")
        c_sl = sem("c_sl")
        c_hk = sem("c_hk")
        c_ht = sem("c_ht")
        c_hea = sem("c_hea")
        c_hed = sem("c_hed")
        c_d = sem("c_d")
        c_yk = sem("c_yk")
        c_st = [sem(f"c_st{i}") for i in range(4)]
        c_pad = sem("c_pad")

        s_in = sem("s_in")
        s_hi = sem("s_hi")
        s_lo = sem("s_lo")
        xT_in = sem("xT_in")
        ob_in = sem("ob_in")
        y_in = sem("y_in")
        m_in = [sem(f"m_in{i}") for i in range(2)]
        b_r, b_v, b_qk, b_s, b_mt, b_st, b_pv, b_g, b_gu, b_ot, b_at, b_res, b_dn, b_out = (
            sem(f"b_{n}") for n in ("r", "v", "qk", "s", "mt", "st", "pv", "g", "gu", "ot", "at", "res", "dn", "out"))
        a_r, a_v, a_qk, a_exp, a_th, a_hh, a_ot, a_at, a_res = (
            sem(f"a_{n}") for n in ("r", "v", "qk", "exp", "th", "hh", "ot", "at", "res"))
        d_r, d_qk, d_max, d_mh, d_m, d_mt, d_ga, d_hf, d_inv, d_ao, d_at, d_res, d_dn, d_out = (
            sem(f"d_{n}") for n in ("r", "qk", "max", "mh", "m", "mt", "ga", "hf", "inv", "ao", "at", "res", "dn", "out"))
        p_h = sem("p_h")
        p_ys = sem("p_ys")
        p_yy = sem("p_yy")
        p_y = sem("p_y")
        o_st = sem("o_st")

        block = ctx.enter_context(nc.Block())

        s_bank, st_bank, ot_bank, g_bank, u_bank, m_bank = bank[0:2], bank[2:4], bank[4], bank[5], bank[6], bank[7]

        STEPS = 4 * TPB
        AHEAD = 5
        LAST = NB - 1
        F0 = (None, 3, None, 0)
        QK_STEP = ((0, 2, 4, 6), (0, 2, 5, 7), (6, 7, 8, 9), (0, 2, 5, 7))
        QK_BANK = ((m_bank,) * 4, (m_bank,) * 4, (m_bank, u_bank, g_bank, m_bank), (m_bank,) * 4)
        R_BANK = (m_bank, g_bank, u_bank)

        def there(b):
            return not isinstance(b, int) or 0 <= b < NB

        def after(b, g, n):
            return (b + (g + n) // NG, (g + n) % NG)

        def slots(eng, slot):
            slot(-1, 2)
            slot(-1, 3)
            for g in range(NG):
                slot(0, g)
            with eng.Fori(1, LAST) as b:
                for g in range(NG):
                    slot(b, g)
            for g in range(NG):
                slot(LAST, g)
            slot(NB, 0)

        xt_bank = [[bank[2], bank[3]], [bank[4], bank[5]]]
        lg_bank = bank[6]
        gu_bank = [[bank[0], bank[1]], [bank[2], bank[3]]]
        xg_bank, y_bank = bank[4], bank[5]
        ht_bank = [bank[6], bank[7]]

        @block.sync
        def _(sp):
            def load_x(q):
                n = NB // 4
                for j in range(n):
                    sp.dma_start(x_all[:, (q * n + j) * TPB:(q * n + j + 1) * TPB, :],
                                 x[q * n + j].rearrange("(t p) d -> p t d", p=P)).then_inc(x_in[q], 16)

            load_x(0)
            sp.dma_start(gate_raw[:, :], gate_w).then_inc(small_in, 16)
            for i, name in enumerate(PROJ):
                basis, ph, am = attn[name]
                sp.dma_start(basis_raw[i * HARM:(i + 1) * HARM, :], basis).then_inc(small_in, 16)
                sp.dma_start(phase[:, i, :, :], ph.rearrange("(a p) h -> p a h", p=P)).then_inc(small_in, 16)
                sp.dma_start(amp[:, i, :, :], am.rearrange("(a p) h -> p a h", p=P)).then_inc(small_in, 16)
            for q in range(1, 4):
                load_x(q)
            wait(sp, consts, 1)
            def load_experts(e2):
                for i in range(2):
                    e = e2 * 2 + i
                    r = raw[i]
                    wait(sp, hi_done, e2 * 2 + i - 1)
                    wait(sp, lo_done, e2 * 2 + i - 1)
                    gu = r[:, 0:W_GU].rearrange("p (k n) -> p k n", k=KT)
                    dn = r[:, W_GU:W_ALL].rearrange("p (k n) -> p k n", k=FT)
                    one = lambda w: w[bass.ds(e, 1)] if not isinstance(e, int) else w[e:e + 1]
                    sp.dma_start(gu[:, :, 0:F], one(w_gate).rearrange("a (k p) f -> p (a k) f", p=P)).then_inc(raw_in[i], 16)
                    sp.dma_start(gu[:, :, F:GU], one(w_up).rearrange("a (k p) f -> p (a k) f", p=P)).then_inc(raw_in[i], 16)
                    sp.dma_start(dn[:, 0:FT - 1, :],
                                 one(w_down)[:, 0:(FT - 1) * P, :].rearrange("a (k p) f -> p (a k) f", p=P)).then_inc(raw_in[i], 16)
                    sp.dma_start(dn[0:F_LAST, FT - 1, :],
                                 one(w_down)[:, (FT - 1) * P:F, :].rearrange("a p f -> (a p) f")).then_inc(raw_in[i], 16)

            def store_rows(b2):
                for i in range(2):
                    b = b2 * 2 + i
                    rows = xn_dram.rearrange("(b t p) c -> b p t c", t=TPB, p=P)
                    wait(sp, xn_ok, b + 1)
                    sp.dma_start(rows[b] if isinstance(b, int) else rows[bass.ds(b, 1)].rearrange("b p t c -> (b p) t c"),
                                 x_n[i][:, :, :]).then_inc(xn_stored[i], 16)
                    wait(sp, xt_hi, b + 1)
                    wait(sp, xt_lo, b + 1)
                    sp.dma_start(xT_dram[b] if isinstance(b, int) else xT_dram[bass.ds(b, 1)].rearrange("b p n -> (b p) n"),
                                 x_T[i][:, :, :, :].rearrange("p a k l -> p (a k l)").bitcast(F32)).then_inc(xT_stored[i], 16)

            load_experts(0)
            store_rows(0)
            load_experts(1)
            with sp.Fori(1, PAIRS - 1) as b2:
                store_rows(b2)
                load_experts(b2 + 1)
            store_rows(PAIRS - 1)
            sp.wait_ge(hi_done, NE)
            sp.wait_ge(lo_done, NE)
            gu = s_raw[:, 0:S_GU].rearrange("p (k n) -> p k n", k=KT)
            dn = s_raw[:, S_GU:S_ALL].rearrange("p (k n) -> p k n", k=SFT)
            sp.dma_start(gu[:, :, 0:SF], sw_gate.rearrange("(k p) f -> p k f", p=P)).then_inc(s_in, 16)
            sp.dma_start(gu[:, :, SF:2 * SF], sw_up.rearrange("(k p) f -> p k f", p=P)).then_inc(s_in, 16)
            sp.dma_start(dn[:, 0:SFT - 1, :], sw_down[0:(SFT - 1) * P, :].rearrange("(k p) f -> p k f", p=P)).then_inc(s_in, 16)
            sp.dma_start(dn[0:SF_LAST, SFT - 1, :], sw_down[(SFT - 1) * P:SF, :]).then_inc(s_in, 16)


            with sp.Fori(0, NS // 4) as s4:
                for i in range(4):
                    s = s4 * 4 + i
                    wait(sp, c_yk, s + 1)
                    sp.dma_start(y_dram.rearrange("(s p) d -> s p d", p=P)[bass.ds(s, 1)].rearrange("a p d -> (a p) d"),
                                 c_y[i][:, :]).then_inc(c_st[i], 16)
            for i in range(4):
                sp.wait_ge(c_st[i], 16 * (NS // 4))

            for i in range(2):
                sp.wait_ge(xT_stored[i], 16 * PAIRS)
            sp.wait_ge(c_yk, NS)
            sp.wait_ge(c_hed, NS)
            sp.dma_start(xT_b[:, :, :, :].rearrange("p a k l -> p (a k l)").bitcast(F32), xT_dram[0]).then_inc(xT_in, 16)

            def load_xT(b):
                wait(sp, b_gu, b * SFT)
                one = xT_dram[bass.ds(b, 1)].rearrange("b p n -> (b p) n") if not isinstance(b, int) else xT_dram[b]
                sp.dma_start(xT_b[:, :, :, :].rearrange("p a k l -> p (a k l)").bitcast(F32), one).then_inc(xT_in, 16)

            def load_x_b(b):
                wait(sp, o_st, b * 32)
                sp.dma_start(o_b[:, :, :], x[bass.ds(b, 1)].rearrange("b (t p) d -> p (b t) d", p=P)).then_inc(ob_in, 16)

            def slot(b, g):
                if g == 1 and there(b):
                    load_x_b(b)
                nb, ng = after(b, g, 1)
                if there(nb):
                    wait(sp, d_mt, nb * NG + ng + 1)
                    for n in range(4):
                        par, pair = n // 2, n % 2
                        sp.dma_start(q_rows[ng][64 * par + 48:64 * par + 50, pair, :].bitcast(F32),
                                     top_T[ng % 2][2 * n:2 * n + 2, :].bitcast(F32)).then_inc(m_in[ng % 2], 16)
                if g == 1 and there(b + 1):
                    load_xT(b + 1)
                if g == 0 and there(b - 1):
                    for h in range(2):
                        wait(sp, d_out, (b - 1) * 2 + h + 1)
                        sp.dma_start(out[bass.ds(b - 1, 1), h * 2 * P:(h + 1) * 2 * P, :].rearrange("a (t p) d -> p (a t) d", p=P),
                                     o_b[:, 2 * h:2 * h + 2, :]).then_inc(o_st, 16)

            slots(sp, slot)
            sp.wait_ge(o_st, 32 * NB)

        @block.gpsimd
        def _(pool):
            st = Steps(pool, c_pad)
            for i in range(2):
                pool.memset(raw[i][96:128, W_GU + (FT - 1) * D:W_ALL], 0.0).then_inc(c_pad, 1)
            pool.wait_ge(c_pad, 2)
            pool.memset(zeros[:, :], 0.0).then_inc(consts, 1)
            st.n = 2
            st.did(pool.memset(ident_f[:, :], 0.0))
            st.did(pool.memset(upper[:, :], 1.0))
            pool.memset(ones_b[:, :], 1.0)
            pool.iota(iota_e[:, :], [[1, NE]], base=0, channel_multiplier=0, allow_small_or_imprecise_dtypes=True)
            pool.iota(iota_s[:, :], [[1, NS]], base=0, channel_multiplier=0, allow_small_or_imprecise_dtypes=True)
            pool.iota(iota_r[:, :], [[1, P]], base=0, channel_multiplier=0, allow_small_or_imprecise_dtypes=True)
            pool.iota(token_id[:, :], [[P, NT]], base=0, channel_multiplier=1, allow_small_or_imprecise_dtypes=True)
            pool.memset(wq_rows[:, :, :].bitcast(F32), 0.0)
            st.did(pool.memset(wk_rows[:, :, :].bitcast(F32), 0.0))
            st.wait()
            st.did(pool.affine_select(out=ident_f[:, :], in_=ident_f[:, :], compare_op=ALU.not_equal, fill=1.0,
                                      base=0, pattern=[[-1, P]], channel_multiplier=1))
            st.did(pool.affine_select(out=upper[:, :], in_=upper[:, :], compare_op=ALU.is_gt, fill=0.0,
                                      base=0, pattern=[[1, P]], channel_multiplier=-1))
            st.wait()
            pool.memset(zeros[:, :], 0.0).then_inc(consts, 1)
            def low_parts(e2):
                for i in range(2):
                    e = e2 * 2 + i
                    wait(pool, hi_done, e + 1)
                    pool.tensor_tensor(w_exp[:, bass.ds(e, 1), LO, :].rearrange("p a n -> p (a n)"), raw[i][:, :],
                                       w_exp[:, bass.ds(e, 1), HI, :].rearrange("p a n -> p (a n)").bitcast(F32),
                                       ALU.subtract).then_inc(lo_done, 1)

            with pool.Fori(0, NE // 2 - 1) as e2:
                low_parts(e2)
            pool.wait_ge(a_done, 1)
            for i in range(2):
                pool.wait_ge(xn_stored[i], 16 * PAIRS)

            def gather(s):
                wait(pool, c_xt, s - 3)
                pool.indirect_dma_start(xg[s % 4][:, :], None, xn_dram,
                                        bass.IndirectOffsetOnAxis(token_of[:, s:s + 1], 0)).then_inc(c_x[s % 4], 16)

            for s in range(4):
                gather(s)
            low_parts(NE // 2 - 1)
            for s in range(4, NS):
                gather(s)

            for i in range(4):
                pool.wait_ge(c_st[i], 16 * (NS // 4))
            pool.wait_ge(s_hi, 1)
            pool.tensor_tensor(w_sh[:, LO, :], s_raw[:, :], w_sh[:, HI, :].bitcast(F32), ALU.subtract).then_inc(s_lo, 1)
            pool.wait_ge(s_lo, 1)

            def hidden_low(b, f):
                m = P if f < SFT - 1 else SF_LAST
                n = b * SFT + f
                wait(pool, a_hh, n + 1)
                wait(pool, b_dn, b * TPB)
                pool.tensor_tensor(h_T[0:m, LO, f, :], h_f[f % 2][0:m, :], h_T[0:m, HI, f, :].bitcast(F32),
                                   ALU.subtract).then_inc(p_h, 1)

            for b in range(NB):
                for f in range(3):
                    hidden_low(b, f)
                wait(pool, p_y, b)
                for t in range(TPB):
                    for k in range(2):
                        pool.indirect_dma_start(y_b[:, t, k, :], None, y_dram,
                                                bass.IndirectOffsetOnAxis(slot_of[:, k, b * TPB + t:b * TPB + t + 1], 0)).then_inc(y_in, 16)
                wait(pool, y_in, (b + 1) * TPB * 32)
                for t in range(TPB):
                    for k in range(2):
                        pool.tensor_scalar(y_b[:, t, k, :], y_b[:, t, k, :], share[:, b * TPB + t, k:k + 1], None, ALU.mult).then_inc(p_ys, 1)
                wait(pool, p_ys, (b + 1) * TPB * 2)
                pool.tensor_tensor(y_b[:, :, 0, :], y_b[:, :, 0, :], y_b[:, :, 1, :], ALU.add).then_inc(p_yy, 1)
                hidden_low(b, 3)
                hidden_low(b, 4)
                wait(pool, p_yy, b + 1)
                wait(pool, ob_in, (b + 1) * 16)
                pool.tensor_tensor(o_b[:, :, :], o_b[:, :, :], y_b[:, :, 0, :], ALU.add).then_inc(p_y, 1)
                hidden_low(b, 5)

        @block.scalar
        def _(act):
            st = Steps(act, act_a)
            wait(act, dve_a, A_ANGLE)
            act.activation(angle[:, :], angle[:, :], ACT.Sin).then_inc(sin_done, 1)
            wait(act, stats_ok, 1)
            act.activation(rs[:, 1, :], rs[:, 0, :], ACT.Sqrt).then_inc(root_ok, 1)

            def high_parts(e2):
                for i in range(2):
                    e = e2 * 2 + i
                    wait(act, raw_in[i], (e2 + 1) * 64)
                    act.activation(w_exp[:, bass.ds(e, 1), HI, :].rearrange("p a n -> p (a n)"), raw[i][:, :],
                                   ACT.Copy).then_inc(hi_done, 1)

            def pair(b2, experts=True):
                for i in range(2):
                    b = b2 * 2 + i
                    wait(act, xt_ps, b + 1)
                    wait(act, lg_ps, b - 1)
                    wait(act, xT_stored[i], b2 * 16)
                    for k in range(KT):
                        ins = act.activation(x_T[i][:, HI, k, :], xt_bank[i][k][:, :], ACT.Copy)
                    ins.then_inc(xt_hi, 1)
                if experts:
                    high_parts(b2)

            act.wait_ge(prep_done, 1)
            pair(0)
            with act.Fori(1, PAIRS - 1) as b2:
                pair(b2)
            pair(PAIRS - 1, experts=False)
            act.wait_ge(lg_max, 1)
            act.activation(pr[:, :, :], lg[:, :, :], ACT.Exp).then_inc(lg_exp, 1)

            def x_out(s, i):
                wait(act, c_xt, s + 1)
                wait(act, c_u, s - 1)
                act.activation(xg_T[i % 2][:, 0:KT, :].rearrange("p a t -> p (a t)"), xg_bank[:, 0:D], ACT.Copy).then_inc(c_xe, 1)

            def silu(s, i):
                wait(act, c_g, s + 1)
                wait(act, c_hk, s - 1)
                act.activation(c_sil[i % 2][:, :], gu_bank[i % 2][0][:, 0:F], ACT.Silu).then_inc(c_sl, 1)

            def h_out(s, i):
                wait(act, c_ht, s + 1)
                wait(act, c_d, s - 1)
                act.activation(c_hT[i % 2][:, HI, :, :].rearrange("p a t -> p (a t)"), ht_bank[i % 2][:, 0:FT * P], ACT.Copy).then_inc(c_hea, 1)

            def y_out(s, i):
                wait(act, c_d, s + 1)
                wait(act, c_st[i], (s // 4) * 16 if isinstance(s, int) else (s - i) * 4)
                act.activation(c_y[i][:, :], y_bank[:, 0:D], ACT.Copy).then_inc(c_yk, 1)

            def step(s, i, first=False, last=False):
                silu(s, i)
                if not (first and i < 1):
                    h_out(s - 1, (i - 1) % 4)
                if not (last and i == 3):
                    x_out(s + 1, (i + 1) % 4)
                if not (first and i < 2):
                    y_out(s - 2, (i - 2) % 4)

            act.wait_ge(a_done, 1)
            high_parts(NE // 2 - 1)
            x_out(0, 0)
            for i in range(4):
                step(i, i, first=True)
            with act.Fori(1, NS // 4 - 1) as s4:
                for i in range(4):
                    step(s4 * 4 + i, i)
            for i in range(4):
                step(NS - 4 + i, i, last=True)
            h_out(NS - 1, 3)
            y_out(NS - 2, 2)
            y_out(NS - 1, 3)

            def qk_high(b, g, n, gs):
                wait(act, b_qk, (b * NG + g) * 4 + n + 1)
                wait(act, d_qk, (b * NG + g) * 4 + n - 1)
                act.activation(qk_hi[n % 2][:, :], QK_BANK[gs][n][:, :], ACT.Copy).then_inc(a_qk, 1)

            def tanh(b, f):
                wait(act, b_g, b * SFT + f + 1)
                wait(act, p_h, b * SFT + f - 1)
                m = P if f < SFT - 1 else SF_LAST
                act.activation(h_f[f % 2][0:m, :], g_bank[0:m, :], ACT.Tanh, scale=0.5).then_inc(a_th, 1)

            def hidden_high(b, f):
                wait(act, d_hf, b * SFT + f + 1)
                wait(act, b_dn, b * TPB)
                m = P if f < SFT - 1 else SF_LAST
                act.activation(h_T[0:m, HI, f, :], h_f[f % 2][0:m, :], ACT.Copy).then_inc(a_hh, 1)

            def values_out(b, half):
                wait(act, b_v, b * 2 + half + 1)
                wait(act, b_pv, (b - 1) * 16 + (half + 1) * 8)
                act.activation(v_ones[:, :, half * 8:half * 8 + 8, 0:HD],
                               (u_bank, m_bank)[half][:, :].rearrange("p (t h d) -> p t h d", t=TPB, h=HEADS // 2), ACT.Copy).then_inc(a_v, 1)

            def low_rank_high(b, n):
                wait(act, b_r, b * 3 + n + 1)
                act.activation(r_rows[n][0:96, :], R_BANK[n][0:96, :], ACT.Copy).then_inc(a_r, 1)

            def exponent(b, g, s):
                kt, j = s // 4, s % 4
                if j == 0:
                    wait(act, b_pv, b * 16 + g * 4 + kt - 1)
                wait(act, b_st, b * 64 + g * 16 + s + 1)
                act.activation(prob[kt % 2][:, j, :], st_bank[s % 2][:, :], ACT.Exp, scale=HD ** -0.5).then_inc(a_exp, 1)

            def o_out(b, g):
                wait(act, b_pv, b * 16 + g * 4 + 4)
                wait(act, b_ot, b * TPB)
                act.activation(o_T[:, g, :], ot_bank[:, :], ACT.Copy).then_inc(a_ot, 1)

            def slot(b, g):
                now, (pb, pg), (qb, qg) = there(b), after(b, g, -1), after(b, g, 2)
                for s in range(STEPS):
                    if s == 2 and there(pb):
                        o_out(pb, pg)
                    if now:
                        exponent(b, g, s)
                    for n in range(4):
                        if s == QK_STEP[g][n] and there(qb):
                            qk_high(qb, qg, n, g)
                    if g == 0 and there(b - 1):
                        if s in (5, 7, 9, 11):
                            t = s // 2 - 2
                            wait(act, b_at, (b - 1) * TPB + t + 1)
                            act.activation(ao_T[:, HI, :, t * P:(t + 1) * P],
                                           u_bank[:, t % 2 * D:(t % 2 + 1) * D].rearrange("p (k t) -> p k t", k=KT), ACT.Copy).then_inc(a_at, 1)
                        if s == 13:
                            wait(act, b_res, b)
                            act.activation(ro[:, :], g_bank[0:96, :], ACT.Copy).then_inc(a_res, 1)
                    if g == 0 and s == 8 and there(b):
                        values_out(b, 1)
                    if F0[g] is not None and s in (2, 5, 7, 10, 12, 15):
                        fb = b + (g == 3)
                        if there(fb):
                            if s % 5:
                                tanh(fb, F0[g] + s // 5)
                            else:
                                hidden_high(fb, F0[g] + s // 5 - 1)
                    if g == 2 and there(b + 1):
                        if s in (3, 5, 11):
                            low_rank_high(b + 1, (3, 5, 11).index(s))
                        if s == 14:
                            values_out(b + 1, 0)
                if not there(b) and g == 2:
                    act.wait_ge(s_in, 64)
                    act.activation(w_sh[:, HI, :], s_raw[:, :], ACT.Copy).then_inc(s_hi, 1)

            slots(act, slot)

        @block.tensor
        def _(pe):
            pe.wait_ge(consts, 2)
            pe.wait_ge(small_in, 16 * 13)
            for k in range(KT):
                pe.matmul(bank[0][:, k * P:(k + 1) * P], basis_raw[:, k * P:(k + 1) * P], ident_f[:, :], start=True, stop=True)
                ins = pe.matmul(bank[0][:, 256 + k * NE:256 + (k + 1) * NE], gate_raw[:, k * P:(k + 1) * P], ident_f[0:NE, 0:NE],
                                start=True, stop=True)
            ins.then_inc(pe_prep, 1)
            wait(pe, dve_a, A_THRICE)
            for i in range(len(PROJ)):
                for k in range(KT):
                    ins = pe.matmul(bank[(1, 7)[i // 2]][0:96, (i % 2) * D + k * P:(i % 2) * D + (k + 1) * P],
                                    w_thrice[:, i * KT + k, :, :].rearrange("p r h -> p (r h)"), ident_f[:, :], start=True, stop=True)
            ins.then_inc(pe_prep, 1)

            def turn_rows(b, i):
                wait(pe, xn_ok, b + 1)
                wait(pe, xt_lo, b - 1)
                for k in range(KT):
                    for t in range(TPB):
                        ins = pe.transpose(xt_bank[i][k][:, t * P:(t + 1) * P], x_n[i][:, t, k * P:(k + 1) * P], ident_f[:, :])
                ins.then_inc(xt_ps, 1)

            def logits(b, i):
                wait(pe, xt_lo, b + 1)
                for t in range(TPB):
                    at = (b * TPB + t) * 2 * NE
                    o = lg_bank[:, at:at + 2 * NE] if isinstance(b, int) else lg_bank[:, bass.ds(at, 2 * NE)]
                    for a in (HI, LO):
                        for k in range(KT):
                            ins = pe.matmul(o, x_T[i][:, a, k, t * P:(t + 1) * P], gate_T[:, k, :, :].rearrange("p c e -> p (c e)"),
                                            start=(a == HI and k == 0), stop=(a == LO and k == KT - 1))
                ins.then_inc(lg_ps, 1)

            turn_rows(0, 0)
            pe.wait_ge(prep_done, 1)
            turn_rows(1, 1)
            logits(0, 0)
            with pe.Fori(1, PAIRS) as b2:
                for i in range(2):
                    turn_rows(b2 * 2 + i, i)
                    logits(b2 * 2 + i - 1, 1 - i)
            logits(NB - 1, 1)
            pe.wait_ge(hot_ok, 1)
            hb = hot_b[:, :, :].rearrange("p t e -> p (t e)")
            pe.matmul(bank[0][:, 0:NT * NE], upper[:, :], hb, start=True, stop=True)
            pe.matmul(bank[1][:, 0:NT * NE], ones_b[:, :], hb, start=True, stop=True).then_inc(count_ps, 1)

            def invert(t2, first=False, last=False):
                for n in range(4):
                    wait(pe, inv_ok, t2 * 4 + n + 1)
                    pe.matmul(bank[2][:, 0:NS], at_row[n][:, :], at_tile[n][:, :], start=first and n == 0,
                              stop=last and n == 3).then_inc(inv_ps, 1)

            invert(0, first=True)
            with pe.Fori(1, NT // 2 - 1) as t2:
                invert(t2)
            invert(NT // 2 - 1, last=True)

            def turn_x(s, i):
                wait(pe, c_x[i], (s // 4 + 1) * 16 if isinstance(s, int) else (s - i) * 4 + 16)
                wait(pe, c_xl, s)
                for n in range(KT):
                    ins = pe.transpose(xg_bank[:, n * P:(n + 1) * P], xg[i][:, n * P:(n + 1) * P], ident_f[:, :])
                ins.then_inc(c_xt, 1)

            def gate_up(s, i):
                e = pe.value_load(expert_of[0:1, s:s + 1] if isinstance(s, int) else expert_of[0:1, bass.ds(s, 1)],
                                  min_val=0, max_val=NE - 1)
                wait(pe, c_xl, s + 1)
                for n, (free, done) in enumerate(((c_sl, c_g), (c_hk, c_u))):
                    wait(pe, free, s - 1)
                    for m, (a, c) in enumerate(PRODUCTS):
                        for k in range(KT):
                            w = w_exp[:, bass.ds(e, 1), c, k * GU + n * F:k * GU + (n + 1) * F].rearrange("p a n -> p (a n)")
                            ins = pe.matmul(gu_bank[i % 2][n][:, 0:F], xg_T[i % 2][:, a * KT + k, :], w,
                                            start=(m == 0 and k == 0), stop=(m == 2 and k == KT - 1))
                    ins.then_inc(done, 1)

            def turn_h(s, i):
                wait(pe, c_hk, s + 1)
                wait(pe, c_hed, s - 1)
                for k in range(FT):
                    ins = pe.transpose(ht_bank[i % 2][:, k * P:(k + 1) * P], c_h[i % 2][:, k * P:(k + 1) * P], ident_f[:, :])
                ins.then_inc(c_ht, 1)

            def down(s, i):
                e = pe.value_load(expert_of[0:1, s:s + 1] if isinstance(s, int) else expert_of[0:1, bass.ds(s, 1)],
                                  min_val=0, max_val=NE - 1)
                wait(pe, c_hed, s + 1)
                wait(pe, c_yk, s)
                for m, (a, c) in enumerate(PRODUCTS):
                    for k in range(FT):
                        n = P if k < FT - 1 else F_LAST
                        w = w_exp[0:n, bass.ds(e, 1), c, W_GU + k * D:W_GU + (k + 1) * D].rearrange("p a n -> p (a n)")
                        ins = pe.matmul(y_bank[:, 0:D], c_hT[i % 2][0:n, a, k, :], w,
                                        start=(m == 0 and k == 0), stop=(m == 2 and k == FT - 1))
                ins.then_inc(c_d, 1)

            def step(s, i, first=False, last=False):
                gate_up(s, i)
                if not (first and i < 1):
                    turn_h(s - 1, (i - 1) % 4)
                if not (last and i == 3):
                    turn_x(s + 1, (i + 1) % 4)
                if not (first and i < 2):
                    down(s - 2, (i - 2) % 4)

            pe.wait_ge(a_done, 1)
            pe.wait_ge(hi_done, NE - 2)
            pe.wait_ge(lo_done, NE - 2)
            turn_x(0, 0)
            for i in range(4):
                step(i, i, first=True)
            pe.wait_ge(hi_done, NE)
            pe.wait_ge(lo_done, NE)
            with pe.Fori(1, NS // 4 - 1) as s4:
                for i in range(4):
                    step(s4 * 4 + i, i)
            for i in range(4):
                step(NS - 4 + i, i, last=True)
            turn_h(NS - 1, 3)
            down(NS - 2, 2)
            down(NS - 1, 3)

            pe.wait_ge(c_yk, NS)
            pe.wait_ge(c_hed, NS)

            def project(b, g, n, gs):
                rows, w, k = (r_rows[0], wq_rows, 96) if n < 2 else (r_rows[1], wk_rows, 97)
                pair = 2 * g + n % 2
                if gs == 2:
                    if n == 1:
                        wait(pe, d_dn, (b - 1) * TPB + 2)
                    elif n == 3:
                        wait(pe, d_qk, (b * NG + g) * 4 + 1)
                    else:
                        wait(pe, d_r, b * 3 + n // 2 + 1)
                elif n == 0:
                    wait(pe, d_mt, b * NG + g - 1)
                else:
                    wait(pe, d_qk, (b * NG + g) * 4 + n)
                pe.matmul(QK_BANK[gs][n][:, :], w[0:k, 2 * pair:2 * pair + 2, :].rearrange("p h j -> p (h j)"), rows[0:k, :],
                          start=True, stop=True).then_inc(b_qk, 1)

            def score(b, g, u):
                j, qt = u // 4, u % 4
                r = 64 * (j % 2)
                if u == 0:
                    wait(pe, d_qk, (b * NG + g) * 4 + 4)
                wait(pe, d_max, b * 64 + g * 16 + u - 1)
                pe.matmul(s_bank[u % 2][:, :], q_rows[g][r:r + 48, j // 2, qt * P:(qt + 1) * P], k_rows[g][r:r + 48, j // 2, :],
                          start=True, stop=True).then_inc(b_s, 1)

            def turn_max(b, g):
                wait(pe, d_m, b * NG + g + 1)
                if g == 1:
                    wait(pe, a_v, b * 2 + 2)
                for qt in range(TPB):
                    ins = pe.transpose(m_bank[0:8, qt * P:(qt + 1) * P],
                                       top_parts[g % 2][:, qt, :, :, :].rearrange("p a b c -> p (a b c)").bitcast(F32), ident_f[:, :])
                ins.then_inc(b_mt, 1)

            def gate_up_shared(b, f, quarter):
                m = P if f < SFT - 1 else SF_LAST
                if quarter == 0:
                    if f == 0:
                        wait(pe, d_dn, b * TPB)
                        wait(pe, a_v, b * 2 + 1)
                    elif f == 3:
                        wait(pe, d_out, b * 2)
                        wait(pe, d_hf, b * SFT + f)
                    else:
                        wait(pe, d_hf, b * SFT + f)
                n = quarter // 2
                for i in range(3 * (quarter % 2), 3 * (quarter % 2) + 3):
                    (a, c), k = PRODUCTS[i // 2], i % 2
                    o = k * 2 * SF + n * SF + f * P
                    ins = pe.matmul((g_bank, u_bank)[n][0:m, :], w_sh[:, a, o:o + m], xT_b[:, c, k, :], start=(i == 0), stop=(i == 5))
                if quarter == 1:
                    ins.then_inc(b_g, 1)
                if quarter == 3:
                    ins.then_inc(b_gu, 1)

            def score_T(b, g, s):
                kt, j = s // 4, s % 4
                r = 64 * (j % 2)
                if s == 0:
                    wait(pe, m_in[g % 2], b * 128 + 64 * (g // 2 + 1))
                wait(pe, a_exp, b * 64 + g * 16 + s - 1)
                pe.matmul(st_bank[s % 2][:, :], k_rows[g][r:r + QKV_ROWS, j // 2, kt * P:(kt + 1) * P],
                          q_rows[g][r:r + QKV_ROWS, j // 2, :], start=True, stop=True).then_inc(b_st, 1)

            def values(b, g, kt):
                wait(pe, a_exp, b * 64 + g * 16 + kt * 4 + 4)
                if kt == 0:
                    wait(pe, a_ot, b * NG + g)
                    if g % 2 == 0:
                        wait(pe, a_v, b * 2 + g // 2 + 1)
                for j in range(4):
                    ins = pe.matmul(ot_bank[32 * j:32 * j + 32, :], v_ones[:, kt, 4 * g + j, :], prob[kt % 2][:, j, :],
                                    start=(kt == 0), stop=(kt == TPB - 1))
                ins.then_inc(b_pv, 1)

            def low_rank(b, n, half):
                if half == 0:
                    if n == 0:
                        wait(pe, xT_in, (b + 1) * 16)
                        wait(pe, d_mt, (b - 1) * NG + 3)
                    elif n == 1:
                        wait(pe, d_dn, (b - 1) * TPB + 1)
                    else:
                        wait(pe, d_qk, b * NG * 4 + 2)
                for i in range(3 * half, 3 * half + 3):
                    (a, c), k = PRODUCTS[i // 2], i % 2
                    ins = pe.matmul(R_BANK[n][0:96, :], basis_T[:, k, a, n, :, :].rearrange("p r h -> p (r h)"), xT_b[:, c, k, :],
                                    start=(i == 0), stop=(i == 5))
                if half:
                    ins.then_inc(b_r, 1)

            def project_values(b, half):
                if half == 0:
                    wait(pe, d_r, b * 3 + 3)
                else:
                    wait(pe, d_qk, b * 16 + 12)
                for t in range(TPB):
                    ins = pe.matmul((u_bank, m_bank)[half][:, t * P:(t + 1) * P], r_rows[2][0:96, t * P:(t + 1) * P],
                                    wv_rows[:, half * P:(half + 1) * P], start=True, stop=True)
                ins.then_inc(b_v, 1)

            def down_shared(b, t, half):
                dst = (g_bank, u_bank, g_bank, g_bank)[t][:, 0:D]
                if half == 0:
                    if t == 0:
                        wait(pe, d_hf, b * SFT + SFT)
                    if t == 2:
                        wait(pe, d_qk, (b + 1) * NG * 4 + 3) if there(b + 1) else wait(pe, d_dn, b * TPB + 1)
                    if t == 3:
                        wait(pe, d_dn, b * TPB + 3)
                if half == 0 and t == 0:
                    wait(pe, p_h, b * SFT + SFT - 1)
                if half == 1 and t == 0:
                    wait(pe, p_h, b * SFT + SFT)
                for i in range(9 * half, 9 * half + 9):
                    f, (a, c) = i // 3, PRODUCTS[i % 3]
                    m = P if f < SFT - 1 else SF_LAST
                    ins = pe.matmul(dst, h_T[0:m, a, f, t * P:(t + 1) * P], w_sh[0:m, c, S_GU + f * D:S_GU + (f + 1) * D],
                                    start=(i == 0), stop=(i == 17))
                if half:
                    ins.then_inc(b_dn, 1)

            def turn_o(b, t):
                if t == 0:
                    wait(pe, a_ot, b * NG + NG)
                    if there(b + 1):
                        wait(pe, d_hf, (b + 1) * SFT + 3)
                    else:
                        wait(pe, d_dn, b * TPB + TPB)
                wait(pe, d_ao, b * TPB + t)
                for g in range(NG):
                    ins = pe.transpose(g_bank[:, g * P:(g + 1) * P], o_T[:, g, t * P:(t + 1) * P], ident_f[:, :])
                ins.then_inc(b_ot, 1)

            def turn_back(b, t):
                wait(pe, d_ao, b * TPB + t + 1)
                wait(pe, d_at, b * TPB + t)
                for k in range(KT):
                    ins = pe.transpose(u_bank[:, t % 2 * D + k * P:t % 2 * D + (k + 1) * P], ao[t % 2][:, k * P:(k + 1) * P], ident_f[:, :])
                ins.then_inc(b_at, 1)

            def low_rank_o(b):
                wait(pe, d_at, b * TPB + TPB)
                for i in range(6):
                    (a, c), k = PRODUCTS[i // 2], i % 2
                    ins = pe.matmul(g_bank[0:96, :], basis_T[:, k, a, 3, :, :].rearrange("p r h -> p (r h)"), ao_T[:, c, k, :],
                                    start=(i == 0), stop=(i == 5))
                ins.then_inc(b_res, 1)

            def project_o(b, half):
                wait(pe, d_res, b + 1)
                for t in range(2):
                    q = 2 * half + t
                    ins = pe.matmul((u_bank, g_bank)[half][:, t * D:(t + 1) * D], ro[:, q * P:(q + 1) * P], wo_rows[:, :], start=True, stop=True)
                ins.then_inc(b_out, 1)

            def slot(b, g):
                now, (pb, pg), (nb, ng), (qb, qg) = there(b), after(b, g, -1), after(b, g, 1), after(b, g, 2)
                if not there(b) and g == 3:
                    pe.wait_ge(s_lo, 1)
                for s in range(STEPS):
                    if now:
                        score_T(b, g, s)
                    if s < STEPS - AHEAD:
                        if there(nb):
                            score(nb, ng, s + AHEAD)
                    elif there(qb):
                        score(qb, qg, s - STEPS + AHEAD)
                    if s == 1 and there(pb):
                        values(pb, pg, TPB - 1)
                    if s in (5, 9, 13) and now:
                        values(b, g, s // 4 - 1)
                    for n in range(4):
                        if s == QK_STEP[g][n] and there(qb):
                            project(qb, qg, n, g)
                    if g == 0 and there(b - 1):
                        if s in (3, 5, 7, 9):
                            turn_o(b - 1, s // 2 - 1)
                        if s in (5, 7, 9, 11):
                            turn_back(b - 1, s // 2 - 2)
                        if s == 13:
                            low_rank_o(b - 1)
                        if s == 15:
                            project_o(b - 1, 0)
                            project_o(b - 1, 1)
                    if g == 0 and s == 8 and now:
                        project_values(b, 1)
                    if F0[g] is not None and there(b + (g == 3)) and s % 5:
                        gate_up_shared(b + (g == 3), F0[g] + s // 5, s % 5 - 1)
                    if g == 2 and now:
                        for t, at in enumerate((1, 3, 10, 13)):
                            if s in (at, at + 1):
                                down_shared(b, t, s - at)
                    if g == 2 and there(b + 1):
                        for n, at in enumerate((2, 4, 10)):
                            if s in (at, at + 1):
                                low_rank(b + 1, n, s - at)
                        if s == 14:
                            project_values(b + 1, 0)
                    if s == STEPS - AHEAD and there(nb):
                        turn_max(nb, ng)

            slots(pe, slot)

        @block.vector
        def _(dve):
            st = Steps(dve, dve_a)
            dve.wait_ge(small_in, 16 * 13)
            ph = phase[:, :, :, :].rearrange("p i k h -> p (i k h)")
            am = amp[:, :, :, :].rearrange("p i k h -> p (i k h)")
            st.then(dve.tensor_scalar(turns[:, :], ph, 1 / (2 * math.pi), 0.25, ALU.mult, ALU.add))
            st.then(dve.tensor_scalar(turns[:, :], turns[:, :], ROUNDER, ROUNDER, ALU.add, ALU.subtract))
            st.then(dve.scalar_tensor_tensor(angle[:, :], turns[:, :], -TURN_1, ph, ALU.mult, ALU.add))
            st.then(dve.scalar_tensor_tensor(angle[:, :], turns[:, :], -TURN_2, angle[:, :], ALU.mult, ALU.add))
            st.then(dve.scalar_tensor_tensor(angle[:, :], turns[:, :], -TURN_3, angle[:, :], ALU.mult, ALU.add))
            st.then(dve.tensor_scalar(angle[:, :], angle[:, :], math.pi / 2, PI_BELOW, ALU.add, ALU.min))
            st.then(dve.tensor_scalar(angle[:, :], angle[:, :], -PI_BELOW, None, ALU.max))
            assert st.n == A_ANGLE
            st.did(dve.memset(q_minus[:, :], 0.0))
            st.then(dve.memset(k_minus[:, :], 0.0))
            for h in range(2):
                st.did(dve.memset(q_minus[64 * h + 32:64 * h + 48, :], -1.0))
                st.did(dve.memset(k_minus[64 * h:64 * h + 32, :], -1.0))
            st.wait()
            for h in range(2):
                st.did(dve.memset(k_minus[64 * h:64 * h + 16, :], 0.0))
            dve.wait_ge(consts, 2)
            st.did(dve.memset(wk_rows[96:97, :, 48:50].bitcast(F32), -1.0))
            dve.wait_ge(pe_prep, 1)
            for k in range(KT):
                b = bank[0][:, k * P:(k + 1) * P].rearrange("p (i r h) -> p i r h", i=len(PROJ), r=1)
                b = b.to_broadcast([P, len(PROJ), 3, HARM])
                g = bank[0][:, 256 + k * NE:256 + (k + 1) * NE]
                st.did(dve.tensor_copy(basis_T[:, k, HI, :, :, :], b))
                st.then(dve.tensor_copy(gate_T[:, k, HI, :], g))
                st.did(dve.tensor_tensor(basis_T[:, k, LO, :, :, :], b, basis_T[:, k, HI, :, :, :].bitcast(F32), ALU.subtract))
                st.did(dve.tensor_tensor(gate_T[:, k, LO, :], g, gate_T[:, k, HI, :].bitcast(F32), ALU.subtract))
            dve.wait_ge(sin_done, 1)
            sn = angle[:, :].rearrange("p (i r h) -> p i r h", r=1, h=HARM).to_broadcast([P, len(PROJ) * KT, 3, HARM])
            ab = am.rearrange("p (i r h) -> p i r h", r=1, h=HARM).to_broadcast([P, len(PROJ) * KT, 3, HARM])
            st.then(dve.tensor_tensor(w_thrice[:, :, :, :], sn, ab, ALU.mult))
            assert st.n == A_THRICE
            for q in range(4):
                dve.wait_ge(x_in[q], 16 * (NB // 4))
                for n in range(q * NT // 4, (q + 1) * NT // 4):
                    ins = dve.bn_stats(stats[:, n, :], x_all[:, n, :])
                st.did(ins)
            dve.wait_ge(pe_prep, 2)
            dve.wait_ge(consts, 2)
            for i in range(len(PROJ)):
                st.did(dve.tensor_copy(w_hi[:, i, :], bank[(1, 7)[i // 2]][0:96, (i % 2) * D:(i % 2 + 1) * D]))
            st.wait()
            for i in range(len(PROJ)):
                src = bank[(1, 7)[i // 2]][0:96, (i % 2) * D:(i % 2 + 1) * D]
                st.did(dve.tensor_tensor(w_hi[32:64, i, :], src[32:64, :], w_hi[32:64, i, :].bitcast(F32), ALU.subtract))
            st.wait()
            for i, dst in enumerate((wq_rows, wk_rows)):
                v = w_hi[:, i, :].rearrange("p (h r j) -> p h r j", h=HEADS, r=1).to_broadcast([96, HEADS, 3, HD]).bitcast(F32)
                st.did(dve.tensor_copy(dst[0:96, :, 0:48].rearrange("p h (r j) -> p h r j", r=3), v))
            st.did(dve.tensor_copy(wv_rows[:, :], w_hi[:, 2, :].bitcast(F32)))
            st.did(dve.tensor_copy(wo_rows[:, :], w_hi[:, 3, :].bitcast(F32)))
            for n in range(NT):
                ins = dve.bn_aggr(mean_var[:, n, :], stats[:, n, :])
            st.then(ins)
            dve.tensor_scalar(rs[:, 0, :], mean_var[:, :, 1], LN_EPS, None, ALU.add).then_inc(stats_ok, 1)
            dve.wait_ge(root_ok, 1)
            st.then(dve.reciprocal(rs[:, 2, :], rs[:, 1, :]))
            st.then(dve.tensor_tensor(rs[:, 3, :], rs[:, 2, :], rs[:, 2, :], ALU.mult))
            st.then(dve.tensor_tensor(rs[:, 3, :], rs[:, 3, :], rs[:, 0, :], ALU.mult))
            st.then(dve.tensor_scalar(rs[:, 3, :], rs[:, 3, :], -0.5, 1.5, ALU.mult, ALU.add))
            st.then(dve.tensor_tensor(rs[:, 3, :], rs[:, 2, :], rs[:, 3, :], ALU.mult))
            dve.memset(rs[:, 1, :], 0.0).then_inc(prep_done, 1)

            def normal(b2, i):
                b = b2 * 2 + i
                wait(dve, xt_ps, b - 1)
                wait(dve, xn_stored[i], b2 * 16)
                for t in range(TPB):
                    n = b * TPB + t
                    at = slice(n, n + 1) if isinstance(n, int) else bass.ds(n, 1)
                    ins = dve.tensor_scalar(x_n[i][:, t, :], x_all[:, at, :].rearrange("p a d -> p (a d)"),
                                            mean_var[:, at, 0:1].rearrange("p a c -> p (a c)"), rs[:, 3, at], ALU.subtract, ALU.mult)
                ins.then_inc(xn_ok, 1)

            def pair(b2, last=False):
                for i in range(2):
                    b = b2 * 2 + i
                    if not (last and i):
                        normal(b2 + i, 1 - i)
                    wait(dve, xt_hi, b + 1)
                    for k in range(KT):
                        ins = dve.tensor_tensor(x_T[i][:, LO, k, :], xt_bank[i][k][:, :], x_T[i][:, HI, k, :].bitcast(F32), ALU.subtract)
                    ins.then_inc(xt_lo, 1)

            normal(0, 0)
            pair(0)
            with dve.Fori(1, PAIRS - 1) as b2:
                pair(b2)
            pair(PAIRS - 1, last=True)

            def over_e(v):
                return v.rearrange("p (t r) -> p t r", r=1).to_broadcast([P, NT, NE])

            def over_t(v):
                return v.rearrange("p (r e) -> p r e", r=1).to_broadcast([P, NT, NE])

            dve.wait_ge(lg_ps, NB)
            dve.wait_ge(xT_stored[1], 16 * PAIRS)
            parts = lg_bank[:, :].rearrange("p (t c e) -> p t c e", c=2, e=NE)
            st.then(dve.tensor_copy(pr[:, :, :], parts[:, :, LO, :]))
            st.then(dve.tensor_tensor(lg[:, :, :], parts[:, :, HI, :], pr[:, :, :], ALU.add))
            st.then(dve.tensor_reduce(row[:, 0, :], lg[:, :, :], AX_X, ALU.max))
            dve.tensor_tensor(lg[:, :, :], lg[:, :, :], over_e(row[:, 0, :]), ALU.subtract).then_inc(lg_max, 1)
            dve.wait_ge(lg_exp, 1)
            st.then(dve.tensor_reduce(row[:, 1, :], pr[:, :, :], AX_X, ALU.add))
            st.then(dve.reciprocal(row[:, 2, :], row[:, 1, :]))
            st.then(dve.tensor_tensor(pr[:, :, :], pr[:, :, :], over_e(row[:, 2, :]), ALU.mult))
            for n in range(NT):
                ins = dve.max(best[:, n, :], pr[:, n, :])
            st.then(ins)
            for n in range(NT):
                ins = dve.max_index(best_at[:, n, :], best[:, n, :], pr[:, n, :])
            st.did(ins)
            st.then(dve.tensor_tensor(row[:, 3, :], best[:, :, 0], best[:, :, 1], ALU.add))
            st.then(dve.tensor_scalar(row[:, 3, :], row[:, 3, :], TOPK_EPS, None, ALU.add))
            st.then(dve.reciprocal(row[:, 0, :], row[:, 3, :]))
            for k in range(2):
                st.did(dve.scalar_tensor_tensor(share[:, :, k], best[:, :, k], ROUTE_SCALE, row[:, 0, :], ALU.mult, ALU.mult))
                st.did(dve.tensor_copy(best_atf[:, k, :], best_at[:, :, k]))
            st.wait()
            for k in range(2):
                st.did(dve.tensor_tensor(hot[k][:, :, :], over_e(best_atf[:, k, :]), over_t(iota_e[:, :]), ALU.is_equal))
            st.wait()
            st.did(dve.tensor_tensor(hot_b[:, :, :], hot[0][:, :, :], hot[1][:, :, :], ALU.add))
            st.wait()
            dve.memset(row[:, 1, :], 0.0).then_inc(hot_ok, 1)
            dve.wait_ge(count_ps, 1)
            st.then(dve.tensor_copy(totals[:, :, :], bank[1][:, 0:NT * NE].rearrange("p (t e) -> p e t", e=NE)))
            for e in range(NE):
                st.did(dve.tensor_tensor_scan(before[:, e, :], totals[:, e, :], zeros[:, :], 0.0, ALU.add, ALU.add))
            st.wait()
            st.then(dve.tensor_scalar(tiles[:, 0, :], before[:, :, NT - 1], 1 / P, (P - 1) / P - 0.5 + 1 / 512, ALU.mult, ALU.add))
            st.then(dve.tensor_scalar(tiles[:, 0, :], tiles[:, 0, :], ROUNDER, ROUNDER, ALU.add, ALU.subtract))
            st.then(dve.tensor_scalar(tiles[:, 1, :], tiles[:, 0, :], 1.0, None, ALU.max))
            st.then(dve.tensor_tensor_scan(tiles[:, 2, :], tiles[:, 1, :], zeros[:, 0:NE], 0.0, ALU.add, ALU.add))
            st.then(dve.tensor_tensor(tiles[:, 3, :], tiles[:, 2, :], tiles[:, 1, :], ALU.subtract))
            st.then(dve.tensor_tensor(before[:, :, :], before[:, :, :], totals[:, :, :], ALU.subtract))
            st.then(dve.tensor_tensor(slot_base[:, :, :], bank[0][:, 0:NT * NE].rearrange("p (t e) -> p t e", e=NE),
                                      before[:, :, :].rearrange("p e t -> p t e"), ALU.add))
            st.then(dve.scalar_tensor_tensor(slot_base[:, :, :], over_t(tiles[:, 3, :]), float(P), slot_base[:, :, :], ALU.mult, ALU.add))
            for k in range(2):
                st.then(dve.tensor_tensor(slot_hot[:, :, :], slot_base[:, :, :], hot[k][:, :, :], ALU.mult))
                st.then(dve.tensor_reduce(slot_f[:, k, :], slot_hot[:, :, :], AX_X, ALU.add))
            st.did(dve.tensor_copy(slot_of[:, :, :], slot_f[:, :, :]))
            st.then(dve.tensor_scalar(slot_q[:, :, :], slot_f[:, :, :], 1 / P, 1 / 512 - 0.5, ALU.mult, ALU.add))
            st.then(dve.tensor_scalar(slot_q[:, :, :], slot_q[:, :, :], ROUNDER, ROUNDER, ALU.add, ALU.subtract))
            st.did(dve.scalar_tensor_tensor(slot_r[:, :, :], slot_q[:, :, :], -float(P), slot_f[:, :, :], ALU.mult, ALU.add))
            st.then(dve.tensor_tensor(started[:, :, :], iota_s[0:1, :].rearrange("p (s r) -> p s r", r=1).to_broadcast([1, NS, NE]),
                                      tiles[0:1, 3, :].rearrange("p (r e) -> p r e", r=1).to_broadcast([1, NS, NE]), ALU.is_ge))
            st.then(dve.tensor_reduce(started_n[:, :], started[:, :, :], AX_X, ALU.add))
            st.did(dve.tensor_scalar(expert_of[:, :], started_n[:, :], -1.0, None, ALU.add))
            st.wait()

            def one_hots(t2, ring):
                for n in range(4):
                    t, k = t2 * 2 + n // 2, n % 2
                    if ring:
                        wait(dve, inv_ps, t2 * 4 - 3 + n)
                    one = (lambda v: v[:, k, t:t + 1]) if isinstance(t, int) else (lambda v: v[:, k, bass.ds(t, 1)])
                    tid = token_id[:, t:t + 1] if isinstance(t, int) else token_id[:, bass.ds(t, 1)]
                    dve.tensor_scalar(at_row[n][:, :], iota_r[:, :], one(slot_r), None, ALU.is_equal)
                    dve.tensor_scalar(at_tile[n][:, :], iota_s[:, :], one(slot_q), tid, ALU.is_equal, ALU.mult).then_inc(inv_ok, 1)

            one_hots(0, False)
            with dve.Fori(1, NT // 2) as t2:
                one_hots(t2, True)
            dve.wait_ge(inv_ps, 2 * NT)
            st.then(dve.tensor_copy(token_of[:, :], bank[2][:, 0:NS]))
            for i in range(2):
                st.did(dve.memset(c_h[i][:, F:FT * P], 0.0))
            st.wait()
            dve.memset(zeros[:, :], 0.0).then_inc(a_done, 1)

            def hidden(s, i):
                wait(dve, c_sl, s + 1)
                wait(dve, c_u, s + 1)
                wait(dve, c_ht, s - 1)
                dve.tensor_tensor(c_h[i % 2][:, 0:F], c_sil[i % 2][:, :], gu_bank[i % 2][1][:, 0:F], ALU.mult).then_inc(c_hk, 1)

            def h_out(s, i):
                wait(dve, c_hea, s + 1)
                dve.tensor_tensor(c_hT[i % 2][:, LO, :, :].rearrange("p a t -> p (a t)"), ht_bank[i % 2][:, 0:FT * P],
                                  c_hT[i % 2][:, HI, :, :].rearrange("p a t -> p (a t)").bitcast(F32), ALU.subtract).then_inc(c_hed, 1)

            def x_low(s, i):
                wait(dve, c_xe, s + 1)
                dve.tensor_tensor(xg_T[i % 2][:, KT:2 * KT, :].rearrange("p a t -> p (a t)"), xg_bank[:, 0:D],
                                  xg_T[i % 2][:, 0:KT, :].rearrange("p a t -> p (a t)").bitcast(F32), ALU.subtract).then_inc(c_xl, 1)

            def step(s, i, first=False, last=False):
                hidden(s, i)
                if not (first and i < 1):
                    h_out(s - 1, (i - 1) % 4)
                if not (last and i == 3):
                    x_low(s + 1, (i + 1) % 4)

            x_low(0, 0)

            for i in range(4):
                step(i, i, first=True)
            with dve.Fori(1, NS // 4 - 1) as s4:
                for i in range(4):
                    step(s4 * 4 + i, i)
            for i in range(4):
                step(NS - 4 + i, i, last=True)
            h_out(NS - 1, 3)

            dve.wait_ge(c_yk, NS)
            for i in range(4):
                dve.wait_ge(c_st[i], 16 * (NS // 4))
            dve.memset(r_rows[1][96:97, :].bitcast(F32), 1.0)
            dve.memset(v_ones[:, :, :, HD:2 * HD], 1.0)

            def qk_split(b, g, n, gs):
                minus, dst = (q_minus, q_rows) if n < 2 else (k_minus, k_rows)
                wait(dve, a_qk, (b * NG + g) * 4 + n + 1)
                if n == 0:
                    wait(dve, b_st, (b * NG + g - 3) * 16)
                dve.scalar_tensor_tensor(dst[g][:, n % 2, :], qk_hi[n % 2][:, :].bitcast(F32), minus[:, 0:1], QK_BANK[gs][n][:, :],
                                         ALU.mult, ALU.add).then_inc(d_qk, 1)

            def maximum(b, g, u):
                j, qt = u // 4, u % 4
                wait(dve, b_s, b * 64 + g * 16 + u + 1)
                if u == 0:
                    wait(dve, d_m, b * NG + g - 1)
                dve.tensor_reduce(top[g % 2][:, j % 2, j // 2, qt:qt + 1], s_bank[u % 2][:, :], AX_X, ALU.max).then_inc(d_max, 1)

            def split_max(b, g):
                wait(dve, d_max, b * 64 + g * 16 + 16)
                wait(dve, b_mt, b * NG + g - 1)
                dst = top_parts[g % 2]
                src = top[g % 2][:, :, :, :].rearrange("p a b t -> p t a b")
                dve.tensor_copy(dst[:, :, :, :, HI], src).then_inc(d_mh, 1)
                wait(dve, d_mh, b * NG + g + 1)
                dve.tensor_tensor(dst[:, :, :, :, LO], src, dst[:, :, :, :, HI].bitcast(F32), ALU.subtract).then_inc(d_m, 1)

            def max_rows(b, g):
                wait(dve, b_mt, b * NG + g + 1)
                wait(dve, m_in[g % 2], b * 128 + 64 * (g // 2))
                dve.tensor_copy(top_T[g % 2][:, :], m_bank[0:8, :]).then_inc(d_mt, 1)

            def hidden_shared(b, f):
                m = P if f < SFT - 1 else SF_LAST
                h = h_f[f % 2][0:m, :]
                wait(dve, b_gu, b * SFT + f + 1)
                wait(dve, a_th, b * SFT + f + 1)
                dve.scalar_tensor_tensor(h, h, 1.0, u_bank[0:m, :], ALU.add, ALU.mult).then_inc(d_ga, 1)
                wait(dve, d_ga, b * SFT + f + 1)
                dve.scalar_tensor_tensor(h, h, 0.5, g_bank[0:m, :], ALU.mult, ALU.mult).then_inc(d_hf, 1)

            def low_rank_low(b, n):
                wait(dve, a_r, b * 3 + n + 1)
                dve.tensor_tensor(r_rows[n][64:96, :], R_BANK[n][64:96, :], r_rows[n][64:96, :].bitcast(F32), ALU.subtract).then_inc(d_r, 1)

            def add_down(b, t):
                wait(dve, b_dn, b * TPB + t + 1)
                if t == 0:
                    wait(dve, p_y, b + 1)
                dve.tensor_tensor(o_b[:, t, :], (g_bank, u_bank, g_bank, g_bank)[t][:, 0:D], o_b[:, t, :], ALU.add).then_inc(d_dn, 1)

            def normalise(b, t):
                ov = g_bank[:, :].rearrange("p (h c) -> p h c", h=HEADS)
                wait(dve, b_ot, b * TPB + t + 1)
                wait(dve, d_ao, b * TPB + max(t - 1, 0))
                dve.reciprocal(o_inv[:, t % 2, :], ov[:, :, HD]).then_inc(d_inv, 1)
                wait(dve, d_inv, b * TPB + t + 1)
                wait(dve, b_at, b * TPB + max(t - 1, 0))
                dve.tensor_tensor(ao[t % 2][:, :].rearrange("p (h d) -> p h d", h=HEADS), ov[:, :, 0:HD],
                                  o_inv[:, t % 2, :].rearrange("p (h r) -> p h r", r=1).to_broadcast([P, HEADS, HD]),
                                  ALU.mult).then_inc(d_ao, 1)

            def back_low(b, t):
                wait(dve, a_at, b * TPB + t + 1)
                o = ao_T[:, :, :, t * P:(t + 1) * P]
                dve.tensor_tensor(o[:, LO, :, :], u_bank[:, t % 2 * D:(t % 2 + 1) * D].rearrange("p (k t) -> p k t", k=KT),
                                  o[:, HI, :, :].bitcast(F32), ALU.subtract).then_inc(d_at, 1)

            def add_o(b, half):
                wait(dve, b_out, b * 2 + half + 1)
                wait(dve, d_dn, b * TPB + TPB)
                o = o_b[:, 2 * half:2 * half + 2, :].rearrange("p t d -> p (t d)")
                dve.tensor_tensor(o, (u_bank, g_bank)[half][:, :], o, ALU.add).then_inc(d_out, 1)

            def slot(b, g):
                now, (pb, pg), (nb, ng), (qb, qg) = there(b), after(b, g, -1), after(b, g, 1), after(b, g, 2)
                for s in range(STEPS):
                    if s == STEPS - AHEAD and there(nb):
                        split_max(nb, ng)
                    if s < STEPS - AHEAD:
                        if there(nb):
                            maximum(nb, ng, s + AHEAD)
                    elif there(qb):
                        maximum(qb, qg, s - STEPS + AHEAD)
                    if s == STEPS - AHEAD and there(nb):
                        max_rows(nb, ng)
                    for n in range(4):
                        if s == QK_STEP[g][n] + 1 and there(qb):
                            qk_split(qb, qg, n, g)
                    if g == 0 and there(b - 1):
                        if s in (3, 5, 7, 9):
                            normalise(b - 1, s // 2 - 1)
                        if s in (6, 8, 10, 12):
                            back_low(b - 1, s // 2 - 3)
                        if s == 14:
                            wait(dve, a_res, b)
                            dve.tensor_tensor(ro[64:96, :], g_bank[64:96, :], ro[64:96, :].bitcast(F32), ALU.subtract).then_inc(d_res, 1)
                        if s == 15:
                            add_o(b - 1, 0)
                            add_o(b - 1, 1)
                    if F0[g] is not None and there(b + (g == 3)) and s in (4, 9, 14):
                        hidden_shared(b + (g == 3), F0[g] + s // 5)
                    if g == 2 and now:
                        for t, at in enumerate((2, 4, 11, 14)):
                            if s == at:
                                add_down(b, t)
                    if g == 2 and there(b + 1):
                        for n, at in enumerate((4, 6, 12)):
                            if s == at:
                                low_rank_low(b + 1, n)

            slots(dve, slot)


A_ANGLE = 7
A_THRICE = 25


_INS = (["L0_attn_x"] + [f"L0_attn_{what}_{name}" for name in "qkvo" for what in ("basis", "phase", "amp")]
        + [f"L0_ffn_{name}" for name in ("gate_w", "w_gate", "w_up", "w_down", "sw_gate", "sw_up", "sw_down")])


def kernel(**inputs):
    import numpy as _np
    import concourse.bacc as _bacc
    from concourse import mybir as _mybir
    from concourse.bass_utils import run_bass_kernel_spmd as _run

    nc = _bacc.Bacc("TRN2", target_bir_lowering=False, num_devices=1)
    arrays, args = {}, {}
    for name in _INS:
        a = _np.ascontiguousarray(inputs[name])
        arrays[f"in_{name}_dram"] = a
        args[name] = nc.dram_tensor(f"in_{name}_dram", a.shape, _mybir.dt.from_np(a.dtype), kind="ExternalInput").ap()
    x = inputs["L0_attn_x"]
    out = nc.dram_tensor("out_0_dram", x.shape, _mybir.dt.from_np(_np.dtype("float32")), kind="ExternalOutput").ap()
    attn = {name: tuple(args[f"L0_attn_{what}_{name}"] for what in ("basis", "phase", "amp")) for name in "qkvo"}
    build_program(nc, args["L0_attn_x"], attn, *(args[f"L0_ffn_{name}"] for name in
                                                 ("gate_w", "w_gate", "w_up", "w_down", "sw_gate", "sw_up", "sw_down")), out)
    r = _run(nc, [arrays], core_ids=[0])
    return r.results[0]["out_0_dram"]
```

```python
import math
from contextlib import ExitStack

import concourse.bass as bass
from concourse import mybir

P = 128
ALU = mybir.AluOpType
ACT = mybir.ActivationFunctionType
AX_X = mybir.AxisListType.X
F32 = mybir.dt.float32
F32R = mybir.dt.float32r
BF16 = mybir.dt.bfloat16
I32 = mybir.dt.int32
U32 = mybir.dt.uint32

HI, LO = 0, 1
PRODUCTS = ((HI, HI), (LO, HI), (HI, LO))

LN_EPS = 1e-5
TOPK_EPS = 1e-20
ROUTE_SCALE = 2.5
TURN_1 = 6.28125
TURN_2 = math.floor((2 * math.pi - TURN_1) * 2**21) / 2**21
TURN_3 = 2 * math.pi - TURN_1 - TURN_2
PI_BELOW = 3.1415925
ROUNDER = 1.5 * 2**23


class Steps:

    def __init__(self, eng, sem, base=0):
        self.eng, self.sem, self.base, self.n = eng, sem, base, 0

    def did(self, ins):
        ins.then_inc(self.sem, 1)
        self.n += 1
        return self.n

    def value(self, n=None):
        return self.base + (self.n if n is None else n)

    def wait(self, n=None):
        self.eng.wait_ge(self.sem, self.value(n))

    def then(self, ins):
        self.did(ins)
        self.wait()


def wait(eng, sem, value):
    if isinstance(value, int) and value <= 0:
        return
    eng.wait_ge(sem, value)


def build_program(nc, x, attn, gate_w, w_gate, w_up, w_down, sw_gate, sw_up, sw_down, out):
    NB, L, D = x.shape
    NE, _, F = w_gate.shape
    SF = sw_gate.shape[1]
    HARM = attn["q"][0].shape[0]
    HEADS = 16
    HD = D // HEADS
    PROJ = ("q", "k", "v", "o")
    KT = D // P
    TPB = L // P
    NT = NB * TPB
    FT = -(-F // P)
    F_LAST = F - (FT - 1) * P
    GU = 2 * F
    W_GU = KT * GU
    W_ALL = W_GU + FT * D
    NS = 2 * NT + NE
    PAIRS = NB // 2
    assert NB == NE

    xn_dram = nc.dram_tensor("xn_rows", (NB * L, D), F32).ap()
    xT_dram = nc.dram_tensor("xn_T_split", (NB, P, 2 * KT * L), F32).ap()
    y_dram = nc.dram_tensor("expert_rows", (NS * P, D), F32).ap()

    ctx = ExitStack()

    def sb(name, shape, dt, where=None):
        return (where or ctx).enter_context(nc.sbuf_tensor(name, shape, dt))

    def sem(name):
        return ctx.enter_context(nc.semaphore(name))

    with ctx:
        bank = [ctx.enter_context(nc.psum_tensor(f"bank{i}", [P, 512], F32)) for i in range(8)]

        ident_f = sb("ident_f", [P, P], F32)
        q_minus = sb("q_minus", [P, 1], F32)
        k_minus = sb("k_minus", [P, 1], F32)
        basis_T = sb("basis_T", [P, KT, 2, len(PROJ), 3, HARM], F32R)
        wq_rows = sb("wq_rows", [97, HEADS, 64], F32R)
        wk_rows = sb("wk_rows", [97, HEADS, 64], F32R)
        wv_rows = sb("wv_rows", [96, D], F32R)
        wo_rows = sb("wo_rows", [96, D], F32R)
        share = sb("share", [P, NT, 2], F32)
        slot_of = sb("slot_of", [P, 2, NT], I32)
        token_of = sb("token_of", [P, NS], I32)
        expert_of = sb("expert_of", [1, NS], I32)

        early = ExitStack()
        w_exp = sb("w_exp", [P, NE, 2, W_ALL], F32R, early)
        raw_all = sb("raw_all", [P, 2 * W_ALL], F32, early)
        raw = [raw_all[:, i * W_ALL:(i + 1) * W_ALL] for i in range(2)]
        zeros = sb("zeros", [P, NT], F32, early)

        region = ExitStack()
        gate_T = sb("gate_T", [P, KT, 2, NE], F32R, region)
        stats = sb("stats", [P, NT, 6], F32, region)
        mean_var = sb("mean_var", [P, NT, 2], F32, region)
        rs = sb("rs", [P, 4, NT], F32, region)
        iota_e = sb("iota_e", [P, NE], F32, region)
        iota_s = sb("iota_s", [P, NS], F32, region)
        iota_r = sb("iota_r", [P, P], F32, region)
        token_id = sb("token_id", [P, NT], F32, region)
        rows = ExitStack()
        x_all = sb("x_all", [P, NT, D], F32, rows)
        rows.close()
        routing = ExitStack()
        lg = sb("lg", [P, NT, NE], F32, routing)
        pr = sb("pr", [P, NT, NE], F32, routing)
        best = sb("best", [P, NT, NE], F32, routing)
        best_at = sb("best_at", [P, NT, NE], U32, routing)
        best_atf = sb("best_atf", [P, 2, NT], F32, routing)
        row = sb("row", [P, 4, NT], F32, routing)
        hot = [sb(f"hot{k}", [P, NT, NE], F32, routing) for k in range(2)]
        hot_b = sb("hot_b", [P, NT, NE], BF16, routing)
        before = sb("before", [P, NE, NT], F32, routing)
        totals = sb("totals", [P, NE, NT], F32, routing)
        tiles = sb("tiles", [P, 4, NE], F32, routing)
        slot_base, slot_hot = pr, lg
        slot_f = sb("slot_f", [P, 2, NT], F32, routing)
        slot_q = sb("slot_q", [P, 2, NT], F32, routing)
        slot_r = sb("slot_r", [P, 2, NT], F32, routing)
        started = sb("started", [1, NS, NE], F32, routing)
        started_n = sb("started_n", [1, NS], F32, routing)
        at_row = [sb(f"at_row{i}", [P, 2, TPB, P], F32R, routing) for i in range(2)]
        at_tile1 = [sb(f"at_tile1{i}", [P, 2, TPB, NS], F32, routing) for i in range(2)]
        at_tile = [sb(f"at_tile{i}", [P, 2, TPB, NS], F32R, routing) for i in range(2)]
        routing.close()
        region.close()

        in_c = ExitStack()
        xg = [sb(f"xg{i}", [P, D], F32, in_c) for i in range(4)]
        xg_T = [sb(f"xg_T{i}", [P, 2 * KT, P], F32R, in_c) for i in range(2)]
        c_sil = [sb(f"c_sil{i}", [P, F], F32, in_c) for i in range(2)]
        c_h = [sb(f"c_h{i}", [P, FT * P], F32, in_c) for i in range(2)]
        c_hT = [sb(f"c_hT{i}", [P, 2, FT, P], F32R, in_c) for i in range(2)]
        c_y = [sb(f"c_y{i}", [P, D], F32, in_c) for i in range(4)]
        xT_b = sb("xT_b", [P, 2, KT, L], F32R, in_c)
        in_c.close()
        early.close()

        tail = ExitStack()
        sb("first_experts", [P, NE - 2, 2, W_ALL], F32R, tail)
        x_n = [sb(f"x_n{i}", [P, TPB, D], F32, tail) for i in range(2)]
        x_T = [sb("x_T0", [P, 2, KT, L], F32R, tail)]
        upper = sb("upper", [P, P], BF16, tail)
        ones_b = sb("ones_b", [P, P], BF16, tail)
        second = ExitStack()
        x_T.append(sb("x_T1", [P, 2, KT, L], F32R, second))
        second.close()
        prep = ExitStack()
        gate_raw = sb("gate_raw", [NE, D], F32, prep)
        basis_raw = sb("basis_raw", [P, D], F32, prep)
        phase = sb("phase", [P, len(PROJ), KT, HARM], F32, prep)
        amp = sb("amp", [P, len(PROJ), KT, HARM], F32, prep)
        turns = sb("turns", [P, len(PROJ) * KT * HARM], F32, prep)
        angle = sb("angle", [P, len(PROJ) * KT * HARM], F32, prep)
        w_thrice = sb("w_thrice", [P, len(PROJ) * KT, 3, HARM], F32, prep)
        w_hi = sb("w_hi", [96, len(PROJ), D], F32R, prep)
        prep.close()
        tail.close()

        SFT = -(-SF // P)
        SF_LAST = SF - (SFT - 1) * P
        S_GU = KT * 2 * SF
        S_ALL = S_GU + SFT * D
        NG = HEADS // 4
        QKV_ROWS = 50
        late = ExitStack()
        w_sh = sb("w_sh", [P, 2, S_ALL], F32R, late)
        r_rows = [sb(f"r_{n}", [97, L], F32R, late) for n in "qkv"]
        qk_hi = [sb(f"qk_hi{i}", [P, L], F32R, late) for i in range(2)]
        q_rows = [sb(f"q_rows{g}", [P, 2, L], F32R, late) for g in range(NG)]
        k_rows = [sb(f"k_rows{g}", [P, 2, L], F32R, late) for g in range(NG)]
        top = [sb(f"top{i}", [P, 2, 2, TPB], F32, late) for i in range(2)]
        top_parts = [sb(f"top_parts{i}", [P, TPB, 2, 2, 2], F32R, late) for i in range(2)]
        top_T = [sb(f"top_T{i}", [8, L], F32R, late) for i in range(2)]
        prob = [sb(f"prob{i}", [P, 4, L], F32, late) for i in range(2)]
        v_ones = sb("v_ones", [P, TPB, HEADS, 2 * HD], F32, late)
        o_T = sb("o_T", [P, NG, L], F32, late)
        o_inv = sb("o_inv", [P, 2, HEADS], F32, late)
        ao = [sb(f"ao{i}", [P, D], F32, late) for i in range(2)]
        ao_T = sb("ao_T", [P, 2, KT, L], F32R, late)
        ro = sb("ro", [96, L], F32R, late)
        h_f = [sb(f"h_f{i}", [P, L], F32, late) for i in range(2)]
        o_b = sb("o_b", [P, TPB, D], F32, late)
        y_b = sb("y_b", [P, TPB, 2, D], F32, late)
        s_raw = raw_all
        assert S_ALL == 2 * W_ALL
        h_T = sb("h_T", [P, 2, SFT, L], F32R, late)
        late.close()

        x_in = [sem(f"x_in{q}") for q in range(4)]
        small_in = sem("small_in")
        raw_in = [sem(f"raw_in{i}") for i in range(2)]
        hi_done = sem("hi_done")
        lo_done = sem("lo_done")
        consts = sem("consts")
        dve_a = sem("dve_a")
        act_a = sem("act_a")
        sin_done = sem("sin_done")
        pe_prep = sem("pe_prep")
        prep_done = sem("prep_done")
        stats_ok = sem("stats_ok")
        root_ok = sem("root_ok")
        xn_ok = sem("xn_ok")
        xn_stored = [sem(f"xn_stored{i}") for i in range(2)]
        xT_stored = [sem(f"xT_stored{i}") for i in range(2)]
        xt_ps = sem("xt_ps")
        xt_hi = sem("xt_hi")
        xt_lo = sem("xt_lo")
        lg_ps = sem("lg_ps")
        lg_max = sem("lg_max")
        lg_exp = sem("lg_exp")
        hot_ok = sem("hot_ok")
        count_ps = sem("count_ps")
        inv_eq = sem("inv_eq")
        inv_ok = sem("inv_ok")
        inv_ps = sem("inv_ps")
        a_done = sem("a_done")

        c_x = [sem(f"c_x{i}") for i in range(4)]
        c_xt = sem("c_xt")
        c_xe = sem("c_xe")
        c_xl = sem("c_xl")
        c_g = sem("c_g")
        c_u = sem("c_u")
        c_sl = sem("c_sl")
        c_hk = sem("c_hk")
        c_ht = sem("c_ht")
        c_hea = sem("c_hea")
        c_hed = sem("c_hed")
        c_d = sem("c_d")
        c_yk = sem("c_yk")
        c_st = [sem(f"c_st{i}") for i in range(4)]
        c_pad = sem("c_pad")

        s_in = sem("s_in")
        s_hi = sem("s_hi")
        s_lo = sem("s_lo")
        xT_in = sem("xT_in")
        ob_in = sem("ob_in")
        y_in = sem("y_in")
        m_in = [sem(f"m_in{i}") for i in range(2)]
        b_r, b_v, b_qk, b_s, b_mt, b_st, b_pv, b_g, b_gu, b_ot, b_at, b_res, b_dn, b_out = (
            sem(f"b_{n}") for n in ("r", "v", "qk", "s", "mt", "st", "pv", "g", "gu", "ot", "at", "res", "dn", "out"))
        a_r, a_v, a_qk, a_exp, a_th, a_hh, a_ot, a_at, a_res = (
            sem(f"a_{n}") for n in ("r", "v", "qk", "exp", "th", "hh", "ot", "at", "res"))
        d_r, d_qk, d_max, d_mh, d_m, d_mt, d_ga, d_hf, d_inv, d_ao, d_at, d_res, d_dn, d_out = (
            sem(f"d_{n}") for n in ("r", "qk", "max", "mh", "m", "mt", "ga", "hf", "inv", "ao", "at", "res", "dn", "out"))
        p_h = sem("p_h")
        p_ys = sem("p_ys")
        p_yy = sem("p_yy")
        p_y = sem("p_y")
        o_st = sem("o_st")

        block = ctx.enter_context(nc.Block())

        s_bank, st_bank, ot_bank, g_bank, u_bank, m_bank = bank[0:2], bank[2:4], bank[4], bank[5], bank[6], bank[7]

        STEPS = 4 * TPB
        AHEAD = 5
        LAST = NB - 1
        F_AT = [{}, {}, {}, {}]
        for g, ahead, f, start in ((1, 0, 3, 2), (1, 0, 4, 6), (1, 0, 5, 10), (3, 1, 0, 1), (3, 1, 1, 6), (3, 1, 2, 11)):
            for n in range(5):
                F_AT[g].setdefault(start + n, []).append((ahead, f, n))

        def shared_tiles(b, g, s):
            return [(b + ahead, f, n) for ahead, f, n in F_AT[g].get(s, ()) if there(b + ahead)]

        QK_STEP = ((0, 3, 5, 7), (0, 3, 5, 8), (5, 6, 8, 9), (0, 3, 5, 8))
        QK_BANK = ((m_bank,) * 4, (m_bank,) * 4, (m_bank, u_bank, g_bank, m_bank), (m_bank,) * 4)
        R_BANK = (m_bank, g_bank, u_bank)

        def there(b):
            return not isinstance(b, int) or 0 <= b < NB

        def after(b, g, n):
            return (b + (g + n) // NG, (g + n) % NG)

        def slots(eng, slot):
            slot(-1, 2)
            slot(-1, 3)
            for g in range(NG):
                slot(0, g)
            with eng.Fori(1, LAST) as b:
                for g in range(NG):
                    slot(b, g)
            for g in range(NG):
                slot(LAST, g)
            slot(NB, 0)
            slot(NB, 1)

        xt_bank = [[bank[2], bank[3]], [bank[4], bank[5]]]
        lg_bank = bank[6]
        gu_bank = [[bank[0], bank[1]], [bank[2], bank[3]]]
        xg_bank, y_bank = bank[4], bank[5]
        ht_bank = [bank[6], bank[7]]

        @block.sync
        def _(sp):
            def load_x(q):
                n = NB // 4
                for j in range(n):
                    sp.dma_start(x_all[:, (q * n + j) * TPB:(q * n + j + 1) * TPB, :],
                                 x[q * n + j].rearrange("(t p) d -> p t d", p=P)).then_inc(x_in[q], 16)

            load_x(0)
            sp.dma_start(gate_raw[:, :], gate_w).then_inc(small_in, 16)
            for i, name in enumerate(PROJ):
                basis, ph, am = attn[name]
                sp.dma_start(basis_raw[i * HARM:(i + 1) * HARM, :], basis).then_inc(small_in, 16)
                sp.dma_start(phase[:, i, :, :], ph.rearrange("(a p) h -> p a h", p=P)).then_inc(small_in, 16)
                sp.dma_start(amp[:, i, :, :], am.rearrange("(a p) h -> p a h", p=P)).then_inc(small_in, 16)
            for q in range(1, 4):
                load_x(q)
            wait(sp, consts, 1)
            def load_experts(e2):
                for i in range(2):
                    e = e2 * 2 + i
                    r = raw[i]
                    wait(sp, hi_done, e2 * 2 + i - 1)
                    wait(sp, lo_done, e2 * 2 + i - 1)
                    gu = r[:, 0:W_GU].rearrange("p (k n) -> p k n", k=KT)
                    dn = r[:, W_GU:W_ALL].rearrange("p (k n) -> p k n", k=FT)
                    one = lambda w: w[bass.ds(e, 1)] if not isinstance(e, int) else w[e:e + 1]
                    sp.dma_start(gu[:, :, 0:F], one(w_gate).rearrange("a (k p) f -> p (a k) f", p=P)).then_inc(raw_in[i], 16)
                    sp.dma_start(gu[:, :, F:GU], one(w_up).rearrange("a (k p) f -> p (a k) f", p=P)).then_inc(raw_in[i], 16)
                    sp.dma_start(dn[:, 0:FT - 1, :],
                                 one(w_down)[:, 0:(FT - 1) * P, :].rearrange("a (k p) f -> p (a k) f", p=P)).then_inc(raw_in[i], 16)
                    sp.dma_start(dn[0:F_LAST, FT - 1, :],
                                 one(w_down)[:, (FT - 1) * P:F, :].rearrange("a p f -> (a p) f")).then_inc(raw_in[i], 16)

            def store_rows(b2):
                for i in range(2):
                    b = b2 * 2 + i
                    rows = xn_dram.rearrange("(b t p) c -> b p t c", t=TPB, p=P)
                    wait(sp, xn_ok, b + 1)
                    sp.dma_start(rows[b] if isinstance(b, int) else rows[bass.ds(b, 1)].rearrange("b p t c -> (b p) t c"),
                                 x_n[i][:, :, :]).then_inc(xn_stored[i], 16)
                    wait(sp, xt_hi, b + 1)
                    wait(sp, xt_lo, b + 1)
                    sp.dma_start(xT_dram[b] if isinstance(b, int) else xT_dram[bass.ds(b, 1)].rearrange("b p n -> (b p) n"),
                                 x_T[i][:, :, :, :].rearrange("p a k l -> p (a k l)").bitcast(F32)).then_inc(xT_stored[i], 16)

            load_experts(0)
            store_rows(0)
            with sp.Fori(1, PAIRS) as b2:
                store_rows(b2)
            with sp.Fori(1, PAIRS) as e2:
                load_experts(e2)
            sp.wait_ge(hi_done, NE)
            sp.wait_ge(lo_done, NE)
            gu = s_raw[:, 0:S_GU].rearrange("p (k n) -> p k n", k=KT)
            dn = s_raw[:, S_GU:S_ALL].rearrange("p (k n) -> p k n", k=SFT)
            sp.dma_start(gu[:, :, 0:SF], sw_gate.rearrange("(k p) f -> p k f", p=P)).then_inc(s_in, 16)
            sp.dma_start(gu[:, :, SF:2 * SF], sw_up.rearrange("(k p) f -> p k f", p=P)).then_inc(s_in, 16)
            sp.dma_start(dn[:, 0:SFT - 1, :], sw_down[0:(SFT - 1) * P, :].rearrange("(k p) f -> p k f", p=P)).then_inc(s_in, 16)
            sp.dma_start(dn[0:SF_LAST, SFT - 1, :], sw_down[(SFT - 1) * P:SF, :]).then_inc(s_in, 16)


            sp.wait_ge(a_done, 1)
            for i in range(2):
                sp.wait_ge(xT_stored[i], 16 * PAIRS)
            sp.dma_start(xT_b[:, :, :, :].rearrange("p a k l -> p (a k l)").bitcast(F32), xT_dram[0]).then_inc(xT_in, 16)
            with sp.Fori(0, NS // 4) as s4:
                for i in range(4):
                    s = s4 * 4 + i
                    wait(sp, c_yk, s + 1)
                    sp.dma_start(y_dram.rearrange("(s p) d -> s p d", p=P)[bass.ds(s, 1)].rearrange("a p d -> (a p) d"),
                                 c_y[i][:, :]).then_inc(c_st[i], 16)
            for i in range(4):
                sp.wait_ge(c_st[i], 16 * (NS // 4))

            def load_xT(b):
                wait(sp, b_gu, b * SFT)
                one = xT_dram[bass.ds(b, 1)].rearrange("b p n -> (b p) n") if not isinstance(b, int) else xT_dram[b]
                sp.dma_start(xT_b[:, :, :, :].rearrange("p a k l -> p (a k l)").bitcast(F32), one).then_inc(xT_in, 16)

            def load_x_b(b):
                wait(sp, o_st, b * 32)
                sp.dma_start(o_b[:, :, :], x[bass.ds(b, 1)].rearrange("b (t p) d -> p (b t) d", p=P)).then_inc(ob_in, 16)

            def slot(b, g):
                if g == 1 and there(b - 1):
                    for h in range(2):
                        wait(sp, d_out, (b - 1) * 2 + h + 1)
                        sp.dma_start(out[bass.ds(b - 1, 1), h * 2 * P:(h + 1) * 2 * P, :].rearrange("a (t p) d -> p (a t) d", p=P),
                                     o_b[:, 2 * h:2 * h + 2, :]).then_inc(o_st, 16)
                if g == 1 and there(b):
                    load_x_b(b)
                nb, ng = after(b, g, 1)
                if there(nb):
                    wait(sp, d_mt, nb * NG + ng + 1)
                    for n in range(4):
                        par, pair = n // 2, n % 2
                        sp.dma_start(q_rows[ng][64 * par + 48:64 * par + 50, pair, :].bitcast(F32),
                                     top_T[ng % 2][2 * n:2 * n + 2, :].bitcast(F32)).then_inc(m_in[ng % 2], 16)
                if g == 1 and there(b + 1):
                    load_xT(b + 1)


            slots(sp, slot)
            sp.wait_ge(o_st, 32 * NB)

        @block.gpsimd
        def _(pool):
            st = Steps(pool, c_pad)
            for i in range(2):
                pool.memset(raw[i][96:128, W_GU + (FT - 1) * D:W_ALL], 0.0).then_inc(c_pad, 1)
            pool.wait_ge(c_pad, 2)
            pool.memset(zeros[:, :], 0.0).then_inc(consts, 1)
            st.n = 2
            st.did(pool.memset(ident_f[:, :], 0.0))
            st.did(pool.memset(upper[:, :], 1.0))
            pool.memset(ones_b[:, :], 1.0)
            pool.iota(iota_e[:, :], [[1, NE]], base=0, channel_multiplier=0, allow_small_or_imprecise_dtypes=True)
            pool.iota(iota_s[:, :], [[1, NS]], base=0, channel_multiplier=0, allow_small_or_imprecise_dtypes=True)
            pool.iota(iota_r[:, :], [[1, P]], base=0, channel_multiplier=0, allow_small_or_imprecise_dtypes=True)
            pool.iota(token_id[:, :], [[P, NT]], base=0, channel_multiplier=1, allow_small_or_imprecise_dtypes=True)
            pool.memset(wq_rows[:, :, :].bitcast(F32), 0.0)
            st.did(pool.memset(wk_rows[:, :, :].bitcast(F32), 0.0))
            st.wait()
            st.did(pool.affine_select(out=ident_f[:, :], in_=ident_f[:, :], compare_op=ALU.not_equal, fill=1.0,
                                      base=0, pattern=[[-1, P]], channel_multiplier=1))
            st.did(pool.affine_select(out=upper[:, :], in_=upper[:, :], compare_op=ALU.is_gt, fill=0.0,
                                      base=0, pattern=[[1, P]], channel_multiplier=-1))
            st.wait()
            pool.memset(zeros[:, :], 0.0).then_inc(consts, 1)
            def low_parts(e2):
                for i in range(2):
                    e = e2 * 2 + i
                    wait(pool, hi_done, e + 1)
                    pool.tensor_tensor(w_exp[:, bass.ds(e, 1), LO, :].rearrange("p a n -> p (a n)"), raw[i][:, :],
                                       w_exp[:, bass.ds(e, 1), HI, :].rearrange("p a n -> p (a n)").bitcast(F32),
                                       ALU.subtract).then_inc(lo_done, 1)

            with pool.Fori(0, NE // 2 - 1) as e2:
                low_parts(e2)
            pool.wait_ge(a_done, 1)
            for i in range(2):
                pool.wait_ge(xn_stored[i], 16 * PAIRS)

            def gather(s):
                wait(pool, c_xt, s - 3)
                pool.indirect_dma_start(xg[s % 4][:, :], None, xn_dram,
                                        bass.IndirectOffsetOnAxis(token_of[:, s:s + 1], 0)).then_inc(c_x[s % 4], 16)

            for s in range(4):
                gather(s)
            low_parts(NE // 2 - 1)
            for s in range(4, NS):
                gather(s)

            pool.wait_ge(s_hi, 1)
            pool.tensor_tensor(w_sh[:, LO, :], s_raw[:, :], w_sh[:, HI, :].bitcast(F32), ALU.subtract).then_inc(s_lo, 1)
            pool.wait_ge(s_lo, 1)
            for i in range(4):
                pool.wait_ge(c_st[i], 16 * (NS // 4))

            def hidden_low(b, f):
                m = P if f < SFT - 1 else SF_LAST
                n = b * SFT + f
                wait(pool, a_hh, n + 1)
                wait(pool, b_dn, b * TPB)
                pool.tensor_tensor(h_T[0:m, LO, f, :], h_f[f % 2][0:m, :], h_T[0:m, HI, f, :].bitcast(F32),
                                   ALU.subtract).then_inc(p_h, 1)

            for b in range(NB):
                for f in range(3):
                    hidden_low(b, f)
                wait(pool, p_y, b)
                for t in range(TPB):
                    for k in range(2):
                        pool.indirect_dma_start(y_b[:, t, k, :], None, y_dram,
                                                bass.IndirectOffsetOnAxis(slot_of[:, k, b * TPB + t:b * TPB + t + 1], 0)).then_inc(y_in, 16)
                wait(pool, y_in, (b + 1) * TPB * 32)
                for t in range(TPB):
                    for k in range(2):
                        pool.tensor_scalar(y_b[:, t, k, :], y_b[:, t, k, :], share[:, b * TPB + t, k:k + 1], None, ALU.mult).then_inc(p_ys, 1)
                wait(pool, p_ys, (b + 1) * TPB * 2)
                pool.tensor_tensor(y_b[:, :, 0, :], y_b[:, :, 0, :], y_b[:, :, 1, :], ALU.add).then_inc(p_yy, 1)
                hidden_low(b, 3)
                hidden_low(b, 4)
                wait(pool, p_yy, b + 1)
                wait(pool, ob_in, (b + 1) * 16)
                pool.tensor_tensor(o_b[:, :, :], o_b[:, :, :], y_b[:, :, 0, :], ALU.add).then_inc(p_y, 1)
                hidden_low(b, 5)

        @block.scalar
        def _(act):
            st = Steps(act, act_a)
            wait(act, dve_a, A_ANGLE)
            act.activation(angle[:, :], angle[:, :], ACT.Sin).then_inc(sin_done, 1)
            wait(act, stats_ok, 1)
            act.activation(rs[:, 1, :], rs[:, 0, :], ACT.Sqrt).then_inc(root_ok, 1)

            def high_parts(e2):
                for i in range(2):
                    e = e2 * 2 + i
                    wait(act, raw_in[i], (e2 + 1) * 64)
                    act.activation(w_exp[:, bass.ds(e, 1), HI, :].rearrange("p a n -> p (a n)"), raw[i][:, :],
                                   ACT.Copy).then_inc(hi_done, 1)

            def pair(b2):
                for i in range(2):
                    b = b2 * 2 + i
                    wait(act, xt_ps, b + 1)
                    wait(act, lg_ps, b - 1)
                    wait(act, xT_stored[i], b2 * 16)
                    for k in range(KT):
                        ins = act.activation(x_T[i][:, HI, k, :], xt_bank[i][k][:, :], ACT.Copy)
                    ins.then_inc(xt_hi, 1)

            act.wait_ge(prep_done, 1)
            pair(0)
            with act.Fori(1, PAIRS - 1) as b2:
                pair(b2)
            high_parts(0)
            pair(PAIRS - 1)
            act.wait_ge(lg_max, 1)
            act.activation(pr[:, :, :], lg[:, :, :], ACT.Exp).then_inc(lg_exp, 1)
            with act.Fori(1, PAIRS - 1) as e2:
                high_parts(e2)

            def x_out(s, i):
                wait(act, c_xt, s + 1)
                wait(act, c_u, s - 1)
                act.activation(xg_T[i % 2][:, 0:KT, :].rearrange("p a t -> p (a t)"), xg_bank[:, 0:D], ACT.Copy).then_inc(c_xe, 1)

            def silu(s, i):
                wait(act, c_g, s + 1)
                wait(act, c_hk, s - 1)
                act.activation(c_sil[i % 2][:, :], gu_bank[i % 2][0][:, 0:F], ACT.Silu).then_inc(c_sl, 1)

            def h_out(s, i):
                wait(act, c_ht, s + 1)
                wait(act, c_d, s - 1)
                act.activation(c_hT[i % 2][:, HI, :, :].rearrange("p a t -> p (a t)"), ht_bank[i % 2][:, 0:FT * P], ACT.Copy).then_inc(c_hea, 1)

            def y_out(s, i):
                wait(act, c_d, s + 1)
                wait(act, c_st[i], (s // 4) * 16 if isinstance(s, int) else (s - i) * 4)
                act.activation(c_y[i][:, :], y_bank[:, 0:D], ACT.Copy).then_inc(c_yk, 1)

            def step(s, i, first=False, last=False):
                silu(s, i)
                if not (last and i == 3):
                    x_out(s + 1, (i + 1) % 4)
                if not (first and i < 1):
                    h_out(s - 1, (i - 1) % 4)
                if not (first and i < 2):
                    y_out(s - 2, (i - 2) % 4)

            act.wait_ge(a_done, 1)
            high_parts(NE // 2 - 1)
            x_out(0, 0)
            for i in range(4):
                step(i, i, first=True)
            with act.Fori(1, NS // 4 - 1) as s4:
                for i in range(4):
                    step(s4 * 4 + i, i)
            for i in range(4):
                step(NS - 4 + i, i, last=True)
            h_out(NS - 1, 3)
            y_out(NS - 2, 2)
            y_out(NS - 1, 3)

            def qk_high(b, g, n, gs):
                wait(act, b_qk, (b * NG + g) * 4 + n + 1)
                wait(act, d_qk, (b * NG + g) * 4 + n - 1)
                act.activation(qk_hi[n % 2][:, :], QK_BANK[gs][n][:, :], ACT.Copy).then_inc(a_qk, 1)

            def tanh(b, f):
                wait(act, b_g, b * SFT + f + 1)
                wait(act, p_h, b * SFT + f - 1)
                m = P if f < SFT - 1 else SF_LAST
                act.activation(h_f[f % 2][0:m, :], g_bank[0:m, :], ACT.Tanh, scale=0.5).then_inc(a_th, 1)

            def hidden_high(b, f):
                wait(act, d_hf, b * SFT + f + 1)
                wait(act, b_dn, b * TPB)
                m = P if f < SFT - 1 else SF_LAST
                act.activation(h_T[0:m, HI, f, :], h_f[f % 2][0:m, :], ACT.Copy).then_inc(a_hh, 1)

            def values_out(b, half):
                wait(act, b_v, b * 2 + half + 1)
                wait(act, b_pv, (b - 1) * 16 + (half + 1) * 8)
                act.activation(v_ones[:, :, half * 8:half * 8 + 8, 0:HD],
                               (u_bank, m_bank)[half][:, :].rearrange("p (t h d) -> p t h d", t=TPB, h=HEADS // 2), ACT.Copy).then_inc(a_v, 1)

            def low_rank_high(b, n):
                wait(act, b_r, b * 3 + n + 1)
                act.activation(r_rows[n][0:96, :], R_BANK[n][0:96, :], ACT.Copy).then_inc(a_r, 1)

            def exponent(b, g, s):
                kt, j = s // 4, s % 4
                if j == 0:
                    wait(act, b_pv, b * 16 + g * 4 + kt - 1)
                wait(act, b_st, b * 64 + g * 16 + s + 1)
                act.activation(prob[kt % 2][:, j, :], st_bank[s % 2][:, :], ACT.Exp, scale=HD ** -0.5).then_inc(a_exp, 1)

            def o_out(b, g):
                wait(act, b_pv, b * 16 + g * 4 + 4)
                if g == 0:
                    wait(act, b_ot, b * TPB)
                act.activation(o_T[:, g, :], ot_bank[:, :], ACT.Copy).then_inc(a_ot, 1)

            def slot(b, g):
                now, (pb, pg), (qb, qg) = there(b), after(b, g, -1), after(b, g, 2)
                for s in range(STEPS):
                    if s == 2 and there(pb):
                        o_out(pb, pg)
                    if now:
                        exponent(b, g, s)
                    if g == 0 and there(b - 1):
                        if s in (5, 7, 9, 11):
                            t = s // 2 - 2
                            wait(act, b_at, (b - 1) * TPB + t + 1)
                            act.activation(ao_T[:, HI, :, t * P:(t + 1) * P],
                                           u_bank[:, t % 2 * D:(t % 2 + 1) * D].rearrange("p (k t) -> p k t", k=KT), ACT.Copy).then_inc(a_at, 1)
                        if s == 13:
                            wait(act, b_res, b)
                            act.activation(ro[:, :], g_bank[0:96, :], ACT.Copy).then_inc(a_res, 1)
                    if g == 0 and s == 9 and there(b):
                        values_out(b, 1)
                    for fb, f, n in shared_tiles(b, g, s):
                        if n == 1:
                            tanh(fb, f)
                        if n == 4:
                            hidden_high(fb, f)
                    if g == 2 and there(b + 1):
                        if s in (3, 5, 11):
                            low_rank_high(b + 1, (3, 5, 11).index(s))
                        if s == 13:
                            values_out(b + 1, 0)
                    for n in range(4):
                        if s == QK_STEP[g][n] and there(qb):
                            qk_high(qb, qg, n, g)

            act.wait_ge(s_in, 64)
            act.activation(w_sh[:, HI, :], s_raw[:, :], ACT.Copy).then_inc(s_hi, 1)
            slots(act, slot)

        @block.tensor
        def _(pe):
            pe.wait_ge(consts, 2)
            pe.wait_ge(small_in, 16 * 13)
            for k in range(KT):
                pe.matmul(bank[0][:, k * P:(k + 1) * P], basis_raw[:, k * P:(k + 1) * P], ident_f[:, :], start=True, stop=True)
                ins = pe.matmul(bank[0][:, 256 + k * NE:256 + (k + 1) * NE], gate_raw[:, k * P:(k + 1) * P], ident_f[0:NE, 0:NE],
                                start=True, stop=True)
            ins.then_inc(pe_prep, 1)
            wait(pe, dve_a, A_THRICE)
            for i in range(len(PROJ)):
                for k in range(KT):
                    ins = pe.matmul(bank[(1, 7)[i // 2]][0:96, (i % 2) * D + k * P:(i % 2) * D + (k + 1) * P],
                                    w_thrice[:, i * KT + k, :, :].rearrange("p r h -> p (r h)"), ident_f[:, :], start=True, stop=True)
            ins.then_inc(pe_prep, 1)

            def turn_rows(b, i):
                wait(pe, xn_ok, b + 1)
                wait(pe, xt_lo, b - 1)
                for k in range(KT):
                    for t in range(TPB):
                        ins = pe.transpose(xt_bank[i][k][:, t * P:(t + 1) * P], x_n[i][:, t, k * P:(k + 1) * P], ident_f[:, :])
                ins.then_inc(xt_ps, 1)

            def logits(b, i):
                wait(pe, xt_lo, b + 1)
                for t in range(TPB):
                    at = (b * TPB + t) * 2 * NE
                    o = lg_bank[:, at:at + 2 * NE] if isinstance(b, int) else lg_bank[:, bass.ds(at, 2 * NE)]
                    for a in (HI, LO):
                        for k in range(KT):
                            ins = pe.matmul(o, x_T[i][:, a, k, t * P:(t + 1) * P], gate_T[:, k, :, :].rearrange("p c e -> p (c e)"),
                                            start=(a == HI and k == 0), stop=(a == LO and k == KT - 1))
                ins.then_inc(lg_ps, 1)

            turn_rows(0, 0)
            pe.wait_ge(prep_done, 1)
            turn_rows(1, 1)
            logits(0, 0)
            with pe.Fori(1, PAIRS) as b2:
                for i in range(2):
                    turn_rows(b2 * 2 + i, i)
                    logits(b2 * 2 + i - 1, 1 - i)
            logits(NB - 1, 1)
            pe.wait_ge(hot_ok, 1)
            hb = hot_b[:, :, :].rearrange("p t e -> p (t e)")
            pe.matmul(bank[0][:, 0:NT * NE], upper[:, :], hb, start=True, stop=True)
            pe.matmul(bank[1][:, 0:NT * NE], ones_b[:, :], hb, start=True, stop=True).then_inc(count_ps, 1)

            def invert(b, i, first=False, last=False):
                wait(pe, inv_ok, b + 1)
                for n in range(2 * TPB):
                    k, t = n // TPB, n % TPB
                    ins = pe.matmul(bank[2][:, 0:NS], at_row[i][:, k, t, :], at_tile[i][:, k, t, :], start=first and n == 0,
                                    stop=last and n == 2 * TPB - 1)
                ins.then_inc(inv_ps, 1)

            invert(0, 0, first=True)
            invert(1, 1)
            with pe.Fori(1, PAIRS - 1) as b2:
                for i in range(2):
                    invert(b2 * 2 + i, i)
            invert(NB - 2, 0)
            invert(NB - 1, 1, last=True)

            def turn_x(s, i):
                wait(pe, c_x[i], (s // 4 + 1) * 16 if isinstance(s, int) else (s - i) * 4 + 16)
                wait(pe, c_xl, s)
                for n in range(KT):
                    ins = pe.transpose(xg_bank[:, n * P:(n + 1) * P], xg[i][:, n * P:(n + 1) * P], ident_f[:, :])
                ins.then_inc(c_xt, 1)

            w_flat = w_exp[:, :, :, :].rearrange("p e a n -> p (e a n)")

            def expert(s):
                return pe.value_load(expert_of[0:1, s:s + 1] if isinstance(s, int) else expert_of[0:1, bass.ds(s, 1)],
                                     min_val=0, max_val=(NE - 1) * 2 * W_ALL)

            def gate_up(s, i, e):
                wait(pe, c_xl, s + 1)
                for n, (free, done) in enumerate(((c_sl, c_g), (c_hk, c_u))):
                    wait(pe, free, s - 1)
                    for m, (a, c) in enumerate(PRODUCTS):
                        for k in range(KT):
                            w = w_flat[:, bass.ds(e + (c * W_ALL + k * GU + n * F), F)]
                            ins = pe.matmul(gu_bank[i % 2][n][:, 0:F], xg_T[i % 2][:, a * KT + k, :], w,
                                            start=(m == 0 and k == 0), stop=(m == 2 and k == KT - 1))
                    ins.then_inc(done, 1)

            def turn_h(s, i):
                wait(pe, c_hk, s + 1)
                wait(pe, c_hed, s - 1)
                for k in range(FT):
                    ins = pe.transpose(ht_bank[i % 2][:, k * P:(k + 1) * P], c_h[i % 2][:, k * P:(k + 1) * P], ident_f[:, :])
                ins.then_inc(c_ht, 1)

            def down(s, i, e):
                wait(pe, c_hed, s + 1)
                wait(pe, c_yk, s)
                for m, (a, c) in enumerate(PRODUCTS):
                    for k in range(FT):
                        n = P if k < FT - 1 else F_LAST
                        w = w_flat[0:n, bass.ds(e + (c * W_ALL + W_GU + k * D), D)]
                        ins = pe.matmul(y_bank[:, 0:D], c_hT[i % 2][0:n, a, k, :], w,
                                        start=(m == 0 and k == 0), stop=(m == 2 and k == FT - 1))
                ins.then_inc(c_d, 1)

            def some_tiles(s, first=False, last=False):
                at = [None if first else expert(s - 2), None if first else expert(s - 1), expert(s)]
                for i in range(RUN):
                    if first and i == NE - 2:
                        pe.wait_ge(hi_done, NE)
                        pe.wait_ge(lo_done, NE)
                    gate_up(s + i, i, at[i + 2])
                    if i < RUN - 1:
                        at.append(expert(s + i + 1))
                    if not (last and i == RUN - 1):
                        turn_x(s + i + 1, (i + 1) % 4)
                    if not (first and i < 1):
                        turn_h(s + i - 1, (i - 1) % 4)
                    if not (first and i < 2):
                        down(s + i - 2, (i - 2) % 4, at[i])
                if last:
                    turn_h(NS - 1, 3)
                    down(NS - 2, 2, at[RUN])
                    down(NS - 1, 3, at[RUN + 1])

            RUN = 8
            pe.wait_ge(a_done, 1)
            pe.wait_ge(hi_done, NE - 2)
            pe.wait_ge(lo_done, NE - 2)
            turn_x(0, 0)
            some_tiles(0, first=True)
            with pe.Fori(1, NS // RUN - 1) as s8:
                some_tiles(s8 * RUN)
            some_tiles(NS - RUN, last=True)

            pe.wait_ge(c_yk, NS)
            pe.wait_ge(c_hed, NS)

            def project(b, g, n, gs):
                rows, w, k = (r_rows[0], wq_rows, 96) if n < 2 else (r_rows[1], wk_rows, 97)
                pair = 2 * g + n % 2
                if gs == 2:
                    if n == 1:
                        wait(pe, d_dn, (b - 1) * TPB + 2)
                    elif n == 3:
                        wait(pe, d_qk, (b * NG + g) * 4 + 1)
                    else:
                        wait(pe, d_r, b * 3 + n // 2 + 1)
                elif n == 0:
                    wait(pe, d_mt, b * NG + g - 1)
                else:
                    wait(pe, d_qk, (b * NG + g) * 4 + n)
                pe.matmul(QK_BANK[gs][n][:, :], w[0:k, 2 * pair:2 * pair + 2, :].rearrange("p h j -> p (h j)"), rows[0:k, :],
                          start=True, stop=True).then_inc(b_qk, 1)

            def score(b, g, u):
                j, qt = u // 4, u % 4
                r = 64 * (j % 2)
                if u == 0:
                    wait(pe, d_qk, (b * NG + g) * 4 + 4)
                wait(pe, d_max, b * 64 + g * 16 + u - 1)
                pe.matmul(s_bank[u % 2][:, :], q_rows[g][r:r + 48, j // 2, qt * P:(qt + 1) * P], k_rows[g][r:r + 48, j // 2, :],
                          start=True, stop=True).then_inc(b_s, 1)

            def turn_max(b, g):
                wait(pe, d_m, b * NG + g + 1)
                if g == 1:
                    wait(pe, a_v, b * 2 + 2)
                for qt in range(TPB):
                    ins = pe.transpose(m_bank[0:8, qt * P:(qt + 1) * P],
                                       top_parts[g % 2][:, qt, :, :, :].rearrange("p a b c -> p (a b c)").bitcast(F32), ident_f[:, :])
                ins.then_inc(b_mt, 1)

            def gate_up_shared(b, f, quarter):
                m = P if f < SFT - 1 else SF_LAST
                if quarter == 0:
                    if f == 0:
                        if isinstance(b, int) and b == 0:
                            pe.wait_ge(s_lo, 1)
                        wait(pe, d_dn, b * TPB)
                        wait(pe, a_v, b * 2 + 1)
                    elif f == 3:
                        wait(pe, d_out, b * 2)
                    wait(pe, d_ga, b * SFT + f)
                if quarter == 2:
                    wait(pe, d_hf, b * SFT + f)
                n = quarter // 2
                for i in range(3 * (quarter % 2), 3 * (quarter % 2) + 3):
                    (a, c), k = PRODUCTS[i // 2], i % 2
                    o = k * 2 * SF + n * SF + f * P
                    ins = pe.matmul((g_bank, u_bank)[n][0:m, :], w_sh[:, a, o:o + m], xT_b[:, c, k, :], start=(i == 0), stop=(i == 5))
                if quarter == 1:
                    ins.then_inc(b_g, 1)
                if quarter == 3:
                    ins.then_inc(b_gu, 1)

            def score_T(b, g, s):
                kt, j = s // 4, s % 4
                r = 64 * (j % 2)
                if s == 0:
                    wait(pe, m_in[g % 2], b * 128 + 64 * (g // 2 + 1))
                wait(pe, a_exp, b * 64 + g * 16 + s - 1)
                pe.matmul(st_bank[s % 2][:, :], k_rows[g][r:r + QKV_ROWS, j // 2, kt * P:(kt + 1) * P],
                          q_rows[g][r:r + QKV_ROWS, j // 2, :], start=True, stop=True).then_inc(b_st, 1)

            def values(b, g, kt):
                wait(pe, a_exp, b * 64 + g * 16 + kt * 4 + 4)
                if kt == 0:
                    wait(pe, a_ot, b * NG + g)
                    if g % 2 == 0:
                        wait(pe, a_v, b * 2 + g // 2 + 1)
                for j in range(4):
                    ins = pe.matmul(ot_bank[32 * j:32 * j + 32, :], v_ones[:, kt, 4 * g + j, :], prob[kt % 2][:, j, :],
                                    start=(kt == 0), stop=(kt == TPB - 1))
                ins.then_inc(b_pv, 1)

            def low_rank(b, n, half):
                if half == 0:
                    if n == 0:
                        wait(pe, xT_in, (b + 1) * 16)
                        wait(pe, d_mt, (b - 1) * NG + 3)
                    elif n == 1:
                        wait(pe, d_dn, (b - 1) * TPB + 1)
                    else:
                        wait(pe, d_qk, b * NG * 4 + 2)
                for i in range(3 * half, 3 * half + 3):
                    (a, c), k = PRODUCTS[i // 2], i % 2
                    ins = pe.matmul(R_BANK[n][0:96, :], basis_T[:, k, a, n, :, :].rearrange("p r h -> p (r h)"), xT_b[:, c, k, :],
                                    start=(i == 0), stop=(i == 5))
                if half:
                    ins.then_inc(b_r, 1)

            def project_values(b, half):
                if half == 0:
                    wait(pe, d_r, b * 3 + 3)
                else:
                    wait(pe, d_qk, b * 16 + 12)
                for t in range(TPB):
                    ins = pe.matmul((u_bank, m_bank)[half][:, t * P:(t + 1) * P], r_rows[2][0:96, t * P:(t + 1) * P],
                                    wv_rows[:, half * P:(half + 1) * P], start=True, stop=True)
                ins.then_inc(b_v, 1)

            def down_shared(b, t, half):
                dst = (g_bank, u_bank, g_bank, g_bank)[t][:, 0:D]
                if half == 0:
                    if t == 0:
                        wait(pe, d_hf, b * SFT + SFT)
                    if t == 2:
                        wait(pe, d_qk, (b + 1) * NG * 4 + 3) if there(b + 1) else wait(pe, d_dn, b * TPB + 1)
                    if t == 3:
                        wait(pe, d_dn, b * TPB + 3)
                if half == 0 and t == 0:
                    wait(pe, p_h, b * SFT + SFT - 1)
                if half == 1 and t == 0:
                    wait(pe, p_h, b * SFT + SFT)
                for i in range(9 * half, 9 * half + 9):
                    f, (a, c) = i // 3, PRODUCTS[i % 3]
                    m = P if f < SFT - 1 else SF_LAST
                    ins = pe.matmul(dst, h_T[0:m, a, f, t * P:(t + 1) * P], w_sh[0:m, c, S_GU + f * D:S_GU + (f + 1) * D],
                                    start=(i == 0), stop=(i == 17))
                if half:
                    ins.then_inc(b_dn, 1)

            def turn_o(b, t):
                if t == 0:
                    wait(pe, a_ot, b * NG + NG)
                    if there(b + 1):
                        wait(pe, d_hf, (b + 1) * SFT + 3)
                    else:
                        wait(pe, d_dn, b * TPB + TPB)
                else:
                    wait(pe, d_ao, b * TPB + t)
                for g in range(NG):
                    ins = pe.transpose(g_bank[:, g * P:(g + 1) * P], o_T[:, g, t * P:(t + 1) * P], ident_f[:, :])
                ins.then_inc(b_ot, 1)

            def turn_back(b, t):
                wait(pe, d_ao, b * TPB + t + 1)
                if t:
                    wait(pe, d_at, b * TPB + t)
                for k in range(KT):
                    ins = pe.transpose(u_bank[:, t % 2 * D + k * P:t % 2 * D + (k + 1) * P], ao[t % 2][:, k * P:(k + 1) * P], ident_f[:, :])
                ins.then_inc(b_at, 1)

            def low_rank_o(b):
                wait(pe, d_at, b * TPB + TPB)
                for i in range(6):
                    (a, c), k = PRODUCTS[i // 2], i % 2
                    ins = pe.matmul(g_bank[0:96, :], basis_T[:, k, a, 3, :, :].rearrange("p r h -> p (r h)"), ao_T[:, c, k, :],
                                    start=(i == 0), stop=(i == 5))
                ins.then_inc(b_res, 1)

            def project_o(b, half):
                wait(pe, d_res, b + 1)
                for t in range(2):
                    q = 2 * half + t
                    ins = pe.matmul((u_bank, g_bank)[half][:, t * D:(t + 1) * D], ro[:, q * P:(q + 1) * P], wo_rows[:, :], start=True, stop=True)
                ins.then_inc(b_out, 1)

            def slot(b, g):
                now, (pb, pg), (nb, ng), (qb, qg) = there(b), after(b, g, -1), after(b, g, 1), after(b, g, 2)
                for s in range(STEPS):
                    if now:
                        score_T(b, g, s)
                    if s < STEPS - AHEAD:
                        if there(nb):
                            score(nb, ng, s + AHEAD)
                    elif there(qb):
                        score(qb, qg, s - STEPS + AHEAD)
                    if s == 1 and there(pb):
                        values(pb, pg, TPB - 1)
                    if s in (5, 9, 13) and now:
                        values(b, g, s // 4 - 1)
                    if g == 0 and there(b - 1):
                        if s in (3, 5, 7, 9):
                            turn_o(b - 1, s // 2 - 1)
                        if s in (5, 7, 9, 11):
                            turn_back(b - 1, s // 2 - 2)
                        if s == 13:
                            low_rank_o(b - 1)
                    if g == 0 and s == 9 and now:
                        project_values(b, 1)
                    if g == 1 and s == 0 and there(b - 1):
                        project_o(b - 1, 0)
                        project_o(b - 1, 1)
                    for fb, f, n in shared_tiles(b, g, s):
                        if n < 4:
                            gate_up_shared(fb, f, n)
                    if g == 2 and now:
                        for t, at in enumerate((1, 3, 11, 14)):
                            if s in (at, at + 1):
                                down_shared(b, t, s - at)
                    if g == 2 and there(b + 1):
                        for n, at in enumerate((2, 4, 10)):
                            if s in (at, at + 1):
                                low_rank(b + 1, n, s - at)
                        if s == 13:
                            project_values(b + 1, 0)
                    for n in range(4):
                        if s == QK_STEP[g][n] and there(qb):
                            project(qb, qg, n, g)
                    if s == STEPS - AHEAD and there(nb):
                        turn_max(nb, ng)

            slots(pe, slot)

        @block.vector
        def _(dve):
            st = Steps(dve, dve_a)
            dve.wait_ge(small_in, 16 * 13)
            ph = phase[:, :, :, :].rearrange("p i k h -> p (i k h)")
            am = amp[:, :, :, :].rearrange("p i k h -> p (i k h)")
            st.then(dve.tensor_scalar(turns[:, :], ph, 1 / (2 * math.pi), 0.25, ALU.mult, ALU.add))
            st.then(dve.tensor_scalar(turns[:, :], turns[:, :], ROUNDER, ROUNDER, ALU.add, ALU.subtract))
            st.then(dve.scalar_tensor_tensor(angle[:, :], turns[:, :], -TURN_1, ph, ALU.mult, ALU.add))
            st.then(dve.scalar_tensor_tensor(angle[:, :], turns[:, :], -TURN_2, angle[:, :], ALU.mult, ALU.add))
            st.then(dve.scalar_tensor_tensor(angle[:, :], turns[:, :], -TURN_3, angle[:, :], ALU.mult, ALU.add))
            st.then(dve.tensor_scalar(angle[:, :], angle[:, :], math.pi / 2, PI_BELOW, ALU.add, ALU.min))
            st.then(dve.tensor_scalar(angle[:, :], angle[:, :], -PI_BELOW, None, ALU.max))
            assert st.n == A_ANGLE
            st.did(dve.memset(q_minus[:, :], 0.0))
            st.then(dve.memset(k_minus[:, :], 0.0))
            for h in range(2):
                st.did(dve.memset(q_minus[64 * h + 32:64 * h + 48, :], -1.0))
                st.did(dve.memset(k_minus[64 * h:64 * h + 32, :], -1.0))
            st.wait()
            for h in range(2):
                st.did(dve.memset(k_minus[64 * h:64 * h + 16, :], 0.0))
            dve.wait_ge(consts, 2)
            st.did(dve.memset(wk_rows[96:97, :, 48:50].bitcast(F32), -1.0))
            dve.wait_ge(pe_prep, 1)
            for k in range(KT):
                b = bank[0][:, k * P:(k + 1) * P].rearrange("p (i r h) -> p i r h", i=len(PROJ), r=1)
                b = b.to_broadcast([P, len(PROJ), 3, HARM])
                g = bank[0][:, 256 + k * NE:256 + (k + 1) * NE]
                st.did(dve.tensor_copy(basis_T[:, k, HI, :, :, :], b))
                st.then(dve.tensor_copy(gate_T[:, k, HI, :], g))
                st.did(dve.tensor_tensor(basis_T[:, k, LO, :, :, :], b, basis_T[:, k, HI, :, :, :].bitcast(F32), ALU.subtract))
                st.did(dve.tensor_tensor(gate_T[:, k, LO, :], g, gate_T[:, k, HI, :].bitcast(F32), ALU.subtract))
            dve.wait_ge(sin_done, 1)
            sn = angle[:, :].rearrange("p (i r h) -> p i r h", r=1, h=HARM).to_broadcast([P, len(PROJ) * KT, 3, HARM])
            ab = am.rearrange("p (i r h) -> p i r h", r=1, h=HARM).to_broadcast([P, len(PROJ) * KT, 3, HARM])
            st.then(dve.tensor_tensor(w_thrice[:, :, :, :], sn, ab, ALU.mult))
            assert st.n == A_THRICE
            for q in range(4):
                dve.wait_ge(x_in[q], 16 * (NB // 4))
                for n in range(q * NT // 4, (q + 1) * NT // 4):
                    ins = dve.bn_stats(stats[:, n, :], x_all[:, n, :])
                st.did(ins)
            dve.wait_ge(pe_prep, 2)
            dve.wait_ge(consts, 2)
            for i in range(len(PROJ)):
                st.did(dve.tensor_copy(w_hi[:, i, :], bank[(1, 7)[i // 2]][0:96, (i % 2) * D:(i % 2 + 1) * D]))
            st.wait()
            for i in range(len(PROJ)):
                src = bank[(1, 7)[i // 2]][0:96, (i % 2) * D:(i % 2 + 1) * D]
                st.did(dve.tensor_tensor(w_hi[32:64, i, :], src[32:64, :], w_hi[32:64, i, :].bitcast(F32), ALU.subtract))
            st.wait()
            for i, dst in enumerate((wq_rows, wk_rows)):
                v = w_hi[:, i, :].rearrange("p (h r j) -> p h r j", h=HEADS, r=1).to_broadcast([96, HEADS, 3, HD]).bitcast(F32)
                st.did(dve.tensor_copy(dst[0:96, :, 0:48].rearrange("p h (r j) -> p h r j", r=3), v))
            st.did(dve.tensor_copy(wv_rows[:, :], w_hi[:, 2, :].bitcast(F32)))
            st.did(dve.tensor_copy(wo_rows[:, :], w_hi[:, 3, :].bitcast(F32)))
            for n in range(NT):
                ins = dve.bn_aggr(mean_var[:, n, :], stats[:, n, :])
            st.then(ins)
            dve.tensor_scalar(rs[:, 0, :], mean_var[:, :, 1], LN_EPS, None, ALU.add).then_inc(stats_ok, 1)
            dve.wait_ge(root_ok, 1)
            st.then(dve.reciprocal(rs[:, 2, :], rs[:, 1, :]))
            st.then(dve.tensor_tensor(rs[:, 3, :], rs[:, 2, :], rs[:, 2, :], ALU.mult))
            st.then(dve.tensor_tensor(rs[:, 3, :], rs[:, 3, :], rs[:, 0, :], ALU.mult))
            st.then(dve.tensor_scalar(rs[:, 3, :], rs[:, 3, :], -0.5, 1.5, ALU.mult, ALU.add))
            st.then(dve.tensor_tensor(rs[:, 3, :], rs[:, 2, :], rs[:, 3, :], ALU.mult))
            dve.memset(rs[:, 1, :], 0.0).then_inc(prep_done, 1)

            def normal(b2, i):
                b = b2 * 2 + i
                wait(dve, xt_ps, b - 1)
                wait(dve, xn_stored[i], b2 * 16)
                for t in range(TPB):
                    n = b * TPB + t
                    at = slice(n, n + 1) if isinstance(n, int) else bass.ds(n, 1)
                    ins = dve.tensor_scalar(x_n[i][:, t, :], x_all[:, at, :].rearrange("p a d -> p (a d)"),
                                            mean_var[:, at, 0:1].rearrange("p a c -> p (a c)"), rs[:, 3, at], ALU.subtract, ALU.mult)
                ins.then_inc(xn_ok, 1)

            def pair(b2, last=False):
                for i in range(2):
                    b = b2 * 2 + i
                    if not (last and i):
                        normal(b2 + i, 1 - i)
                    wait(dve, xt_hi, b + 1)
                    for k in range(KT):
                        ins = dve.tensor_tensor(x_T[i][:, LO, k, :], xt_bank[i][k][:, :], x_T[i][:, HI, k, :].bitcast(F32), ALU.subtract)
                    ins.then_inc(xt_lo, 1)

            normal(0, 0)
            pair(0)
            with dve.Fori(1, PAIRS - 1) as b2:
                pair(b2)
            pair(PAIRS - 1, last=True)

            def over_e(v):
                return v.rearrange("p (t r) -> p t r", r=1).to_broadcast([P, NT, NE])

            def over_t(v):
                return v.rearrange("p (r e) -> p r e", r=1).to_broadcast([P, NT, NE])

            dve.wait_ge(lg_ps, NB)
            parts = lg_bank[:, :].rearrange("p (t c e) -> p t c e", c=2, e=NE)
            st.then(dve.tensor_copy(pr[:, :, :], parts[:, :, LO, :]))
            st.then(dve.tensor_tensor(lg[:, :, :], parts[:, :, HI, :], pr[:, :, :], ALU.add))
            st.then(dve.tensor_reduce(row[:, 0, :], lg[:, :, :], AX_X, ALU.max))
            dve.tensor_tensor(lg[:, :, :], lg[:, :, :], over_e(row[:, 0, :]), ALU.subtract).then_inc(lg_max, 1)
            dve.wait_ge(lg_exp, 1)
            st.then(dve.tensor_reduce(row[:, 1, :], pr[:, :, :], AX_X, ALU.add))
            st.then(dve.reciprocal(row[:, 2, :], row[:, 1, :]))
            st.then(dve.tensor_tensor(pr[:, :, :], pr[:, :, :], over_e(row[:, 2, :]), ALU.mult))
            for n in range(NT):
                ins = dve.max(best[:, n, :], pr[:, n, :])
            st.then(ins)
            for n in range(NT):
                ins = dve.max_index(best_at[:, n, :], best[:, n, :], pr[:, n, :])
            st.did(ins)
            st.then(dve.tensor_tensor(row[:, 3, :], best[:, :, 0], best[:, :, 1], ALU.add))
            st.then(dve.tensor_scalar(row[:, 3, :], row[:, 3, :], TOPK_EPS, None, ALU.add))
            st.then(dve.reciprocal(row[:, 0, :], row[:, 3, :]))
            for k in range(2):
                st.did(dve.scalar_tensor_tensor(share[:, :, k], best[:, :, k], ROUTE_SCALE, row[:, 0, :], ALU.mult, ALU.mult))
                st.did(dve.tensor_copy(best_atf[:, k, :], best_at[:, :, k]))
            st.wait()
            for k in range(2):
                st.did(dve.tensor_tensor(hot[k][:, :, :], over_e(best_atf[:, k, :]), over_t(iota_e[:, :]), ALU.is_equal))
            st.wait()
            st.did(dve.tensor_tensor(hot_b[:, :, :], hot[0][:, :, :], hot[1][:, :, :], ALU.add))
            st.wait()
            dve.memset(row[:, 1, :], 0.0).then_inc(hot_ok, 1)
            dve.wait_ge(count_ps, 1)
            st.then(dve.tensor_copy(totals[:, :, :], bank[1][:, 0:NT * NE].rearrange("p (t e) -> p e t", e=NE)))
            for e in range(NE):
                st.did(dve.tensor_tensor_scan(before[:, e, :], totals[:, e, :], zeros[:, :], 0.0, ALU.add, ALU.add))
            st.wait()
            st.then(dve.tensor_scalar(tiles[:, 0, :], before[:, :, NT - 1], 1 / P, (P - 1) / P - 0.5 + 1 / 512, ALU.mult, ALU.add))
            st.then(dve.tensor_scalar(tiles[:, 0, :], tiles[:, 0, :], ROUNDER, ROUNDER, ALU.add, ALU.subtract))
            st.then(dve.tensor_scalar(tiles[:, 1, :], tiles[:, 0, :], 1.0, None, ALU.max))
            st.then(dve.tensor_tensor_scan(tiles[:, 2, :], tiles[:, 1, :], zeros[:, 0:NE], 0.0, ALU.add, ALU.add))
            st.then(dve.tensor_tensor(tiles[:, 3, :], tiles[:, 2, :], tiles[:, 1, :], ALU.subtract))
            st.then(dve.tensor_tensor(before[:, :, :], before[:, :, :], totals[:, :, :], ALU.subtract))
            st.then(dve.tensor_tensor(slot_base[:, :, :], bank[0][:, 0:NT * NE].rearrange("p (t e) -> p t e", e=NE),
                                      before[:, :, :].rearrange("p e t -> p t e"), ALU.add))
            st.then(dve.scalar_tensor_tensor(slot_base[:, :, :], over_t(tiles[:, 3, :]), float(P), slot_base[:, :, :], ALU.mult, ALU.add))
            for k in range(2):
                st.then(dve.tensor_tensor(slot_hot[:, :, :], slot_base[:, :, :], hot[k][:, :, :], ALU.mult))
                st.then(dve.tensor_reduce(slot_f[:, k, :], slot_hot[:, :, :], AX_X, ALU.add))
            st.did(dve.tensor_copy(slot_of[:, :, :], slot_f[:, :, :]))
            st.then(dve.tensor_scalar(slot_q[:, :, :], slot_f[:, :, :], 1 / P, 1 / 512 - 0.5, ALU.mult, ALU.add))
            st.then(dve.tensor_scalar(slot_q[:, :, :], slot_q[:, :, :], ROUNDER, ROUNDER, ALU.add, ALU.subtract))
            st.did(dve.scalar_tensor_tensor(slot_r[:, :, :], slot_q[:, :, :], -float(P), slot_f[:, :, :], ALU.mult, ALU.add))
            st.then(dve.tensor_tensor(started[:, :, :], iota_s[0:1, :].rearrange("p (s r) -> p s r", r=1).to_broadcast([1, NS, NE]),
                                      tiles[0:1, 3, :].rearrange("p (r e) -> p r e", r=1).to_broadcast([1, NS, NE]), ALU.is_ge))
            st.then(dve.tensor_reduce(started_n[:, :], started[:, :, :], AX_X, ALU.add))
            st.did(dve.tensor_scalar(expert_of[:, :], started_n[:, :], -1.0, 2.0 * W_ALL, ALU.add, ALU.mult))
            st.wait()

            def alike(v, n):
                return v.rearrange("p (k t n) -> p k t n", k=1, t=1).to_broadcast([P, 2, TPB, n])

            def one_hots(b, i):
                at = slice(b * TPB, (b + 1) * TPB) if isinstance(b, int) else bass.ds(b * TPB, TPB)

                def own(v, n):
                    return v.rearrange("p k (t n) -> p k t n", n=1).to_broadcast([P, 2, TPB, n])

                wait(dve, inv_ps, b - 1)
                dve.tensor_tensor(at_tile1[i][:, :, :, :], alike(iota_s[:, :], NS), own(slot_q[:, :, at], NS), ALU.is_equal).then_inc(inv_eq, 1)
                dve.tensor_tensor(at_row[i][:, :, :, :], alike(iota_r[:, :], P), own(slot_r[:, :, at], P), ALU.is_equal)
                wait(dve, inv_eq, b + 1)
                dve.tensor_tensor(at_tile[i][:, :, :, :], at_tile1[i][:, :, :, :],
                                  token_id[:, at].rearrange("p (k t n) -> p k t n", k=1, n=1).to_broadcast([P, 2, TPB, NS]),
                                  ALU.mult).then_inc(inv_ok, 1)

            one_hots(0, 0)
            one_hots(1, 1)
            with dve.Fori(1, PAIRS) as b2:
                for i in range(2):
                    one_hots(b2 * 2 + i, i)
            dve.wait_ge(inv_ps, NB)
            st.then(dve.tensor_copy(token_of[:, :], bank[2][:, 0:NS]))
            for i in range(2):
                st.did(dve.memset(c_h[i][:, F:FT * P], 0.0))
            st.wait()
            dve.memset(zeros[:, :], 0.0).then_inc(a_done, 1)

            def hidden(s, i):
                wait(dve, c_sl, s + 1)
                wait(dve, c_u, s + 1)
                wait(dve, c_ht, s - 1)
                dve.tensor_tensor(c_h[i % 2][:, 0:F], c_sil[i % 2][:, :], gu_bank[i % 2][1][:, 0:F], ALU.mult).then_inc(c_hk, 1)

            def h_out(s, i):
                wait(dve, c_hea, s + 1)
                dve.tensor_tensor(c_hT[i % 2][:, LO, :, :].rearrange("p a t -> p (a t)"), ht_bank[i % 2][:, 0:FT * P],
                                  c_hT[i % 2][:, HI, :, :].rearrange("p a t -> p (a t)").bitcast(F32), ALU.subtract).then_inc(c_hed, 1)

            def x_low(s, i):
                wait(dve, c_xe, s + 1)
                dve.tensor_tensor(xg_T[i % 2][:, KT:2 * KT, :].rearrange("p a t -> p (a t)"), xg_bank[:, 0:D],
                                  xg_T[i % 2][:, 0:KT, :].rearrange("p a t -> p (a t)").bitcast(F32), ALU.subtract).then_inc(c_xl, 1)

            def step(s, i, first=False, last=False):
                hidden(s, i)
                if not (last and i == 3):
                    x_low(s + 1, (i + 1) % 4)
                if not (first and i < 1):
                    h_out(s - 1, (i - 1) % 4)

            x_low(0, 0)

            for i in range(4):
                step(i, i, first=True)
            with dve.Fori(1, NS // 4 - 1) as s4:
                for i in range(4):
                    step(s4 * 4 + i, i)
            for i in range(4):
                step(NS - 4 + i, i, last=True)
            h_out(NS - 1, 3)

            dve.wait_ge(c_yk, NS)
            for i in range(4):
                dve.wait_ge(c_st[i], 16 * (NS // 4))
            dve.memset(r_rows[1][96:97, :].bitcast(F32), 1.0)
            dve.memset(v_ones[:, :, :, HD:2 * HD], 1.0)

            def qk_split(b, g, n, gs):
                minus, dst = (q_minus, q_rows) if n < 2 else (k_minus, k_rows)
                wait(dve, a_qk, (b * NG + g) * 4 + n + 1)
                if n == 0:
                    wait(dve, b_st, (b * NG + g - 3) * 16)
                dve.scalar_tensor_tensor(dst[g][:, n % 2, :], qk_hi[n % 2][:, :].bitcast(F32), minus[:, 0:1], QK_BANK[gs][n][:, :],
                                         ALU.mult, ALU.add).then_inc(d_qk, 1)

            def maximum(b, g, u):
                j, qt = u // 4, u % 4
                wait(dve, b_s, b * 64 + g * 16 + u + 1)
                if u == 0:
                    wait(dve, d_m, b * NG + g - 1)
                dve.tensor_reduce(top[g % 2][:, j % 2, j // 2, qt:qt + 1], s_bank[u % 2][:, :], AX_X, ALU.max).then_inc(d_max, 1)

            def split_max(b, g):
                wait(dve, d_max, b * 64 + g * 16 + 16)
                wait(dve, b_mt, b * NG + g - 1)
                dst = top_parts[g % 2]
                src = top[g % 2][:, :, :, :].rearrange("p a b t -> p t a b")
                dve.tensor_copy(dst[:, :, :, :, HI], src).then_inc(d_mh, 1)
                wait(dve, d_mh, b * NG + g + 1)
                dve.tensor_tensor(dst[:, :, :, :, LO], src, dst[:, :, :, :, HI].bitcast(F32), ALU.subtract).then_inc(d_m, 1)

            def max_rows(b, g):
                wait(dve, b_mt, b * NG + g + 1)
                wait(dve, m_in[g % 2], b * 128 + 64 * (g // 2))
                dve.tensor_copy(top_T[g % 2][:, :], m_bank[0:8, :]).then_inc(d_mt, 1)

            def gate_shared(b, f):
                h = h_f[f % 2][0:P if f < SFT - 1 else SF_LAST, :]
                wait(dve, a_th, b * SFT + f + 1)
                dve.scalar_tensor_tensor(h, h, 1.0, g_bank[0:h.shape[0], :], ALU.add, ALU.mult).then_inc(d_ga, 1)

            def hidden_shared(b, f):
                h = h_f[f % 2][0:P if f < SFT - 1 else SF_LAST, :]
                wait(dve, b_gu, b * SFT + f + 1)
                wait(dve, d_ga, b * SFT + f + 1)
                dve.scalar_tensor_tensor(h, h, 0.5, u_bank[0:h.shape[0], :], ALU.mult, ALU.mult).then_inc(d_hf, 1)

            def low_rank_low(b, n):
                wait(dve, a_r, b * 3 + n + 1)
                dve.tensor_tensor(r_rows[n][64:96, :], R_BANK[n][64:96, :], r_rows[n][64:96, :].bitcast(F32), ALU.subtract).then_inc(d_r, 1)

            def add_down(b, t):
                wait(dve, b_dn, b * TPB + t + 1)
                if t == 0:
                    wait(dve, p_y, b + 1)
                dve.tensor_tensor(o_b[:, t, :], (g_bank, u_bank, g_bank, g_bank)[t][:, 0:D], o_b[:, t, :], ALU.add).then_inc(d_dn, 1)

            def normalise(b, t):
                ov = g_bank[:, :].rearrange("p (h c) -> p h c", h=HEADS)
                wait(dve, b_ot, b * TPB + t + 1)
                if t >= 2:
                    wait(dve, d_ao, b * TPB + t - 1)
                dve.reciprocal(o_inv[:, t % 2, :], ov[:, :, HD]).then_inc(d_inv, 1)
                wait(dve, d_inv, b * TPB + t + 1)
                if t >= 2:
                    wait(dve, b_at, b * TPB + t - 1)
                dve.tensor_tensor(ao[t % 2][:, :].rearrange("p (h d) -> p h d", h=HEADS), ov[:, :, 0:HD],
                                  o_inv[:, t % 2, :].rearrange("p (h r) -> p h r", r=1).to_broadcast([P, HEADS, HD]),
                                  ALU.mult).then_inc(d_ao, 1)

            def back_low(b, t):
                wait(dve, a_at, b * TPB + t + 1)
                o = ao_T[:, :, :, t * P:(t + 1) * P]
                dve.tensor_tensor(o[:, LO, :, :], u_bank[:, t % 2 * D:(t % 2 + 1) * D].rearrange("p (k t) -> p k t", k=KT),
                                  o[:, HI, :, :].bitcast(F32), ALU.subtract).then_inc(d_at, 1)

            def add_o(b, half):
                wait(dve, b_out, b * 2 + half + 1)
                wait(dve, d_dn, b * TPB + TPB)
                o = o_b[:, 2 * half:2 * half + 2, :].rearrange("p t d -> p (t d)")
                dve.tensor_tensor(o, (u_bank, g_bank)[half][:, :], o, ALU.add).then_inc(d_out, 1)

            def slot(b, g):
                now, (pb, pg), (nb, ng), (qb, qg) = there(b), after(b, g, -1), after(b, g, 1), after(b, g, 2)
                for s in range(STEPS):
                    if s == STEPS - AHEAD and there(nb):
                        split_max(nb, ng)
                    if s < STEPS - AHEAD:
                        if there(nb):
                            maximum(nb, ng, s + AHEAD)
                    elif there(qb):
                        maximum(qb, qg, s - STEPS + AHEAD)
                    if s == STEPS - AHEAD and there(nb):
                        max_rows(nb, ng)
                    for n in range(4):
                        if s == QK_STEP[g][n] + 1 and there(qb):
                            qk_split(qb, qg, n, g)
                    if g == 0 and there(b - 1):
                        if s in (3, 5, 7, 9):
                            normalise(b - 1, s // 2 - 1)
                        if s in (6, 8, 10, 12):
                            back_low(b - 1, s // 2 - 3)
                        if s == 14:
                            wait(dve, a_res, b)
                            dve.tensor_tensor(ro[64:96, :], g_bank[64:96, :], ro[64:96, :].bitcast(F32), ALU.subtract).then_inc(d_res, 1)
                    if g == 1 and s == 0 and there(b - 1):
                        add_o(b - 1, 0)
                        add_o(b - 1, 1)
                    for fb, f, n in shared_tiles(b, g, s):
                        if n == 2:
                            gate_shared(fb, f)
                        if n == 3:
                            hidden_shared(fb, f)
                    if g == 2 and now:
                        for t, at in enumerate((2, 4, 12, 15)):
                            if s == at:
                                add_down(b, t)
                    if g == 2 and there(b + 1):
                        for n, at in enumerate((4, 6, 12)):
                            if s == at:
                                low_rank_low(b + 1, n)

            slots(dve, slot)


A_ANGLE = 7
A_THRICE = 25


_INS = (["L0_attn_x"] + [f"L0_attn_{what}_{name}" for name in "qkvo" for what in ("basis", "phase", "amp")]
        + [f"L0_ffn_{name}" for name in ("gate_w", "w_gate", "w_up", "w_down", "sw_gate", "sw_up", "sw_down")])


def kernel(**inputs):
    import numpy as _np
    import concourse.bacc as _bacc
    from concourse import mybir as _mybir
    from concourse.bass_utils import run_bass_kernel_spmd as _run

    nc = _bacc.Bacc("TRN2", target_bir_lowering=False, num_devices=1)
    arrays, args = {}, {}
    for name in _INS:
        a = _np.ascontiguousarray(inputs[name])
        arrays[f"in_{name}_dram"] = a
        args[name] = nc.dram_tensor(f"in_{name}_dram", a.shape, _mybir.dt.from_np(a.dtype), kind="ExternalInput").ap()
    x = inputs["L0_attn_x"]
    out = nc.dram_tensor("out_0_dram", x.shape, _mybir.dt.from_np(_np.dtype("float32")), kind="ExternalOutput").ap()
    attn = {name: tuple(args[f"L0_attn_{what}_{name}"] for what in ("basis", "phase", "amp")) for name in "qkvo"}
    build_program(nc, args["L0_attn_x"], attn, *(args[f"L0_ffn_{name}"] for name in
                                                 ("gate_w", "w_gate", "w_up", "w_down", "sw_gate", "sw_up", "sw_down")), out)
    r = _run(nc, [arrays], core_ids=[0])
    return r.results[0]["out_0_dram"]
```
